# Optimizing a Trainium2 kernel written in Bass

```python
import numpy as np
import jax
import jax.numpy as jnp

def _softmax(x, axis=-1):
    return jax.nn.softmax(x, axis=axis)

def _gelu(x):
    return jax.nn.gelu(x, approximate=True)

def _silu(x):
    return jax.nn.silu(x)

def _sigmoid(x):
    return jax.nn.sigmoid(x)

def _layernorm(x, axis=-1, eps=1e-05):
    m = jnp.mean(x, axis=axis, keepdims=True)
    v = jnp.var(x, axis=axis, keepdims=True)
    return (x - m) / jnp.sqrt(v + eps)

def _scatter_add(tgt, idx, src, axis=0):
    return tgt.at[idx].add(src)

def _segment_sum(src, seg, n):
    return jax.ops.segment_sum(src, seg, n)
kernel_name = 'mk_decoder_preln_d2_seqx_r4_0a6ac5'

def setup_inputs(seed: int=0):
    np.random.seed(seed)
    _w = jnp.asarray

    def _rec_inputs():
        import jax
        import jax.numpy as jnp
        _rk = jax.random.key(seed)
        x = 0.0003765 + 1 * jax.random.normal(jax.random.fold_in(_rk, 1), (8, 512, 256), jnp.float32)
        _lenS = 512 - jax.random.randint(jax.random.fold_in(_rk, 7), (8,), 0, max(1, 512 // 4) + 1, jnp.int32)
        _lenS2 = 64 - jax.random.randint(jax.random.fold_in(_rk, 8), (8,), 0, max(1, 64 // 4) + 1, jnp.int32)
        _ctx_1024P = jax.random.normal(jax.random.fold_in(_rk, 11), (8, 16, 256), jnp.float32)
        _ctx_1024c = jax.random.dirichlet(jax.random.fold_in(_rk, 511), 0.3 * jnp.ones((16,), jnp.float32), (8, 64))
        _ctx_1024t = jnp.einsum('bsk,bkd->bsd', _ctx_1024c, _ctx_1024P)
        _ctx_1024t = _ctx_1024t * jax.lax.rsqrt(jnp.mean(jnp.square(_ctx_1024t)) + 1e-12) * 0.953939
        ctx_1024 = -0.000292821 + 1.00034 * (_ctx_1024t + 0.3 * jax.random.normal(jax.random.fold_in(_rk, 611), (8, 64, 256), jnp.float32))
        _validS = jnp.arange(512)[None, :] < _lenS[:, None]
        _validS2 = jnp.arange(64)[None, :] < _lenS2[:, None]
        _causal = jnp.tril(jnp.ones((512, 512), dtype=bool))
        mask_BxSxS2_ff0 = jnp.where(jnp.ones((8, 512, 64), dtype=bool), 0.0, -1000000000.0).astype(jnp.float32)
        return (x, ctx_1024, mask_BxSxS2_ff0)
    x, ctx_1024, mask_BxSxS2_ff0 = _rec_inputs()

    def _L0_attn_setup():
        import jax, jax.numpy as jnp
        import numpy as np
        B, T, C = (4, 512, 256)
        H = 16
        D = C // H
        key = jax.random.key(seed)
        k1, k2, k3 = jax.random.split(key, 3)
        x = jax.random.normal(k1, (B, T, C), dtype=jnp.float32)
        w_attn = jax.random.normal(k2, (3 * C, C), dtype=jnp.float32) * (1.0 / np.sqrt(C))
        w_proj = jax.random.normal(k3, (C, C), dtype=jnp.float32) * (1.0 / np.sqrt(C))
        return {'x': x, 'w_attn': w_attn, 'w_proj': w_proj}
    _L0_attn_all = _L0_attn_setup()
    _L0_attn_in = {k: v for k, v in _L0_attn_all.items() if k in ('w_attn', 'w_proj')}
    del _L0_attn_all

    def _L0_xattn_setup():
        import jax, jax.numpy as jnp
        import numpy as np
        D_MODEL = 256
        NUM_HEADS = 16
        DEPTH = D_MODEL // NUM_HEADS
        B, S = (2, 512)

        def _split_heads(x):
            b, s, _ = x.shape
            return x.reshape(b, s, NUM_HEADS, DEPTH).transpose(0, 2, 1, 3)
        key = jax.random.key(seed)
        ks = jax.random.split(key, 11)
        s = 1.0 / np.sqrt(D_MODEL)
        return {'v': jax.random.normal(ks[0], (B, S, D_MODEL), jnp.float32), 'k': jax.random.normal(ks[1], (B, S, D_MODEL), jnp.float32), 'q': jax.random.normal(ks[2], (B, S, D_MODEL), jnp.float32), 'wq': jax.random.normal(ks[3], (D_MODEL, D_MODEL), jnp.float32) * s, 'bq': jnp.zeros((D_MODEL,), jnp.float32), 'wk': jax.random.normal(ks[4], (D_MODEL, D_MODEL), jnp.float32) * s, 'bk': jnp.zeros((D_MODEL,), jnp.float32), 'wv': jax.random.normal(ks[5], (D_MODEL, D_MODEL), jnp.float32) * s, 'bv': jnp.zeros((D_MODEL,), jnp.float32), 'wo': jax.random.normal(ks[6], (D_MODEL, D_MODEL), jnp.float32) * s, 'bo': jnp.zeros((D_MODEL,), jnp.float32)}
    _L0_xattn_all = _L0_xattn_setup()
    _L0_xattn_in = {k: v for k, v in _L0_xattn_all.items() if k in ('wq', 'bq', 'wk', 'bk', 'wv', 'bv', 'wo', 'bo')}
    del _L0_xattn_all

    def _L0_ffn_setup():
        import math
        import jax, jax.numpy as jnp
        import numpy as np
        B, T, D = (4, 1024, 256)
        H = 16
        HD = D // H
        CAP = int(1024 * 0.125)
        DFF = int(D * 4 * 2 / 3)
        EPS = 1e-06

        def rmsnorm(x, g):
            return x * jax.lax.rsqrt(jnp.mean(x * x, axis=-1, keepdims=True) + EPS) * g
        key = jax.random.key(seed)
        ks = jax.random.split(key, 9)
        s = lambda k, shape: jax.random.normal(k, shape, jnp.float32) * 0.02
        return {'x': jax.random.normal(ks[0], (B, T, D), jnp.float32), 'w_router': s(ks[1], (D,)), 'W_qkv': s(ks[2], (3 * D, D)), 'W_out': s(ks[3], (D, D)), 'g1': jnp.ones((D,), jnp.float32), 'g2': jnp.ones((D,), jnp.float32), 'W1': s(ks[4], (DFF, D)), 'W2': s(ks[5], (DFF, D)), 'W3': s(ks[6], (D, DFF))}
    _L0_ffn_all = _L0_ffn_setup()
    _L0_ffn_in = {k: v for k, v in _L0_ffn_all.items() if k in ('w_router', 'W_qkv', 'W_out', 'g1', 'g2', 'W1', 'W2', 'W3')}
    del _L0_ffn_all

    def _L1_attn_setup():
        import jax, jax.numpy as jnp
        import numpy as np
        NUM_HEADS = 16
        EPS = 1e-06

        def _rmsnorm(h, w):
            h32 = h.astype(jnp.float32)
            var = jnp.mean(h32 * h32, axis=-1, keepdims=True)
            return (w * (h32 * jax.lax.rsqrt(var + EPS))).astype(h.dtype)
        key = jax.random.key(seed)
        ks = jax.random.split(key, 4)
        B, N, C = (16, 256, 256)
        x = jax.random.normal(ks[0], (B, N, C), dtype=jnp.float32)
        qkv_w = jax.random.normal(ks[1], (3 * C, C), dtype=jnp.float32) * C ** (-0.5)
        proj_w = jax.random.normal(ks[2], (C, C), dtype=jnp.float32) * C ** (-0.5)
        proj_b = jnp.zeros((C,), dtype=jnp.float32)
        q_norm_w = jnp.ones((C // NUM_HEADS,), dtype=jnp.float32)
        k_norm_w = jnp.ones((C // NUM_HEADS,), dtype=jnp.float32)
        return {'x': x, 'qkv_w': qkv_w, 'proj_w': proj_w, 'proj_b': proj_b, 'q_norm_w': q_norm_w, 'k_norm_w': k_norm_w}
    _L1_attn_all = _L1_attn_setup()
    _L1_attn_in = {k: v for k, v in _L1_attn_all.items() if k in ('qkv_w', 'proj_w', 'proj_b', 'q_norm_w', 'k_norm_w')}
    del _L1_attn_all

    def _L1_xattn_setup():
        import jax, jax.numpy as jnp
        import numpy as np
        B, S, D, H = (2, 512, 256, 16)
        HD = D // H

        def _split_heads(x):
            b, s, _ = x.shape
            return x.reshape(b, s, H, HD).transpose(0, 2, 1, 3)
        key = jax.random.key(seed)
        ks = jax.random.split(key, 12)
        s = 1.0 / np.sqrt(D)
        return {'query': jax.random.normal(ks[0], (B, S, D), jnp.float32), 'key': jax.random.normal(ks[1], (B, S, D), jnp.float32), 'value': jax.random.normal(ks[2], (B, S, D), jnp.float32), 'attention_mask': jnp.zeros((B, S, S), jnp.float32), 'WQ_w': jax.random.normal(ks[3], (D, D), jnp.float32) * s, 'WQ_b': jnp.zeros((D,), jnp.float32), 'WK_w': jax.random.normal(ks[4], (D, D), jnp.float32) * s, 'WK_b': jnp.zeros((D,), jnp.float32), 'WV_w': jax.random.normal(ks[5], (D, D), jnp.float32) * s, 'WV_b': jnp.zeros((D,), jnp.float32), 'WO_w': jax.random.normal(ks[6], (D, D), jnp.float32) * s, 'WO_b': jnp.zeros((D,), jnp.float32)}
    _L1_xattn_all = _L1_xattn_setup()
    _L1_xattn_in = {k: v for k, v in _L1_xattn_all.items() if k in ('WQ_w', 'WQ_b', 'WK_w', 'WK_b', 'WV_w', 'WV_b', 'WO_w', 'WO_b')}
    del _L1_xattn_all

    def _L1_ffn_setup():
        import jax, jax.numpy as jnp
        import numpy as np
        TOP_K = 2
        key = jax.random.key(seed)
        ks = jax.random.split(key, 6)
        B, S, D, U, E = (4, 256, 256, 1024, 8)
        return {'x': jax.random.normal(ks[0], (B, S, D), dtype=jnp.float32), 'w_up': jax.random.normal(ks[1], (E, U, D), dtype=jnp.float32), 'w_down': jax.random.normal(ks[2], (E, D, U), dtype=jnp.float32), 'b_up': jax.random.normal(ks[3], (E, U), dtype=jnp.float32), 'b_down': jax.random.normal(ks[4], (E, D), dtype=jnp.float32), 'w_router': jax.random.normal(ks[5], (E, D), dtype=jnp.float32)}
    _L1_ffn_all = _L1_ffn_setup()
    _L1_ffn_in = {k: v for k, v in _L1_ffn_all.items() if k in ('w_up', 'w_down', 'b_up', 'b_down', 'w_router')}
    del _L1_ffn_all
    return {'x': x, 'ctx_1024': ctx_1024, 'mask_BxSxS2_ff0': mask_BxSxS2_ff0, 'L0_attn_w_attn': _L0_attn_in['w_attn'], 'L0_attn_w_proj': _L0_attn_in['w_proj'], 'L0_xattn_wq': _L0_xattn_in['wq'], 'L0_xattn_bq': _L0_xattn_in['bq'], 'L0_xattn_wk': _L0_xattn_in['wk'], 'L0_xattn_bk': _L0_xattn_in['bk'], 'L0_xattn_wv': _L0_xattn_in['wv'], 'L0_xattn_bv': _L0_xattn_in['bv'], 'L0_xattn_wo': _L0_xattn_in['wo'], 'L0_xattn_bo': _L0_xattn_in['bo'], 'L0_ffn_w_router': _L0_ffn_in['w_router'], 'L0_ffn_W_qkv': _L0_ffn_in['W_qkv'], 'L0_ffn_W_out': _L0_ffn_in['W_out'], 'L0_ffn_g1': _L0_ffn_in['g1'], 'L0_ffn_g2': _L0_ffn_in['g2'], 'L0_ffn_W1': _L0_ffn_in['W1'], 'L0_ffn_W2': _L0_ffn_in['W2'], 'L0_ffn_W3': _L0_ffn_in['W3'], 'L1_attn_qkv_w': _L1_attn_in['qkv_w'], 'L1_attn_proj_w': _L1_attn_in['proj_w'], 'L1_attn_proj_b': _L1_attn_in['proj_b'], 'L1_attn_q_norm_w': _L1_attn_in['q_norm_w'], 'L1_attn_k_norm_w': _L1_attn_in['k_norm_w'], 'L1_xattn_WQ_w': _L1_xattn_in['WQ_w'], 'L1_xattn_WQ_b': _L1_xattn_in['WQ_b'], 'L1_xattn_WK_w': _L1_xattn_in['WK_w'], 'L1_xattn_WK_b': _L1_xattn_in['WK_b'], 'L1_xattn_WV_w': _L1_xattn_in['WV_w'], 'L1_xattn_WV_b': _L1_xattn_in['WV_b'], 'L1_xattn_WO_w': _L1_xattn_in['WO_w'], 'L1_xattn_WO_b': _L1_xattn_in['WO_b'], 'L1_ffn_w_up': _L1_ffn_in['w_up'], 'L1_ffn_w_down': _L1_ffn_in['w_down'], 'L1_ffn_b_up': _L1_ffn_in['b_up'], 'L1_ffn_b_down': _L1_ffn_in['b_down'], 'L1_ffn_w_router': _L1_ffn_in['w_router']}

def reference(x, ctx_1024, mask_BxSxS2_ff0, L0_attn_w_attn, L0_attn_w_proj, L0_xattn_wq, L0_xattn_bq, L0_xattn_wk, L0_xattn_bk, L0_xattn_wv, L0_xattn_bv, L0_xattn_wo, L0_xattn_bo, L0_ffn_w_router, L0_ffn_W_qkv, L0_ffn_W_out, L0_ffn_g1, L0_ffn_g2, L0_ffn_W1, L0_ffn_W2, L0_ffn_W3, L1_attn_qkv_w, L1_attn_proj_w, L1_attn_proj_b, L1_attn_q_norm_w, L1_attn_k_norm_w, L1_xattn_WQ_w, L1_xattn_WQ_b, L1_xattn_WK_w, L1_xattn_WK_b, L1_xattn_WV_w, L1_xattn_WV_b, L1_xattn_WO_w, L1_xattn_WO_b, L1_ffn_w_up, L1_ffn_w_down, L1_ffn_b_up, L1_ffn_b_down, L1_ffn_w_router):
    import jax
    import jax.numpy as jnp

    def _L0_attn_ref(x, w_attn, w_proj):
        import jax, jax.numpy as jnp
        import numpy as np
        B, T, C = (4, 512, 256)
        H = 16
        D = C // H
        b, t, c = x.shape
        qkv = x @ w_attn.T
        q, k, v = jnp.split(qkv, 3, axis=2)
        q = q.reshape(b, t, H, D).transpose(0, 2, 1, 3)
        k = k.reshape(b, t, H, D).transpose(0, 2, 1, 3)
        v = v.reshape(b, t, H, D).transpose(0, 2, 1, 3)
        att = jnp.einsum('bhqd,bhkd->bhqk', q, k) / jnp.sqrt(jnp.float32(D))
        causal = jnp.tril(jnp.ones((t, t), dtype=bool))
        att = jnp.where(causal[None, None], att, -jnp.inf)
        att = jax.nn.softmax(att, axis=-1)
        y = jnp.einsum('bhqk,bhkd->bhqd', att, v)
        y = y.transpose(0, 2, 1, 3).reshape(b, t, c)
        return y @ w_proj.T

    def _L0_xattn_ref(v, k, q, wq, bq, wk, bk, wv, bv, wo, bo):
        import jax, jax.numpy as jnp
        import numpy as np
        D_MODEL = 256
        NUM_HEADS = 16
        DEPTH = D_MODEL // NUM_HEADS
        B, S = (2, 512)

        def _split_heads(x):
            b, s, _ = x.shape
            return x.reshape(b, s, NUM_HEADS, DEPTH).transpose(0, 2, 1, 3)
        qh = _split_heads(q @ wq + bq)
        kh = _split_heads(k @ wk + bk)
        vh = _split_heads(v @ wv + bv)
        scale = 1.0 / jnp.sqrt(jnp.asarray(DEPTH, jnp.float32))
        logits = jnp.einsum('bhqd,bhkd->bhqk', qh, kh) * scale
        attn = jax.nn.softmax(logits, axis=-1)
        out = jnp.einsum('bhqk,bhkd->bhqd', attn, vh)
        out = out.transpose(0, 2, 1, 3).reshape(q.shape[0], -1, D_MODEL)
        return out @ wo + bo

    def _L0_ffn_ref(x, w_router, W_qkv, W_out, g1, g2, W1, W2, W3):
        import math
        import jax, jax.numpy as jnp
        import numpy as np
        B, T, D = (4, 1024, 256)
        H = 16
        HD = D // H
        CAP = int(1024 * 0.125)
        DFF = int(D * 4 * 2 / 3)
        EPS = 1e-06

        def rmsnorm(x, g):
            return x * jax.lax.rsqrt(jnp.mean(x * x, axis=-1, keepdims=True) + EPS) * g
        Bq, Tq, Dq = x.shape
        scores = x @ w_router
        _, idx = jax.lax.top_k(scores, CAP)
        x_sel = jnp.take_along_axis(x, idx[:, :, None], axis=1)
        h = rmsnorm(x_sel, g1)
        qkv = (h @ W_qkv.T).reshape(Bq, CAP, 3, H, HD)
        q, k, v = jnp.moveaxis(qkv, 2, 0)
        att = jnp.einsum('bqhd,bkhd->bhqk', q, k) / math.sqrt(HD)
        mask = jnp.triu(jnp.ones((CAP, CAP), bool), 1)
        att = jnp.where(mask, -jnp.inf, att)
        att = jax.nn.softmax(att, axis=-1)
        o = jnp.einsum('bhqk,bkhd->bqhd', att, v).reshape(Bq, CAP, Dq)
        x_attn = o @ W_out.T
        h2 = rmsnorm(x_sel + x_attn, g2)
        x_ff = jax.nn.silu(h2 @ W1.T) * (h2 @ W2.T) @ W3.T
        x_proc = x_sel + x_attn + x_ff
        out = x.at[jnp.arange(Bq)[:, None], idx].set(x_proc)
        return out

    def _L1_attn_ref(x, qkv_w, proj_w, proj_b, q_norm_w, k_norm_w):
        import jax, jax.numpy as jnp
        import numpy as np
        NUM_HEADS = 16
        EPS = 1e-06

        def _rmsnorm(h, w):
            h32 = h.astype(jnp.float32)
            var = jnp.mean(h32 * h32, axis=-1, keepdims=True)
            return (w * (h32 * jax.lax.rsqrt(var + EPS))).astype(h.dtype)
        B, N, C = x.shape
        H = NUM_HEADS
        Dh = C // H
        scale = Dh ** (-0.5)
        qkv = (x @ qkv_w.T).reshape(B, N, 3, H, Dh)
        q, k, v = (qkv[:, :, 0], qkv[:, :, 1], qkv[:, :, 2])
        q = _rmsnorm(q, q_norm_w)
        k = _rmsnorm(k, k_norm_w)
        attn = jnp.einsum('bnhd,bmhd->bhnm', q * scale, k)
        attn = jax.nn.softmax(attn, axis=-1)
        out = jnp.einsum('bhnm,bmhd->bnhd', attn, v).reshape(B, N, C)
        return out @ proj_w.T + proj_b

    def _L1_xattn_ref(query, key, value, attention_mask, WQ_w, WQ_b, WK_w, WK_b, WV_w, WV_b, WO_w, WO_b):
        import jax, jax.numpy as jnp
        import numpy as np
        B, S, D, H = (2, 512, 256, 16)
        HD = D // H

        def _split_heads(x):
            b, s, _ = x.shape
            return x.reshape(b, s, H, HD).transpose(0, 2, 1, 3)
        Q = _split_heads(query @ WQ_w.T + WQ_b)
        K = _split_heads(key @ WK_w.T + WK_b)
        V = _split_heads(value @ WV_w.T + WV_b)
        scale = 1.0 / jnp.sqrt(jnp.float32(HD))
        scores = jnp.einsum('bhqd,bhkd->bhqk', Q, K) * scale
        scores = scores + attention_mask[:, None, :, :]
        attn = jax.nn.softmax(scores, axis=-1)
        out = jnp.einsum('bhqk,bhkd->bhqd', attn, V)
        out = out.transpose(0, 2, 1, 3).reshape(query.shape[0], -1, D)
        return out @ WO_w.T + WO_b

    def _L1_ffn_ref(x, w_up, w_down, b_up, b_down, w_router):
        import jax, jax.numpy as jnp
        import numpy as np
        TOP_K = 2
        logits = jnp.einsum('bsd,ed->bse', x, w_router)
        top_vals, top_idx = jax.lax.top_k(logits, TOP_K)
        router_weights = jax.nn.softmax(top_vals, axis=-1)
        up = jnp.einsum('eud,bsd->bseu', w_up, x) + b_up
        h = jax.nn.gelu(up, approximate=False)
        down = jnp.einsum('edu,bseu->bsed', w_down, h) + b_down
        sel = jnp.take_along_axis(down, top_idx[..., None], axis=2)
        return jnp.einsum('bskd,bsk->bsd', sel, router_weights)
    x = x + _L0_attn_ref(_layernorm(x, axis=-1), L0_attn_w_attn, L0_attn_w_proj)
    x = x + _L0_xattn_ref(ctx_1024, ctx_1024, _layernorm(x, axis=-1), L0_xattn_wq, L0_xattn_bq, L0_xattn_wk, L0_xattn_bk, L0_xattn_wv, L0_xattn_bv, L0_xattn_wo, L0_xattn_bo)
    x = x + _L0_ffn_ref(_layernorm(x, axis=-1), L0_ffn_w_router, L0_ffn_W_qkv, L0_ffn_W_out, L0_ffn_g1, L0_ffn_g2, L0_ffn_W1, L0_ffn_W2, L0_ffn_W3)
    x = x + _L1_attn_ref(_layernorm(x, axis=-1), L1_attn_qkv_w, L1_attn_proj_w, L1_attn_proj_b, L1_attn_q_norm_w, L1_attn_k_norm_w)
    x = x + _L1_xattn_ref(_layernorm(x, axis=-1), ctx_1024, ctx_1024, mask_BxSxS2_ff0, L1_xattn_WQ_w, L1_xattn_WQ_b, L1_xattn_WK_w, L1_xattn_WK_b, L1_xattn_WV_w, L1_xattn_WV_b, L1_xattn_WO_w, L1_xattn_WO_b)
    x = x + _L1_ffn_ref(_layernorm(x, axis=-1), L1_ffn_w_up, L1_ffn_w_down, L1_ffn_b_up, L1_ffn_b_down, L1_ffn_w_router)
    return x

_drawn_inputs = setup_inputs


def setup_inputs(seed=0):
    import zlib

    import numpy as np

    out = dict(_drawn_inputs(seed))
    spreads = {'L0_xattn_bq': (0.0, 0.1),
     'L0_xattn_bk': (0.0, 0.8),
     'L0_xattn_bv': (0.0, 0.1),
     'L0_xattn_bo': (0.0, 0.1),
     'L0_ffn_g1': (1.0, 0.6),
     'L0_ffn_g2': (1.0, 0.6),
     'L1_attn_proj_b': (0.0, 0.1),
     'L1_attn_q_norm_w': (1.0, 0.6),
     'L1_attn_k_norm_w': (1.0, 0.538),
     'L1_xattn_WQ_b': (0.0, 0.1),
     'L1_xattn_WK_b': (0.0, 0.8),
     'L1_xattn_WV_b': (0.0, 0.1),
     'L1_xattn_WO_b': (0.0, 0.1)}
    factors = {'L1_ffn_b_down': 8.0}
    for name, (base, spread) in spreads.items():
        noise = np.random.default_rng([zlib.crc32(name.encode()), seed]).standard_normal(out[name].shape)
        drawn = base * np.exp(spread * noise) if base else spread * noise
        out[name] = jnp.asarray(drawn.astype(out[name].dtype))
    for name, factor in factors.items():
        out[name] = (out[name] * factor).astype(out[name].dtype)
    return out
```

```python
from contextlib import ExitStack

import numpy as np

import concourse.bass as bass
from concourse import mybir

F32 = mybir.dt.float32
BF16 = mybir.dt.bfloat16
I32 = mybir.dt.int32
U32 = mybir.dt.uint32
ALU = mybir.AluOpType
ACT = mybir.ActivationFunctionType
AX = mybir.AxisListType.X

P = 128
B, S, D, H = 8, 512, 256, 16
HD = D // H
TT = S // P
KD = D // P
NG, GH = 4, 4
SPLITS = 6
ROWS = SPLITS * HD
SHIFT = ROWS
KROWS = ROWS + 3
NEG = -1.0e30
Q_PART = (0, 1, 2, 0, 1, 0)
K_PART = (0, 0, 0, 1, 1, 2)


def wait(eng, sem, value):
    if not isinstance(value, int) or value > 0:
        eng.wait_ge(sem, value)


def hold(eng, sem, value, passed):
    if not isinstance(value, int):
        eng.wait_ge(sem, value)
        eng.sem_inc(passed)
    elif value > 0:
        eng.wait_ge(sem, value)


def make_constants(nc, c):
    made = nc.alloc_semaphore("constants_made")

    with nc.Block() as block:
        @block.gpsimd
        def _(pool):
            pool.memset(c.ident[:], 0.0).then_inc(made, 1)
            pool.memset(c.causal_kq[:], 0.0).then_inc(made, 1)
            pool.memset(c.causal_qk[:], 0.0).then_inc(made, 1)
            pool.memset(c.head_ones[:], 1.0).then_inc(made, 1)
            pool.memset(c.minus_half[:], -0.5).then_inc(made, 1)
            pool.wait_ge(made, 5)
            pool.affine_select(out=c.ident[:], in_=c.ident[:], compare_op=ALU.not_equal, fill=1.0, base=0,
                               pattern=[[-1, P]], channel_multiplier=1).then_inc(made, 1)
            pool.affine_select(out=c.causal_kq[:], in_=c.causal_kq[:], compare_op=ALU.is_ge, fill=NEG, base=0,
                               pattern=[[1, P]], channel_multiplier=-1).then_inc(made, 1)
            pool.affine_select(out=c.causal_qk[:], in_=c.causal_qk[:], compare_op=ALU.is_ge, fill=NEG, base=0,
                               pattern=[[-1, P]], channel_multiplier=1).then_inc(made, 1)
            view = c.head_ones[:].rearrange("p (h d) -> p h d", d=HD)
            pool.affine_select(out=view, in_=view, compare_op=ALU.is_ge, fill=0.0, base=0,
                               pattern=[[-HD, P // HD], [0, HD]], channel_multiplier=1).then_inc(made, 1)
            pool.wait_ge(made, 9)
            pool.affine_select(out=view, in_=view, compare_op=ALU.is_ge, fill=0.0, base=HD - 1,
                               pattern=[[HD, P // HD], [0, HD]], channel_multiplier=-1).then_inc(made, 1)
            pool.tensor_copy(c.ident_b[:], c.ident[:]).then_inc(made, 1)
            pool.wait_ge(made, 11)
    return [made]


def self_attention(nc, c, name, w_qk, w_v, w_o, causal, norm_weights=None, x_in=None):
    norm = norm_weights is not None
    made = []

    def sem(what):
        s = nc.alloc_semaphore(f"{name}_{what}")
        made.append(s)
        return s

    with ExitStack() as ctx:
        def sb(what, shape, dt=F32):
            return ctx.enter_context(nc.sbuf_tensor(f"{name}_{what}", shape, dt))

        def ps(what, shape, dt=F32):
            return ctx.enter_context(nc.psum_tensor(f"{name}_{what}", shape, dt))

        wqk = sb("wqk", [P, KD, 2 * D])
        wv = sb("wv", [P, KD, D])
        wo = sb("wo", [P, NG, D])
        stats = sb("stats", [P, TT, 6])
        mean_var = sb("mean_var", [P, TT, 2])
        var_eps = sb("var_eps", [P, TT])
        rstd = sb("rstd", [P, TT])
        xn = sb("xn", [P, TT, D])
        xnT = sb("xnT", [P, KD, S])
        qk = sb("qk", [P, 4, S])
        parts = sb("parts", [P, 4, 3, S], BF16)
        rest = sb("rest", [P, 4, S])
        q_stack = sb("q_stack", [P, H, S], BF16)
        k_stack = sb("k_stack", [P, H, S], BF16)
        values = sb("values", [P, TT, H, 32])
        neg_max = sb("neg_max", [P, 2, TT, GH])
        shift1 = sb("shift1", [GH, 2, 3, S], BF16)
        shift_rest = sb("shift_rest", [GH, 2, S])
        probs = sb("probs", [P, 8, S])
        o_raw = sb("o_raw", [P, 2, S])
        denom = sb("denom", [P, 2, S])
        r_denom = sb("r_denom", [P, 2, S])
        log_sum = sb("log_sum", [P, S])
        residue = sb("residue", [P, S])
        o_norm = sb("o_norm", [P, NG, S])
        if norm:
            squares = sb("squares", [P, 2, S])
            log_ms = sb("log_ms", [P, 2, S])
            r_rms = sb("r_rms", [P, 2, S])
            qk_raw = sb("qk_raw", [P, 4, S])
            gains = sb("gains", [P, 2])
            rms_eps = sb("rms_eps", [P, 1])
        scratch = nc.dram_tensor(f"{name}_parts_dram", [4, P, 3, S], BF16).ap()

        general = ps("general", [P, 2, S])
        max_ps = ps("max_ps", [P, 2, S])
        score_ps = ps("score_ps", [P, 3, S])
        out_ps = ps("out_ps", [P, S])

        ready = sem("ready")
        pool_passed, dve_passed, sp_passed = sem("pool_passed"), sem("dve_passed"), sem("sp_passed")
        loaded = sem("loaded")
        x_loaded = [sem(f"x_loaded{b}") for b in range(B)] if x_in is not None else None
        scaled = sem("scaled")
        ln_stats, ln_aggr, ln_eps, ln_rstd, ln_done = (sem(s) for s in ("ln_stats", "ln_aggr", "ln_eps", "ln_rstd", "ln_done"))
        xt_full, xt_copied = sem("xt_full"), sem("xt_copied")
        qk_full, qk_copied = sem("qk_full"), sem("qk_copied")
        sq_done, ss_full, ss_log, ss_rstd, qk_normed = (sem(s) for s in ("sq_done", "ss_full", "ss_log", "ss_rstd", "qk_normed")) if norm else [None] * 5
        part0_cut, rest_done, part1_cut, part2_cut = (sem(s) for s in ("part0_cut", "rest_done", "part1_cut", "part2_cut"))
        parts_stored = [sem(f"parts_stored{i}") for i in range(2)]
        stacked = [sem(f"stacked{g}") for g in range(NG)]
        max_full, max_read = sem("max_full"), sem("max_read")
        mt_full, shift_a, shift_r, shift_b, shift_c = (sem(s) for s in ("mt_full", "shift_a", "shift_r", "shift_b", "shift_c"))
        shift_placed = [sem(f"shift_placed{g}") for g in range(NG)]
        score_full, exp_done, pv_done = sem("score_full"), sem("exp_done"), sem("pv_done")
        o_copied, denom_done, recip_done, o_done = sem("o_copied"), sem("denom_done"), sem("recip_done"), sem("o_done")
        log_done, guess_done, residue_done = sem("log_done"), sem("guess_done"), sem("residue_done")
        v_full, v_copied = sem("v_full"), sem("v_copied")
        e_full, x_done = sem("e_full"), sem("x_done")

        ITEMS = range(4)
        COLUMNS = (0, D, P, D + P)

        order = ["mt1", "xt0", "xt1", "p0", "p1", "p2"] + (["s0", "p3", "s1", "s2", "s3"] if norm else ["p3"])
        order += ["mt2", "mt3", "mt0", "v0", "v1", "e0", "e1"]
        assert len(order) % 2 == 0
        bank = {what: n % 2 for n, what in enumerate(order)}

        def width(j):
            return S - P * j if causal else S

        with nc.Block() as block:
            @block.sync
            def _(sp):
                def load_x(b):
                    sp.dma_start(c.x[:, b], x_in[b].rearrange("(t p) d -> p t d", p=P)).then_inc(x_loaded[b], 16)

                if x_in is not None:
                    load_x(0)
                sp.dma_start(wqk[:], w_qk.rearrange("(k p) n -> p k n", p=P)).then_inc(loaded, 16)
                sp.dma_start(wv[:], w_v.rearrange("(k p) n -> p k n", p=P)).then_inc(loaded, 16)
                sp.dma_start(wo[:], w_o.rearrange("g p n -> p g n")).then_inc(loaded, 16)
                if norm:
                    for i in range(2):
                        sp.dma_start(gains[:, i:i + 1], norm_weights[i]).then_inc(loaded, 16)

                if x_in is not None:
                    for b in range(1, B):
                        load_x(b)

                def stack(b, g):
                    half = g // 2
                    if g % 2 == 0:
                        for item in (2 * half, 2 * half + 1):
                            hold(sp, part2_cut, 4 * b + item + 1, sp_passed)
                            hold(sp, stacked[2 * half], 192 * b, sp_passed)
                            hold(sp, stacked[2 * half + 1], 192 * b, sp_passed)
                            sp.dma_start(scratch[item], parts[:, item]).then_inc(parts_stored[half], 16)
                        hold(sp, parts_stored[half], 32 * b + 32, sp_passed)
                    rows = slice((g % 2) * 64, (g % 2) * 64 + 64)
                    for stk, item, which in ((q_stack, 2 * half, Q_PART), (k_stack, 2 * half + 1, K_PART)):
                        for r, part in enumerate(which):
                            sp.dma_start(stk[HD * r:HD * r + HD, GH * g:GH * g + GH, :],
                                         scratch[item, rows, part, :].rearrange("(h d) t -> d h t", d=HD)
                                         ).then_inc(stacked[g], 16)

                def place_shift(number, g):
                    hold(sp, shift_c, number, sp_passed)
                    for i in range(3):
                        sp.dma_start(q_stack[SHIFT + i:SHIFT + i + 1, GH * g:GH * g + GH, :],
                                     shift1[:, g % 2, i, :]).then_inc(shift_placed[g], 16)

                for g in range(NG):
                    stack(0, g)
                place_shift(1, 0)

                def sequence(b):
                    for g in range(NG):
                        place_shift(4 * b + g + 2, (g + 1) % NG)
                        hold(sp, score_full, 64 * b + 16 * g + 16, sp_passed)
                        stack(b + 1, g)

                sequence(0)
                with sp.Fori(1, B - 1) as b:
                    sequence(b)
                for g in (1, 2, 3):
                    place_shift(4 * (B - 1) + g + 1, g)

            @block.gpsimd
            def _(pool):
                pool.memset(values[:, :, :, HD:], 1.0).then_inc(ready, 1)
                pool.wait_ge(ready, 1)
                pool.memset(k_stack[SHIFT:KROWS], 1.0).then_inc(ready, 1)
                pool.wait_ge(ready, 2)
                if norm:
                    pool.memset(rms_eps[:], 1e-6).then_inc(ready, 1)
                pool.wait_ge(loaded, 16 * (5 if norm else 3))
                if norm:
                    pool.tensor_scalar(gains[:, 0:1], gains[:, 0:1], HD ** -0.5, None, ALU.mult).then_inc(scaled, 1)
                else:
                    pool.tensor_scalar(wqk[:, :, 0:D], wqk[:, :, 0:D], HD ** -0.5, None, ALU.mult).then_inc(scaled, 1)

                def layer_norm(b):
                    hold(pool, ln_aggr, 4 * b + 4, pool_passed)
                    pool.tensor_scalar(var_eps[:], mean_var[:, :, 1], 1e-5, None, ALU.add).then_inc(ln_eps, 1)
                    pool.wait_ge(ln_eps, b + 1)
                    pool.tensor_tensor(rstd[:], var_eps[:], c.minus_half[:, 0:TT], ALU.pow).then_inc(ln_rstd, 1)

                def square(b, i):
                    pool.wait_ge(qk_copied, 4 * b + i + 1)
                    if i >= 2:
                        pool.wait_ge(ss_full, 4 * b + i - 1)
                    pool.tensor_tensor(squares[:, i % 2], qk_raw[:, i], qk_raw[:, i], ALU.mult).then_inc(sq_done, 1)

                def square_all(b):
                    for i in ITEMS:
                        square(b, i)

                def cut(b, i):
                    if norm:
                        pool.wait_ge(part0_cut, 4 * b + i + 1)
                        pool.tensor_tensor(rest[:, i], qk[:, i], parts[:, i, 0], ALU.subtract).then_inc(rest_done, 1)
                    pool.wait_ge(part1_cut, 4 * b + i + 1)
                    pool.tensor_tensor(parts[:, i, 2], rest[:, i], parts[:, i, 1], ALU.subtract).then_inc(part2_cut, 1)

                def cut_all(b):
                    for i in ITEMS:
                        cut(b, i)

                def shift(b, g):
                    n = 4 * b + g
                    hold(pool, shift_r, n + 1, pool_passed)
                    pool.tensor_copy(shift1[:, g % 2, 1], shift_rest[:, g % 2]).then_inc(shift_b, 1)
                    pool.wait_ge(shift_b, n + 1)
                    pool.tensor_tensor(shift1[:, g % 2, 2], shift_rest[:, g % 2], shift1[:, g % 2, 1],
                                       ALU.subtract).then_inc(shift_c, 1)

                def normalise(b, g):
                    pool.wait_ge(recip_done, 4 * b + g + 1)
                    wait(pool, e_full, 2 * b)
                    pool.tensor_tensor(o_norm[:, g], o_raw[:, g % 2], r_denom[:, g % 2], ALU.mult).then_inc(o_done, 1)

                layer_norm(0)
                if norm:
                    square_all(0)
                cut_all(0)
                shift(0, 0)

                def sequence(b):
                    layer_norm(b + 1)
                    shift(b, 1)
                    if norm:
                        square_all(b + 1)
                    cut_all(b + 1)
                    normalise(b, 0)
                    shift(b, 2)
                    normalise(b, 1)
                    shift(b, 3)
                    normalise(b, 2)
                    shift(b + 1, 0)
                    normalise(b, 3)

                sequence(0)
                with pool.Fori(1, B - 1) as b:
                    sequence(b)
                last = B - 1
                for g in range(NG):
                    if g + 1 < NG:
                        shift(last, g + 1)
                    normalise(last, g)

            @block.scalar
            def _(act):
                act.preload_act_table_set("natural_log_exp_and_others")
                act.wait_ge(ready, 3 if norm else 2)

                def transposed(b):
                    for k in range(KD):
                        act.wait_ge(xt_full, 2 * b + k + 1)
                        act.activation(xnT[:, k], general[:, bank[f"xt{k}"]], ACT.Copy).then_inc(xt_copied, 1)

                def mean_square(b, i):
                    act.wait_ge(ss_full, 4 * b + i + 1)
                    wait(act, qk_normed, 4 * b + i - 1)
                    act.activation(log_ms[:, i % 2], general[:, bank[f"s{i}"]], ACT.Ln, bias=rms_eps[:],
                                   scale=1.0 / HD).then_inc(ss_log, 1)
                    act.wait_ge(ss_log, 4 * b + i + 1)
                    act.activation(r_rms[:, i % 2], log_ms[:, i % 2], ACT.Exp, scale=-0.5).then_inc(ss_rstd, 1)

                def projected(b):
                    for i in ITEMS:
                        act.wait_ge(qk_full, 4 * b + i + 1)
                        if norm:
                            wait(act, qk_normed, 4 * b + i - 3)
                            act.activation(qk_raw[:, i], general[:, bank[f"p{i}"]], ACT.Copy).then_inc(qk_copied, 1)
                            if i >= 2:
                                mean_square(b, i - 2)
                        else:
                            first_part(b, i)
                    if norm:
                        mean_square(b, 2)
                        mean_square(b, 3)

                def first_part(b, i):
                    wait(act, parts_stored[i // 2], 32 * b)
                    if norm:
                        act.wait_ge(qk_normed, 4 * b + i + 1)
                    act.activation(parts[:, i, 0], qk[:, i] if norm else general[:, bank[f"p{i}"]], ACT.Copy).then_inc(part0_cut, 1)

                def second_part(b, i):
                    act.wait_ge(rest_done, 4 * b + i + 1)
                    act.activation(parts[:, i, 1], rest[:, i], ACT.Copy).then_inc(part1_cut, 1)

                def shift(b, g):
                    act.wait_ge(mt_full, 4 * b + g + 1)
                    wait(act, shift_placed[(g + 2) % NG], 48 * b + (48 if g >= 2 else 0))
                    act.activation(shift1[:, g % 2, 0], general[0:GH, bank[f"mt{g}"]], ACT.Copy).then_inc(shift_a, 1)

                def invert(b, g):
                    n = 4 * b + g
                    act.wait_ge(denom_done, n + 1)
                    act.activation(log_sum[:], denom[:, g % 2], ACT.Ln).then_inc(log_done, 1)
                    act.wait_ge(log_done, n + 1)
                    wait(act, o_done, n - 1)
                    act.activation(r_denom[:, g % 2], log_sum[:], ACT.Exp, scale=-1.0).then_inc(guess_done, 1)

                def copy_out(b, g):
                    n = 4 * b + g
                    act.wait_ge(pv_done, 4 * n + 4)
                    wait(act, o_done, n - 1)
                    act.activation(o_raw[:, g % 2], out_ps[:], ACT.Copy).then_inc(o_copied, 1)

                def group(b, g, after):
                    n = 4 * b + g
                    for j in range(TT):
                        w = width(j)
                        wait(act, pv_done, 4 * n + j - 1)
                        for h in range(GH):
                            i = 4 * j + h
                            act.wait_ge(score_full, 16 * n + i + 1)
                            act.activation(probs[:, i % 8, 0:w], score_ps[:, i % 3, 0:w], ACT.Exp).then_inc(exp_done, 1)
                        for work, *of in after.get(j, ()):
                            work(*of)

                def cuts(b):
                    if norm:
                        return ([(first_part, b, 0), (first_part, b, 1)],
                                [(second_part, b, 0), (first_part, b, 2), (second_part, b, 1), (first_part, b, 3)],
                                [(second_part, b, 2), (second_part, b, 3)])
                    return [(second_part, b, 0), (second_part, b, 1)], [(second_part, b, 2), (second_part, b, 3)], []

                transposed(0)
                projected(0)
                for work, *of in sum(cuts(0), []):
                    work(*of)
                shift(0, 0)

                def sequence(b):
                    group(b, 0, {1: [(shift, b, 1)]})
                    transposed(b + 1)
                    copy_out(b, 0)
                    projected(b + 1)
                    c0, c1, c2 = cuts(b + 1)
                    group(b, 1, {0: c0, 1: [(shift, b, 2), (invert, b, 0)] + c1, 2: c2})
                    group(b, 2, {0: [(copy_out, b, 1)], 1: [(shift, b, 3), (invert, b, 1)]})
                    group(b, 3, {0: [(copy_out, b, 2)], 1: [(shift, b + 1, 0), (invert, b, 2)]})
                    copy_out(b, 3)
                    invert(b, 3)

                sequence(0)
                with act.Fori(1, B - 1) as b:
                    sequence(b)
                last = B - 1
                group(last, 0, {1: [(shift, last, 1)]})
                for g in range(1, NG):
                    group(last, g, {0: [(copy_out, last, g - 1)],
                                    1: ([(shift, last, g + 1)] if g < 3 else []) + [(invert, last, g - 1)]})
                copy_out(last, 3)
                invert(last, 3)

            @block.vector
            def _(dve):
                def layer_norm(b):
                    if x_in is not None:
                        x_arrived(dve, b)
                    wait(dve, ln_aggr, 4 * b)
                    for t in range(TT):
                        dve.bn_stats(stats[:, t], xtile(b, t)).then_inc(ln_stats, 1)
                    for t in range(TT):
                        hold(dve, ln_stats, 4 * b + t + 1, dve_passed)
                        if t == 0:
                            hold(dve, ln_eps, b, dve_passed)
                            hold(dve, ln_done, 4 * b, dve_passed)
                        dve.bn_aggr(mean_var[:, t], stats[:, t]).then_inc(ln_aggr, 1)
                    dve.wait_ge(ln_aggr, 4 * b + 4)
                    wait(dve, xt_full, 2 * b)
                    dve.wait_ge(ln_rstd, b + 1)
                    for t in range(TT):
                        dve.tensor_scalar(xn[:, t], xtile(b, t), mean_var[:, t, 0:1], rstd[:, t:t + 1],
                                          ALU.subtract, ALU.mult).then_inc(ln_done, 1)

                def xtile(b, t):
                    return c.x[:, b, t] if isinstance(b, int) else c.x[:, bass.ds(b, 1), t, :]

                def x_arrived(eng, b):
                    for s in (x_loaded[b:b + 1] if b < 1 else x_loaded[1:]) if isinstance(b, int) else ():
                        eng.wait_ge(s, 16)

                def normed(b, items):
                    for i in items:
                        dve.wait_ge(ss_rstd, 4 * b + i + 1)
                        wait(dve, part2_cut, 4 * b + i - 3)
                        dve.scalar_tensor_tensor(qk[:, i], qk_raw[:, i], gains[:, i % 2:i % 2 + 1], r_rms[:, i % 2],
                                                 ALU.mult, ALU.mult).then_inc(qk_normed, 1)

                def leftover(b):
                    for i in ITEMS:
                        dve.wait_ge(part0_cut, 4 * b + i + 1)
                        wait(dve, part2_cut, 4 * b + i - 3)
                        dve.tensor_tensor(rest[:, i], general[:, bank[f"p{i}"]], parts[:, i, 0], ALU.subtract).then_inc(rest_done, 1)

                def maxima(b, g, tiles):
                    n = 4 * b + g
                    for i in tiles:
                        h, t = i // TT, i % TT
                        if i == 0:
                            wait(dve, mt_full, n - 1)
                        dve.wait_ge(max_full, 16 * n + i + 1)
                        w = P * (t + 1) if causal else S
                        dve.tensor_reduce(neg_max[:, g % 2, t, h:h + 1], max_ps[:, i % 2, 0:w], AX, ALU.max,
                                          negate=True).then_inc(max_read, 1)

                def shift(b, g):
                    n = 4 * b + g
                    dve.wait_ge(shift_a, n + 1)
                    wait(dve, shift_c, n - 1)
                    dve.tensor_tensor(shift_rest[:, g % 2], general[0:GH, bank[f"mt{g}"]], shift1[:, g % 2, 0],
                                      ALU.subtract).then_inc(shift_r, 1)

                def spread(b, g):
                    n = 4 * b + g
                    hold(dve, o_copied, n + 1, dve_passed)
                    dve.stream_shuffle(denom[:, g % 2], o_raw[:, g % 2], mask=[HD + d % HD for d in range(32)]).then_inc(denom_done, 1)

                def refine(b, g):
                    n = 4 * b + g
                    dve.wait_ge(guess_done, n + 1)
                    dve.scalar_tensor_tensor(residue[:], denom[:, g % 2], -1.0, r_denom[:, g % 2], ALU.mult, ALU.mult).then_inc(residue_done, 1)
                    dve.wait_ge(residue_done, n + 1)
                    dve.scalar_tensor_tensor(r_denom[:, g % 2], residue[:], 2.0, r_denom[:, g % 2], ALU.add, ALU.mult).then_inc(recip_done, 1)

                def valued(b):
                    for t in range(2):
                        dve.wait_ge(v_full, 2 * b + t + 1)
                        dve.tensor_copy(values[:, 2 * t:2 * t + 2, :, 0:HD],
                                        general[:, bank[f"v{t}"]].rearrange("p (t h d) -> p t h d", t=2, d=HD)).then_inc(v_copied, 1)

                def add(b):
                    for t in range(2):
                        dve.wait_ge(e_full, 2 * b + t + 1)
                        dst = c.x[:, b, 2 * t:2 * t + 2] if isinstance(b, int) else c.x[:, bass.ds(b, 1), 2 * t:2 * t + 2, :]
                        dve.tensor_tensor(dst, general[:, bank[f"e{t}"]].rearrange("p (t d) -> p t d", t=2), dst, ALU.add).then_inc(x_done, 1)

                def group(b, g, nxt, turned, behind=()):
                    def some(tiles):
                        if nxt is not None:
                            maxima(*nxt, tiles)

                    some(range(2))
                    for work, *of in behind:
                        work(*of)
                    some(range(2, 6))
                    if g >= 2 or (g == 1 and isinstance(b, int) and b == B - 1):
                        spread(b, g - 1)
                    some(range(6, 10))
                    if turned is not None:
                        shift(*turned)
                    if g >= 1:
                        refine(b, g - 1)
                    some(range(10, 16))

                dve.wait_ge(ready, 3 if norm else 2)
                layer_norm(0)
                if norm:
                    normed(0, ITEMS)
                else:
                    leftover(0)
                valued(0)
                maxima(0, 0, range(16))
                maxima(0, 1, range(16))
                shift(0, 0)

                def sequence(b):
                    layer_norm(b + 1)
                    group(b, 0, (b, 2), (b, 1))
                    spread(b, 0)
                    if norm:
                        normed(b + 1, (0, 1))
                    else:
                        leftover(b + 1)
                    group(b, 1, (b, 3), (b, 2), [(normed, b + 1, (2, 3))] if norm else ())
                    group(b, 2, (b + 1, 0), (b, 3))
                    group(b, 3, (b + 1, 1), (b + 1, 0))
                    spread(b, 3)
                    valued(b + 1)
                    refine(b, 3)
                    add(b)

                sequence(0)
                with dve.Fori(1, B - 1) as b:
                    sequence(b)
                last = B - 1
                group(last, 0, (last, 2), (last, 1))
                group(last, 1, (last, 3), (last, 2))
                group(last, 2, None, (last, 3))
                group(last, 3, None, None)
                spread(last, 3)
                refine(last, 3)
                add(last)
                dve.wait_ge(x_done, 2 * B)

            @block.tensor
            def _(pe):
                freed = qk_copied if norm else rest_done

                def transposes(b):
                    for k in range(KD):
                        pe.wait_ge(ln_done, 4 * b + 4)
                        if k == 0:
                            wait(pe, x_done, 2 * b - 2)
                        else:
                            wait(pe, shift_r, 4 * b - 2)
                        for t in range(TT):
                            last = pe.transpose(general[:, bank[f"xt{k}"], P * t:P * t + P], xn[:, t, P * k:P * k + P], c.ident[:])
                        last.then_inc(xt_full, 1)

                def project(b, i, *free):
                    wait(pe, *free)
                    for k in range(KD):
                        last = pe.matmul(general[:, bank[f"p{i}"]], wqk[:, k, COLUMNS[i]:COLUMNS[i] + P], xnT[:, k],
                                         start=(k == 0), stop=(k == KD - 1))
                    last.then_inc(qk_full, 1)

                def sum_squares(b, i, *free):
                    wait(pe, *free)
                    pe.wait_ge(sq_done, 4 * b + i + 1)
                    pe.matmul(general[:, bank[f"s{i}"]], c.head_ones[:], squares[:, i % 2], start=True, stop=True).then_inc(ss_full, 1)

                def projections(b):
                    project(b, 0, xt_copied, 2 * b + 2)
                    project(b, 1, xt_copied, 2 * b + 2)
                    project(b, 2, freed, 4 * b + 1)
                    if norm:
                        sum_squares(b, 0, freed, 4 * b + 2)
                        project(b, 3, freed, 4 * b + 3)
                        sum_squares(b, 1, ss_log, 4 * b + 1)
                        sum_squares(b, 2, freed, 4 * b + 4)
                        sum_squares(b, 3, ss_log, 4 * b + 2)
                    else:
                        project(b, 3, freed, 4 * b + 2)

                def value_rows(b, t, *free):
                    wait(pe, *free)
                    for t2 in range(2):
                        tok = P * (2 * t + t2)
                        for k in range(KD):
                            last = pe.matmul(general[:, bank[f"v{t}"], D * t2:D * t2 + D], xnT[:, k, tok:tok + P], wv[:, k],
                                             start=(k == 0), stop=(k == KD - 1))
                    last.then_inc(v_full, 1)

                def max_tile(b, g, i):
                    n = 16 * (4 * b + g) + i
                    h, t = GH * g + i // TT, i % TT
                    if i == 0:
                        pe.wait_ge(stacked[g], 192 * b + 192)
                    wait(pe, max_read, n - 1)
                    w = P * (t + 1) if causal else S
                    last = pe.matmul(max_ps[:, i % 2, 0:w], q_stack[0:ROWS, h, P * t:P * t + P], k_stack[0:ROWS, h, 0:w],
                                     start=True, stop=not causal)
                    if causal:
                        last = pe.matmul(max_ps[:, i % 2, w - P:w], c.ident_b[:], c.causal_qk[:], start=False, stop=True)
                    last.then_inc(max_full, 1)

                def turn_maxima(b, g, *free):
                    wait(pe, *free)
                    pe.wait_ge(max_read, 16 * (4 * b + g) + 16)
                    for t in range(TT):
                        last = pe.transpose(general[0:GH, bank[f"mt{g}"], P * t:P * t + P], neg_max[:, g % 2, t], c.ident[:])
                    last.then_inc(mt_full, 1)

                def with_values(b, g, j):
                    n = 4 * b + g
                    pe.wait_ge(exp_done, 16 * n + 4 * j + 4)
                    if j == 0:
                        pe.wait_ge(v_copied, 2 * b + 2)
                        wait(pe, o_copied, n)
                    w = width(j)
                    for h in range(GH):
                        last = pe.matmul(out_ps[32 * h:32 * h + 32, S - w:S], values[:, j, GH * g + h], probs[:, (4 * j + h) % 8, 0:w],
                                         start=(j == 0), stop=(j == TT - 1), tile_position=(0, 32 * h))
                    last.then_inc(pv_done, 1)

                def group(b, g, nxt, turn, carried=None):
                    n = 4 * b + g
                    pe.wait_ge(shift_placed[g], 48 * b + 48)
                    for j in range(TT):
                        w = width(j)
                        for h in range(GH):
                            i = 4 * j + h
                            wait(pe, exp_done, 16 * n + (i - 2 if i >= 3 else (0, -2, -1)[i]))
                            head = GH * g + h
                            last = pe.matmul(score_ps[:, i % 3, 0:w], k_stack[0:KROWS, head, P * j:P * j + P],
                                             q_stack[0:KROWS, head, S - w:S], start=True, stop=not causal)
                            if causal:
                                last = pe.matmul(score_ps[:, i % 3, 0:P], c.ident_b[:], c.causal_kq[:], start=False, stop=True)
                            last.then_inc(score_full, 1)
                            if nxt is not None:
                                max_tile(*nxt, i)
                        if j == 0 and carried is not None:
                            with_values(*carried, TT - 1)
                        if j == 1 and turn is not None:
                            turn_maxima(*turn)
                        if j >= 1:
                            with_values(b, g, j - 1)

                def output(b, t, *free):
                    wait(pe, *free)
                    pe.wait_ge(o_done, 4 * b + 4)
                    for t2 in range(2):
                        tok = P * (2 * t + t2)
                        for g in range(NG):
                            last = pe.matmul(general[:, bank[f"e{t}"], D * t2:D * t2 + D], o_norm[:, g, tok:tok + P], wo[:, g],
                                             start=(g == 0), stop=(g == NG - 1))
                    last.then_inc(e_full, 1)

                pe.wait_ge(loaded, 16 * (5 if norm else 3))
                pe.wait_ge(scaled, 1)
                pe.wait_ge(ready, 3 if norm else 2)
                transposes(0)
                projections(0)
                value_rows(0, 0, ss_log if norm else freed, 4)
                value_rows(0, 1, ss_log if norm else freed, 4)
                for g in range(2):
                    for i in range(16):
                        max_tile(0, g, i)
                turn_maxima(0, 0, v_copied, 2)
                pe.wait_ge(shift_r, 1)

                left = ((ss_log, 3), (ss_log, 4)) if norm else ((freed, 3), (freed, 4))

                def sequence(b):
                    group(b, 0, (b, 2), (b, 1, x_done, 2 * b - 1))
                    transposes(b + 1)
                    with_values(b, 0, TT - 1)
                    projections(b + 1)
                    group(b, 1, (b, 3), (b, 2, left[0][0], 4 * b + 4 + left[0][1]))
                    group(b, 2, (b + 1, 0), (b, 3, left[1][0], 4 * b + 4 + left[1][1]), (b, 1))
                    group(b, 3, (b + 1, 1), (b + 1, 0, shift_r, 4 * b + 3), (b, 2))
                    with_values(b, 3, TT - 1)
                    value_rows(b + 1, 0, shift_r, 4 * b + 4)
                    value_rows(b + 1, 1, shift_r, 4 * b + 5)
                    output(b, 0, v_copied, 2 * b + 3)
                    output(b, 1, v_copied, 2 * b + 4)

                sequence(0)
                with pe.Fori(1, B - 1) as b:
                    sequence(b)
                last = B - 1
                group(last, 0, (last, 2), (last, 1, x_done, 2 * last - 1))
                group(last, 1, (last, 3), (last, 2, x_done, 2 * last), (last, 0))
                group(last, 2, None, (last, 3, shift_r, 4 * last + 2), (last, 1))
                group(last, 3, None, None, (last, 2))
                with_values(last, 3, TT - 1)
                output(last, 0, shift_r, 4 * last + 4)
                output(last, 1, shift_r, 4 * last + 3)

    nc.clear_and_free_semaphores(made)
    nc.all_engine_barrier()


def cross_attention(nc, c, name, w_q, w_k, w_v, w_o, bias_q, bias_k, bias_v, ctx_t, ctx_twice, mask_t=None):
    masked = mask_t is not None
    made = []
    S2 = ctx_t.shape[1] // B
    NP = H // 2

    def sem(what):
        s = nc.alloc_semaphore(f"{name}_{what}")
        made.append(s)
        return s

    with ExitStack() as ctx:
        def sb(what, shape, dt=F32):
            return ctx.enter_context(nc.sbuf_tensor(f"{name}_{what}", shape, dt))

        def ps(what, shape, dt=F32):
            return ctx.enter_context(nc.psum_tensor(f"{name}_{what}", shape, dt))

        wq, wk, wv = (sb(what, [P, KD, D]) for what in ("wq", "wk", "wv"))
        wo = sb("wo", [P, NG, D])
        bias = sb("bias", [P, 4])
        bias_row = sb("bias_row", [P, D])
        ctx_all = sb("ctx_all", [P, KD, S])
        ctx_one = sb("ctx_one", [P, KD, P])
        stats = sb("stats", [P, TT, 6])
        mean_var = sb("mean_var", [P, TT, 2])
        var_eps = sb("var_eps", [P, TT])
        rstd = sb("rstd", [P, TT])
        xn = sb("xn", [P, TT, D])
        xnT = sb("xnT", [P, KD, S])
        parts = sb("parts", [P, 2, 3, S], BF16)
        rest = sb("rest", [P, 2, S])
        q_stack = sb("q_stack", [P, 2, H, S], BF16)
        k_stack = sb("k_stack", [P, H, B * S2], BF16)
        k_one = sb("k_one", [P, H, S2], BF16)
        values = sb("values", [P, NP, 64])
        neg_max = sb("neg_max", [P, TT, H])
        shift1 = sb("shift1", [H, 3, S], BF16)
        shift_rest = sb("shift_rest", [H, S])
        probs = sb("probs", [P, 4, S])
        o_raw, denom, r_denom, o_norm = (sb(what, [P, NG, S]) for what in ("o_raw", "denom", "r_denom", "o_norm"))
        log_sum, residue = sb("log_sum", [P, S]), sb("residue", [P, S])
        if masked:
            mask_raw = sb("mask_raw", [P, S])
            mask_rest = sb("mask_rest", [P, S])
            mask12 = sb("mask12", [P, 2, S], BF16)
            mask3 = sb("mask3", [P, 2, S], BF16)
            spread_keys = sb("spread_keys", [P, S], BF16)
        scratch = nc.dram_tensor(f"{name}_parts_dram", [2, P, 3, S], BF16).ap()

        general = ps("general", [P, 2, S])
        max_ps = ps("max_ps", [P, 2, S])
        score_ps = ps("score_ps", [P, 2, S])
        out_ps = ps("out_ps", [P, 2, S])

        ready, scaled = sem("ready"), sem("scaled")
        pool_passed, dve_passed, sp_passed = sem("pool_passed"), sem("dve_passed"), sem("sp_passed")
        loaded, ctx_loaded = sem("loaded"), sem("ctx_loaded")
        ln_stats, ln_aggr, ln_eps, ln_rstd, ln_done = (sem(s) for s in ("ln_stats", "ln_aggr", "ln_eps", "ln_rstd", "ln_done"))
        xt_full, xt_copied, qk_full = sem("xt_full"), sem("xt_copied"), sem("qk_full")
        part0_cut, rest_done, part1_cut, part2_cut = (sem(s) for s in ("part0_cut", "rest_done", "part1_cut", "part2_cut"))
        parts_stored, k_stacked, stacked, k_copied = (sem(s) for s in ("parts_stored", "k_stacked", "stacked", "k_copied"))
        max_full, max_read = sem("max_full"), sem("max_read")
        mt_full, shift_a, shift_r, shift_b, shift_c, shift_placed = (
            sem(s) for s in ("mt_full", "shift_a", "shift_r", "shift_b", "shift_c", "shift_placed"))
        score_full, exp_done, pv_done = sem("score_full"), sem("exp_done"), sem("pv_done")
        o_copied, denom_done, log_done, guess_done, residue_done, recip_done, o_done = (
            sem(s) for s in ("o_copied", "denom_done", "log_done", "guess_done", "residue_done", "recip_done", "o_done"))
        v_full, v_copied, e_full, x_done = sem("v_full"), sem("v_copied"), sem("e_full"), sem("x_done")
        if masked:
            mask_loaded, mask_a, mask_r, mask_b, mask_c = (sem(s) for s in ("mask_loaded", "mask_a", "mask_r", "mask_b", "mask_c"))
        constants = 8 if masked else 4

        order = ["xt0", "xt1", "q0", "q1", "v", "mt", "e0", "e1"]
        bank = {what: n % 2 for n, what in enumerate(order)}

        def loop(eng, sequence):
            sequence(0, 0)
            with eng.Fori(0, (B - 2) // 2) as i:
                sequence(2 * i + 1, 1)
                sequence(2 * i + 2, 0)

        with nc.Block() as block:
            @block.sync
            def _(sp):
                sp.dma_start(ctx_all[:], ctx_t.rearrange("(k p) n -> p k n", p=P)).then_inc(loaded, 16)
                for dst, src in ((wk, w_k), (wq, w_q), (wv, w_v)):
                    sp.dma_start(dst[:], src.rearrange("(k p) n -> p k n", p=P)).then_inc(loaded, 16)
                sp.dma_start(bias[:, 0:2], bias_k).then_inc(loaded, 16)
                sp.dma_start(bias[:, 2:4], bias_q).then_inc(loaded, 16)
                sp.dma_start(bias_row[:], bias_v).then_inc(loaded, 16)
                sp.dma_start(wo[:], w_o.rearrange("g p n -> p g n")).then_inc(loaded, 16)

                def load(b):
                    hold(sp, v_full, b, sp_passed)
                    src = ctx_twice[b] if isinstance(b, int) else ctx_twice[bass.ds(b, 1)].rearrange("o k p n -> (o k) p n")
                    sp.dma_start(ctx_one[:], src.rearrange("k p n -> p k n")).then_inc(ctx_loaded, 16)
                    if masked:
                        hold(sp, mask_r, b, sp_passed)
                        hold(sp, mask_a, b, sp_passed)
                        src = mask_t[b] if isinstance(b, int) else mask_t[bass.ds(b, 1)].rearrange("o k s -> (o k) s")
                        for half in range(2):
                            sp.dma_start(mask_raw[S2 * half:S2 * half + S2, :], src).then_inc(mask_loaded, 16)

                def store_parts(s):
                    for i in range(2):
                        hold(sp, part2_cut, 2 * s + i + 1, sp_passed)
                        if not isinstance(s, int) or s > 0:
                            sp.wait_ge(k_stacked, 192)
                            hold(sp, stacked, 192 * (s - 1), sp_passed)
                        sp.dma_start(scratch[i], parts[:, i]).then_inc(parts_stored, 16)
                    hold(sp, parts_stored, 32 * s + 32, sp_passed)

                def stack(dst, which, signal):
                    for half in range(2):
                        for r, part in enumerate(which):
                            sp.dma_start(dst[HD * r:HD * r + HD, 8 * half:8 * half + 8, :],
                                         scratch[half, :, part, :].rearrange("(h d) t -> d h t", d=HD)).then_inc(signal, 16)

                def queries(b, slot):
                    store_parts(b + 1)
                    hold(sp, score_full, NP * (b - 1), sp_passed)
                    stack(q_stack[:, slot], Q_PART, stacked)

                def place_shift(b, slot):
                    hold(sp, shift_c, b + 1, sp_passed)
                    for i in range(3):
                        sp.dma_start(q_stack[SHIFT + i:SHIFT + i + 1, slot, :, :], shift1[:, i, :]).then_inc(shift_placed, 16)

                load(0)
                store_parts(0)
                stack(k_stack, K_PART, k_stacked)
                queries(0, 0)
                place_shift(0, 0)

                def sequence(b, slot):
                    load(b + 1)
                    queries(b + 1, 1 - slot)
                    place_shift(b + 1, 1 - slot)

                loop(sp, sequence)

            @block.gpsimd
            def _(pool):
                n = 0

                def constant(instruction):
                    nonlocal n
                    n += 1
                    instruction.then_inc(ready, 1)
                    pool.wait_ge(ready, n)

                constant(pool.memset(values[:], 0.0))
                constant(pool.memset(values[0:S2, :, HD:2 * HD], 1.0))
                constant(pool.memset(values[S2:P, :, 3 * HD:4 * HD], 1.0))
                constant(pool.memset(k_stack[SHIFT:KROWS], 1.0))
                if masked:
                    constant(pool.memset(mask3[:], 0.0))
                    constant(pool.memset(spread_keys[:], 0.0))
                    view = spread_keys[:].rearrange("p (h k) -> p h k", k=S2)
                    for base in (0, -S2):
                        constant(pool.affine_select(out=view, in_=view, compare_op=ALU.not_equal, fill=1.0, base=base,
                                                    pattern=[[0, S // S2], [-1, S2]], channel_multiplier=1))
                pool.wait_ge(loaded, 16 * 8)
                pool.tensor_scalar(wq[:], wq[:], HD ** -0.5, None, ALU.mult).then_inc(scaled, 1)
                pool.tensor_scalar(bias[:, 2:4], bias[:, 2:4], HD ** -0.5, None, ALU.mult).then_inc(scaled, 1)

                def layer_norm(b):
                    hold(pool, ln_aggr, 4 * b + 4, pool_passed)
                    pool.tensor_scalar(var_eps[:], mean_var[:, :, 1], 1e-5, None, ALU.add).then_inc(ln_eps, 1)
                    pool.wait_ge(ln_eps, b + 1)
                    pool.tensor_tensor(rstd[:], var_eps[:], c.minus_half[:, 0:TT], ALU.pow).then_inc(ln_rstd, 1)

                def cut(s):
                    for i in range(2):
                        pool.wait_ge(part1_cut, 2 * s + i + 1)
                        pool.tensor_tensor(parts[:, i, 2], rest[:, i], parts[:, i, 1], ALU.subtract).then_inc(part2_cut, 1)

                def shift(b):
                    hold(pool, shift_r, b + 1, pool_passed)
                    hold(pool, shift_placed, 48 * b, pool_passed)
                    pool.tensor_copy(shift1[:, 1], shift_rest[:]).then_inc(shift_b, 1)
                    pool.wait_ge(shift_b, b + 1)
                    pool.tensor_tensor(shift1[:, 2], shift_rest[:], shift1[:, 1], ALU.subtract).then_inc(shift_c, 1)

                def normalise(b, g):
                    pool.wait_ge(recip_done, 4 * b + g + 1)
                    wait(pool, e_full, 2 * b)
                    pool.tensor_tensor(o_norm[:, g], o_raw[:, g], r_denom[:, g], ALU.mult).then_inc(o_done, 1)

                def cut_mask(b, slot):
                    pool.wait_ge(mask_a, b + 1)
                    pool.tensor_tensor(mask_rest[:], mask_raw[:], mask12[:, slot], ALU.subtract).then_inc(mask_r, 1)
                    pool.wait_ge(mask_b, b + 1)
                    pool.tensor_tensor(mask3[S2:P, slot], mask_rest[S2:P], mask12[S2:P, slot], ALU.subtract).then_inc(mask_c, 1)
                    hold(pool, mask_c, b + 1, pool_passed)

                layer_norm(0)
                cut(0)
                cut(1)
                if masked:
                    cut_mask(0, 0)
                shift(0)

                def sequence(b, slot):
                    layer_norm(b + 1)
                    cut(b + 2)
                    if masked:
                        cut_mask(b + 1, 1 - slot)
                    for g in range(NG):
                        normalise(b, g)
                    shift(b + 1)

                loop(pool, sequence)
                for g in range(NG):
                    normalise(B - 1, g)

            @block.scalar
            def _(act):
                act.preload_act_table_set("natural_log_exp_and_others")

                def cut(s, column):
                    for i in range(2):
                        act.wait_ge(qk_full, 2 * s + i + 1)
                        wait(act, parts_stored, 32 * s)
                        act.activation(parts[:, i, 0], general[:, bank[f"q{i}"]], ACT.Identity, bias=bias[:, column + i:column + i + 1]).then_inc(part0_cut, 1)
                    for i in range(2):
                        act.wait_ge(rest_done, 2 * s + i + 1)
                        act.activation(parts[:, i, 1], rest[:, i], ACT.Copy).then_inc(part1_cut, 1)

                def transposed(b):
                    for k in range(KD):
                        act.wait_ge(xt_full, 2 * b + k + 1)
                        act.activation(xnT[:, k], general[:, bank[f"xt{k}"]], ACT.Copy).then_inc(xt_copied, 1)

                def cut_mask(b, slot):
                    act.wait_ge(mask_loaded, 32 * b + 32)
                    wait(act, score_full, NP * (b - 1))
                    act.activation(mask12[:, slot], mask_raw[:], ACT.Copy).then_inc(mask_a, 1)
                    act.wait_ge(mask_r, b + 1)
                    act.activation(mask12[S2:P, slot], mask_rest[S2:P], ACT.Copy).then_inc(mask_b, 1)

                def shift(b):
                    act.wait_ge(mt_full, b + 1)
                    wait(act, shift_placed, 48 * b)
                    act.activation(shift1[:, 0], general[0:H, bank["mt"]], ACT.Copy).then_inc(shift_a, 1)

                def exponentials(b, pairs):
                    for p in pairs:
                        act.wait_ge(score_full, NP * b + p + 1)
                        wait(act, pv_done, NP * b + p - 3)
                        act.activation(probs[:, p % 4], score_ps[:, p % 2], ACT.Exp).then_inc(exp_done, 1)

                def copy_out(b, g):
                    act.wait_ge(pv_done, NP * b + 2 * g + 2)
                    wait(act, o_done, 4 * b + g - 3)
                    act.activation(o_raw[:, g], out_ps[:, g % 2], ACT.Copy).then_inc(o_copied, 1)

                def invert(b, g):
                    n = 4 * b + g
                    act.wait_ge(denom_done, n + 1)
                    wait(act, guess_done, n)
                    act.activation(log_sum[:], denom[:, g], ACT.Ln).then_inc(log_done, 1)
                    act.wait_ge(log_done, n + 1)
                    act.activation(r_denom[:, g], log_sum[:], ACT.Exp, scale=-1.0).then_inc(guess_done, 1)

                act.wait_ge(loaded, 16 * 8)
                act.wait_ge(scaled, 2)
                cut(0, 0)
                transposed(0)
                cut(1, 2)
                if masked:
                    cut_mask(0, 0)
                shift(0)

                def attend(b):
                    exponentials(b, range(4))
                    copy_out(b, 0)
                    exponentials(b, (4, 5))
                    copy_out(b, 1)
                    invert(b, 0)
                    exponentials(b, (6, 7))
                    copy_out(b, 2)
                    invert(b, 1)
                    copy_out(b, 3)
                    invert(b, 2)
                    invert(b, 3)

                def sequence(b, slot):
                    transposed(b + 1)
                    cut(b + 2, 2)
                    if masked:
                        cut_mask(b + 1, 1 - slot)
                    attend(b)
                    shift(b + 1)

                loop(act, sequence)
                attend(B - 1)

            @block.vector
            def _(dve):
                def xtile(b, t):
                    return c.x[:, b, t] if isinstance(b, int) else c.x[:, bass.ds(b, 1), t, :]

                def layer_norm(b):
                    wait(dve, ln_aggr, 4 * b)
                    for t in range(TT):
                        dve.bn_stats(stats[:, t], xtile(b, t)).then_inc(ln_stats, 1)
                    for t in range(TT):
                        hold(dve, ln_stats, 4 * b + t + 1, dve_passed)
                        if t == 0:
                            hold(dve, ln_eps, b, dve_passed)
                            hold(dve, ln_done, 4 * b, dve_passed)
                        dve.bn_aggr(mean_var[:, t], stats[:, t]).then_inc(ln_aggr, 1)
                    dve.wait_ge(ln_aggr, 4 * b + 4)
                    wait(dve, xt_full, 2 * b)
                    dve.wait_ge(ln_rstd, b + 1)
                    for t in range(TT):
                        dve.tensor_scalar(xn[:, t], xtile(b, t), mean_var[:, t, 0:1], rstd[:, t:t + 1],
                                          ALU.subtract, ALU.mult).then_inc(ln_done, 1)

                def leftover(s, column):
                    for i in range(2):
                        dve.wait_ge(part0_cut, 2 * s + i + 1)
                        wait(dve, part2_cut, 2 * s + i - 1)
                        dve.scalar_tensor_tensor(rest[:, i], general[:, bank[f"q{i}"]], bias[:, column + i:column + i + 1],
                                                 parts[:, i, 0], ALU.add, ALU.subtract).then_inc(rest_done, 1)

                def keys(b):
                    wait(dve, score_full, NP * b)
                    src = k_stack[0:KROWS, :, S2 * b:S2 * b + S2] if isinstance(b, int) else k_stack[0:KROWS, :, bass.ds(S2 * b, S2)]
                    dve.tensor_copy(k_one[0:KROWS], src).then_inc(k_copied, 1)

                def valued(b):
                    dve.wait_ge(v_full, b + 1)
                    for half in range(2):
                        rows = slice(S2 * half, S2 * half + S2)
                        heads = lambda a: a.rearrange("p (h two d) -> p h two d", two=2, d=HD)[:, :, half, :]
                        dve.tensor_tensor(values[rows, :, 2 * HD * half:2 * HD * half + HD], heads(general[rows, bank["v"], 0:D]),
                                          heads(bias_row[rows]), ALU.add).then_inc(v_copied, 1)

                def maxima(b):
                    wait(dve, mt_full, b)
                    for n in range(8):
                        t, half = n // 2, n % 2
                        dve.wait_ge(max_full, 8 * b + n + 1)
                        dve.tensor_reduce(neg_max[:, t, 8 * half:8 * half + 8], max_ps[:, half].rearrange("p (h k) -> p h k", k=S2),
                                          AX, ALU.max, negate=True).then_inc(max_read, 1)

                def shift(b):
                    dve.wait_ge(shift_a, b + 1)
                    wait(dve, shift_c, b)
                    dve.tensor_tensor(shift_rest[:], general[0:H, bank["mt"]], shift1[:, 0], ALU.subtract).then_inc(shift_r, 1)

                def spread(b, g):
                    hold(dve, o_copied, 4 * b + g + 1, dve_passed)
                    dve.stream_shuffle(denom[:, g], o_raw[:, g], mask=[HD + d % HD for d in range(32)]).then_inc(denom_done, 1)

                def refine(b, g):
                    n = 4 * b + g
                    dve.wait_ge(guess_done, n + 1)
                    wait(dve, recip_done, n)
                    dve.scalar_tensor_tensor(residue[:], denom[:, g], -1.0, r_denom[:, g], ALU.mult, ALU.mult).then_inc(residue_done, 1)
                    dve.wait_ge(residue_done, n + 1)
                    dve.scalar_tensor_tensor(r_denom[:, g], residue[:], 2.0, r_denom[:, g], ALU.add, ALU.mult).then_inc(recip_done, 1)

                def add(b):
                    for t in range(2):
                        dve.wait_ge(e_full, 2 * b + t + 1)
                        dst = c.x[:, b, 2 * t:2 * t + 2] if isinstance(b, int) else c.x[:, bass.ds(b, 1), 2 * t:2 * t + 2, :]
                        dve.tensor_tensor(dst, general[:, bank[f"e{t}"]].rearrange("p (t d) -> p t d", t=2), dst, ALU.add).then_inc(x_done, 1)

                def attended(b):
                    spread(b, 0)
                    spread(b, 1)
                    refine(b, 0)
                    spread(b, 2)
                    refine(b, 1)
                    spread(b, 3)

                dve.wait_ge(ready, constants)
                dve.wait_ge(loaded, 16 * 8)
                dve.wait_ge(scaled, 2)
                layer_norm(0)
                leftover(0, 0)
                leftover(1, 2)
                dve.wait_ge(k_stacked, 192)
                valued(0)
                keys(0)
                maxima(0)
                shift(0)

                def sequence(b, slot):
                    layer_norm(b + 1)
                    leftover(b + 2, 2)
                    attended(b)
                    keys(b + 1)
                    valued(b + 1)
                    refine(b, 2)
                    refine(b, 3)
                    maxima(b + 1)
                    shift(b + 1)
                    add(b)

                loop(dve, sequence)
                attended(B - 1)
                refine(B - 1, 2)
                refine(B - 1, 3)
                add(B - 1)
                dve.wait_ge(x_done, 2 * B)

            @block.tensor
            def _(pe):
                def project(item, weights, source, free, *value):
                    i = item
                    wait(pe, free, *value)
                    for k in range(KD):
                        last = pe.matmul(general[:, bank[f"q{i}"]], weights[:, k, P * i:P * i + P], source[:, k],
                                         start=(k == 0), stop=(k == KD - 1))
                    last.then_inc(qk_full, 1)

                def queries(b, last_x):
                    for k in range(KD):
                        pe.wait_ge(ln_done, 4 * b + 4)
                        wait(pe, *last_x[k])
                        for t in range(TT):
                            last = pe.transpose(general[:, bank[f"xt{k}"], P * t:P * t + P], xn[:, t, P * k:P * k + P], c.ident[:])
                        last.then_inc(xt_full, 1)
                    for i in range(2):
                        project(i, wq, xnT, xt_copied, 2 * b + 2)

                def value_rows(b):
                    pe.wait_ge(ctx_loaded, 16 * b + 16)
                    pe.wait_ge(rest_done, 2 * b + 3)
                    for k in range(KD):
                        last = pe.matmul(general[:, bank["v"], 0:D], ctx_one[:, k], wv[:, k], start=(k == 0), stop=(k == KD - 1))
                    last.then_inc(v_full, 1)

                def maxima(b, slot):
                    pe.wait_ge(stacked, 192 * b + 192)
                    pe.wait_ge(k_copied, b + 1)
                    if masked:
                        pe.wait_ge(mask_c, b + 1)
                    for n in range(8):
                        t, half = n // 2, n % 2
                        tok = slice(P * t, P * t + P)
                        wait(pe, max_read, 8 * b + n - 1)
                        for h in range(8):
                            last = pe.matmul(max_ps[:, half, S2 * h:S2 * h + S2], q_stack[0:ROWS, slot, 8 * half + h, tok],
                                             k_one[0:ROWS, 8 * half + h], start=(h == 0 or not masked), stop=not masked, skip_group_check=masked)
                        if masked:
                            pe.matmul(max_ps[:, half], mask12[:, slot, tok], spread_keys[:], start=False, stop=False, skip_group_check=True)
                            last = pe.matmul(max_ps[:, half], mask3[:, slot, tok], spread_keys[:], start=False, stop=True, skip_group_check=True)
                        last.then_inc(max_full, 1)
                    pe.wait_ge(rest_done, 2 * b + 4)
                    pe.wait_ge(max_read, 8 * b + 8)
                    for t in range(TT):
                        last = pe.transpose(general[0:H, bank["mt"], P * t:P * t + P], neg_max[:, t], c.ident[:])
                    last.then_inc(mt_full, 1)

                def scores(b, slot, p):
                    wait(pe, exp_done, NP * b + p - 1)
                    for half in range(2):
                        rows = slice(S2 * half, S2 * half + S2)
                        last = pe.matmul(score_ps[rows, p % 2], k_one[0:KROWS, 2 * p + half], q_stack[0:KROWS, slot, 2 * p + half],
                                         start=True, stop=not masked, tile_position=(0, S2 * half), skip_group_check=masked)
                    if masked:
                        pe.matmul(score_ps[:, p % 2], spread_keys[:, 0:P], mask12[:, slot], start=False, stop=False, skip_group_check=True)
                        last = pe.matmul(score_ps[:, p % 2], spread_keys[:, 0:P], mask3[:, slot], start=False, stop=True, skip_group_check=True)
                    last.then_inc(score_full, 1)

                def with_values(b, p):
                    pe.wait_ge(exp_done, NP * b + p + 1)
                    g, half = p // 2, p % 2
                    if half == 0:
                        wait(pe, o_copied, 4 * b + g - 1)
                    if p == 0:
                        pe.wait_ge(v_copied, 2 * b + 2)
                    pe.matmul(out_ps[64 * half:64 * half + 64, g % 2], values[:, p], probs[:, p % 4],
                              start=True, stop=True, tile_position=(0, 64 * half)).then_inc(pv_done, 1)

                def attend(b, slot):
                    pe.wait_ge(shift_placed, 48 * b + 48)
                    for p in range(NP + 2):
                        if p < NP:
                            scores(b, slot, p)
                        if p >= 2:
                            with_values(b, p - 2)

                def output(b, last_of_bank):
                    pe.wait_ge(o_done, 4 * b + 4)
                    for t in range(2):
                        wait(pe, *last_of_bank[t])
                        for t2 in range(2):
                            tok = P * (2 * t + t2)
                            for g in range(NG):
                                last = pe.matmul(general[:, bank[f"e{t}"], D * t2:D * t2 + D], o_norm[:, g, tok:tok + P], wo[:, g],
                                                 start=(g == 0), stop=(g == NG - 1))
                        last.then_inc(e_full, 1)

                pe.wait_ge(loaded, 16 * 8)
                pe.wait_ge(ready, constants)
                pe.wait_ge(scaled, 2)
                for i in range(2):
                    project(i, wk, ctx_all, loaded, 16)
                queries(0, ((rest_done, 1), (rest_done, 2)))
                value_rows(0)
                maxima(0, 0)

                def sequence(b, slot):
                    if isinstance(b, int) and b == 0:
                        queries(1, ((v_copied, 2), (shift_r, 1)))
                    else:
                        queries(b + 1, ((x_done, 2 * b - 1), (x_done, 2 * b)))
                    attend(b, slot)
                    value_rows(b + 1)
                    maxima(b + 1, 1 - slot)
                    output(b, ((v_copied, 2 * b + 4), (shift_r, b + 2)))

                loop(pe, sequence)
                attend(B - 1, 1)
                output(B - 1, ((x_done, 2 * B - 3), (x_done, 2 * B - 2)))

    nc.clear_and_free_semaphores(made)
    nc.all_engine_barrier()


def mixture_of_depths(nc, c, w_router, w_qkv, w_o, gain1, gain2, w_1, w_2, w_3):
    made = []
    R = P
    SB = 2
    BS = B // SB
    F = w_1.shape[1]
    FT = -(-F // P)
    rows_of = lambda f: min(P, F - P * f)
    UNITS = BS * NG

    def sem(what):
        s = nc.alloc_semaphore(f"depths_{what}")
        made.append(s)
        return s

    with ExitStack() as ctx:
        def allocate(to):
            return (lambda what, shape, dt=F32: to.enter_context(nc.sbuf_tensor(f"depths_{what}", shape, dt)),
                    lambda what, shape, dt=F32: to.enter_context(nc.psum_tensor(f"depths_{what}", shape, dt)))

        sb, ps = allocate(ctx)
        wqkv = sb("wqkv", [P, KD, 3 * D])
        wo = sb("wo", [P, NG, D])
        gains = sb("gains", [P, 2, KD])
        w1, w2 = sb("w1", [P, KD, F]), sb("w2", [P, KD, F])
        w3 = sb("w3", [P, FT, D])
        back = sb("back", [P, B, S])
        chosen = sb("chosen", [P, B, D])
        delta = sb("delta", [P, B, D])
        mean_sq = sb("mean_sq", [P, 2, B])
        r_rms = sb("r_rms", [P, 2, B])

        loaded, scaled = sem("loaded"), sem("scaled")
        sq_done = sem("sq_done")

        with ExitStack() as inner:
            sb1, ps1 = allocate(inner)
            router = sb1("router", [P, D])
            column = sb1("column", [P, P])
            before = sb1("before", [P, P])
            stats = sb1("stats", [P, TT, 6])
            mean_var = sb1("mean_var", [P, TT, 2])
            var_eps = sb1("var_eps", [P, TT])
            rstd = sb1("rstd", [P, TT])
            h = sb1("h", [P, 2, TT, D])
            product = sb1("product", [P, TT, D])
            score = sb1("score", [P, 2, TT])
            above = sb1("above", [P, TT, S], BF16)
            tied = sb1("tied", [P, TT, P], BF16)
            counts = sb1("counts", [P, TT, 3])
            rank = sb1("rank", [P, TT])
            pick = sb1("pick", [P, 2, TT, R])
            squares = sb1("squares", [P, D])
            score_rows = ps1("score_rows", [P, 2, S])
            back_ps = ps1("back_ps", [P, 2, S])
            chosen_ps = ps1("chosen_ps", [P, 2, S])

            ready, router_loaded = sem("ready"), sem("router_loaded")
            pool_passed, dve_passed = sem("pool_passed"), sem("dve_passed")
            ln_stats, ln_aggr, ln_eps, ln_rstd, ln_done = (sem(s) for s in ("ln_stats", "ln_aggr", "ln_eps", "ln_rstd", "ln_done"))
            scored, rows_full, counted, ranked, picked = (sem(s) for s in ("scored", "rows_full", "counted", "ranked", "picked"))
            h_added, back_full, back_copied, chosen_full, chosen_copied = (
                sem(s) for s in ("h_added", "back_full", "back_copied", "chosen_full", "chosen_copied"))
            COUNTS = 3 * TT - 1

            def pairs(eng, one):
                one(0, 0)
                one(1, 1)
                with eng.Fori(1, B // 2) as i:
                    one(2 * i, 0)
                    one(2 * i + 1, 1)

            def at(tensor, b):
                return tensor[:, b] if isinstance(b, int) else tensor[:, bass.ds(b, 1)].rearrange(
                    "p o t d -> p (o t) d" if len(tensor.shape) == 4 else "p o n -> p (o n)")

            def xtile(b, t):
                return c.x[:, b, t] if isinstance(b, int) else c.x[:, bass.ds(b, 1), t, :]

            with nc.Block() as block:
                @block.sync
                def _(sp):
                    sp.dma_start(router[:], w_router).then_inc(router_loaded, 16)
                    sp.dma_start(wqkv[:], w_qkv.rearrange("(k p) n -> p k n", p=P)).then_inc(loaded, 16)
                    sp.dma_start(wo[:], w_o.rearrange("g p n -> p g n")).then_inc(loaded, 16)
                    for i, gain in enumerate((gain1, gain2)):
                        sp.dma_start(gains[:, i], gain).then_inc(loaded, 16)
                    sp.dma_start(w1[:], w_1.rearrange("(k p) n -> p k n", p=P)).then_inc(loaded, 16)
                    sp.dma_start(w2[:], w_2.rearrange("(k p) n -> p k n", p=P)).then_inc(loaded, 16)
                    for f in range(FT):
                        sp.dma_start(w3[0:rows_of(f), f], w_3[P * f:P * f + rows_of(f)]).then_inc(loaded, 16)

                @block.gpsimd
                def _(pool):
                    pool.iota(column[:], pattern=[[1, P]], base=0, channel_multiplier=0, allow_small_or_imprecise_dtypes=True).then_inc(ready, 1)
                    pool.memset(before[:], 1.0).then_inc(ready, 1)
                    pool.memset(counts[:], 0.0).then_inc(ready, 1)
                    pool.wait_ge(ready, 3)
                    pool.affine_select(out=before[:], in_=before[:], compare_op=ALU.is_gt, fill=0.0, base=0,
                                       pattern=[[-1, P]], channel_multiplier=1).then_inc(ready, 1)

                    def layer_norm(b):
                        hold(pool, ln_aggr, TT * b + TT, pool_passed)
                        pool.tensor_scalar(var_eps[:], mean_var[:, :, 1], 1e-5, None, ALU.add).then_inc(ln_eps, 1)
                        pool.wait_ge(ln_eps, b + 1)
                        pool.tensor_tensor(rstd[:], var_eps[:], c.minus_half[:, 0:TT], ALU.pow).then_inc(ln_rstd, 1)

                    def add(b, slot):
                        layer_norm(b)
                        hold(pool, ln_done, TT * b + TT, pool_passed)
                        pool.tensor_tensor(at(c.x, b), at(c.x, b), h[:, slot], ALU.add).then_inc(h_added, 1)

                    pairs(pool, add)

                    pool.wait_ge(loaded, 16 * (6 + FT))
                    pool.tensor_scalar(wqkv[:, :, 0:D], wqkv[:, :, 0:D], HD ** -0.5, None, ALU.mult).then_inc(scaled, 1)

                @block.scalar
                def _(act):
                    act.preload_act_table_set("natural_log_exp_and_others")

                    def keep(b, slot):
                        act.wait_ge(back_full, b + 1)
                        act.activation(at(back, b), back_ps[:, slot], ACT.Copy).then_inc(back_copied, 1)
                        act.wait_ge(chosen_full, b + 1)
                        act.activation(at(chosen, b), chosen_ps[:, slot, 0:D], ACT.Copy).then_inc(chosen_copied, 1)
                        wait(act, sq_done, b)
                        total = mean_sq[:, 0, b:b + 1] if isinstance(b, int) else mean_sq[:, 0, bass.ds(b, 1)]
                        act.activation(squares[:], chosen_ps[:, slot, 0:D], ACT.Square, accum_out=total).then_inc(sq_done, 1)

                    pairs(act, keep)

                @block.vector
                def _(dve):
                    def normalise(b, slot):
                        wait(dve, ln_aggr, TT * b)
                        for t in range(TT):
                            dve.bn_stats(stats[:, t], xtile(b, t)).then_inc(ln_stats, 1)
                        for t in range(TT):
                            hold(dve, ln_stats, TT * b + t + 1, dve_passed)
                            if t == 0:
                                hold(dve, ln_eps, b, dve_passed)
                                hold(dve, ln_done, TT * b, dve_passed)
                            dve.bn_aggr(mean_var[:, t], stats[:, t]).then_inc(ln_aggr, 1)
                        dve.wait_ge(ln_aggr, TT * b + TT)
                        wait(dve, chosen_full, b - 1)
                        wait(dve, h_added, b - 1)
                        dve.wait_ge(ln_rstd, b + 1)
                        for t in range(TT):
                            dve.tensor_scalar(h[:, slot, t], xtile(b, t), mean_var[:, t, 0:1], rstd[:, t:t + 1],
                                              ALU.subtract, ALU.mult).then_inc(ln_done, 1)
                        wait(dve, rows_full, b - 1)
                        wait(dve, counted, COUNTS * (b - 1))
                        wait(dve, scored, TT * b)
                        for t in range(TT):
                            dve.wait_ge(ln_done, TT * b + t + 1)
                            dve.scalar_tensor_tensor(product[:, t], h[:, slot, t], 1.0, router[:], ALU.mult, ALU.mult,
                                                     accum_out=score[:, slot, t:t + 1]).then_inc(scored, 1)

                    def choose(b, slot):
                        dve.wait_ge(rows_full, b + 1)
                        wait(dve, counted, COUNTS * b)
                        wait(dve, ranked, b)
                        for t in range(TT):
                            own = score[:, slot, t:t + 1]
                            if t > 0:
                                dve.tensor_scalar(above[:, t, 0:P * t], score_rows[:, slot, 0:P * t], own, 0.0, ALU.is_ge, ALU.add,
                                                  accum_out=counts[:, t, 0:1]).then_inc(counted, 1)
                            dve.tensor_scalar(above[:, t, P * t:S], score_rows[:, slot, P * t:S], own, 0.0, ALU.is_gt, ALU.add,
                                              accum_out=counts[:, t, 1:2]).then_inc(counted, 1)
                            dve.scalar_tensor_tensor(tied[:, t], score_rows[:, slot, P * t:P * t + P], own, before[:], ALU.is_equal, ALU.mult,
                                                     accum_out=counts[:, t, 2:3]).then_inc(counted, 1)
                        dve.wait_ge(counted, COUNTS * b + COUNTS)
                        hold(dve, picked, TT * b, dve_passed)
                        dve.tensor_reduce(rank[:], counts[:], AX, ALU.add).then_inc(ranked, 1)
                        dve.wait_ge(ranked, b + 1)
                        wait(dve, chosen_full, b - 1)
                        for t in range(TT):
                            dve.tensor_scalar(pick[:, slot, t], column[:], rank[:, t:t + 1], None, ALU.is_equal).then_inc(picked, 1)

                    dve.wait_ge(ready, 4)
                    dve.wait_ge(router_loaded, 16)
                    normalise(0, 0)

                    def both(b, slot):
                        normalise(b + 1, 1 - slot)
                        choose(b, slot)

                    both(0, 0)
                    both(1, 1)
                    both(2, 0)
                    with dve.Fori(1, B // 2 - 1) as i:
                        both(2 * i + 1, 1)
                        both(2 * i + 2, 0)
                    choose(B - 1, 1)

                @block.tensor
                def _(pe):
                    def gather(b, slot):
                        pe.wait_ge(scored, TT * b + TT)
                        wait(pe, counted, COUNTS * (b - 1))
                        for t in range(TT):
                            last = pe.transpose(score_rows[:, slot, P * t:P * t + P], score[:, slot, t:t + 1].to_broadcast([P, P]), c.ident[:])
                        last.then_inc(rows_full, 1)
                        pe.wait_ge(picked, TT * b + TT)
                        wait(pe, back_copied, b - 1)
                        for t in range(TT):
                            last = pe.transpose(back_ps[:, slot, P * t:P * t + P], pick[:, slot, t], c.ident[:])
                        last.then_inc(back_full, 1)
                        wait(pe, sq_done, b - 1)
                        for t in range(TT):
                            last = pe.matmul(chosen_ps[:, slot, 0:D], pick[:, slot, t], h[:, slot, t], start=(t == 0), stop=(t == TT - 1))
                        last.then_inc(chosen_full, 1)

                    pairs(pe, gather)

        xT = sb("xT", [P, KD, S])
        rows = sb("rows", [P, BS, D])
        parts = sb("parts", [P, 4, 3, S], BF16)
        rest = sb("rest", [P, 2, S])
        q_stack, k_stack = sb("q_stack", [P, H, S], BF16), sb("k_stack", [P, H, S], BF16)
        values = sb("values", [P, BS, H, 32])
        causal4 = sb("causal4", [P, GH, P], BF16)
        neg_max, sums, r_sums = (sb(what, [P, 4, GH]) for what in ("neg_max", "sums", "r_sums"))
        probs = sb("probs", [P, 3, GH, P])
        probsT = sb("probsT", [P, 2, S])
        attended = sb("attended", [P, 2, S])
        squares2 = sb("squares2", [P, D])
        silu = sb("silu", [P, 2, S])
        gated = sb("gated", [P, FT, S])
        scratch = nc.dram_tensor("depths_parts_dram", [4, P, 3, S], BF16).ap()
        general = ps("general", [P, 2, S])
        score_ps = ps("score_ps", [P, 2, S])
        turned_ps = ps("turned_ps", [P, 2, S])
        out_ps = ps("out_ps", [P, 2, S])

        constants, rms_done, rows_done, t_full, qk_full, v_full, v_copied = (
            sem(s) for s in ("constants", "rms_done", "rows_done", "t_full", "qk_full", "v_full", "v_copied"))
        ms_eps = sem("ms_eps")
        general_read = [sem(f"general_read{i}") for i in range(2)]
        part0_cut, rest_done, part1_cut, part2_cut, parts_stored, stacked = (
            sem(s) for s in ("part0_cut", "rest_done", "part1_cut", "part2_cut", "parts_stored", "stacked"))
        score_full, max_done, exp_done, sums_inverted, probs_scaled, turned, turned_copied = (
            sem(s) for s in ("score_full", "max_done", "exp_done", "sums_inverted", "probs_scaled", "turned", "turned_copied"))
        pv_done, attended_copied, attn_full, attn_kept, attn_added = (
            sem(s) for s in ("pv_done", "attended_copied", "attn_full", "attn_kept", "attn_added"))
        hidden_full, silu_done, gated_done, ff_full, ff_added, back_out = (
            sem(s) for s in ("hidden_full", "silu_done", "gated_done", "ff_full", "ff_added", "back_out"))

        uses = []
        for s in range(SB):
            uses += [("xT", s, k) for k in range(KD)] + [("qk", s, i) for i in range(4)] + [("v", s, i) for i in range(2)]
            if s == 0:
                uses += [("attn", 0, i) for i in range(BS)]
            else:
                uses += [("xT", SB, k) for k in range(KD)] + [("back", 0, i) for i in range(2 * BS)]
                uses += [("attn", 1, i) for i in range(BS)]
                uses += [("xT", SB + 1, k) for k in range(KD)] + [("back", 1, i) for i in range(2 * BS)]
        place = {use: (n % 2, n // 2) for n, use in enumerate(uses)}

        def bank(*use):
            return place[use][0]

        def nth(*use):
            return place[use][1]

        with nc.Block() as block:
            @block.sync
            def _(sp):
                for s in range(SB):
                    for i in range(4):
                        sp.wait_ge(part2_cut, 4 * s + i + 1)
                        wait(sp, stacked, 384 * s)
                        sp.dma_start(scratch[i], parts[:, i]).then_inc(parts_stored, 16)
                    wait(sp, score_full, UNITS * s)
                    sp.wait_ge(parts_stored, 64 * s + 64)
                    for half in range(2):
                        for stk, item, which in ((q_stack, 2 * half, Q_PART), (k_stack, 2 * half + 1, K_PART)):
                            for r, part in enumerate(which):
                                sp.dma_start(stk[HD * r:HD * r + HD, 8 * half:8 * half + 8, :],
                                             scratch[item, :, part, :].rearrange("(h d) t -> d h t", d=HD)).then_inc(stacked, 16)

            @block.gpsimd
            def _(pool):
                def r_rms_of(which, first, count, step):
                    cut = slice(first, first + count)
                    pool.tensor_scalar(mean_sq[:, which, cut], mean_sq[:, which, cut], 1.0 / D, 1e-6, ALU.mult, ALU.add).then_inc(ms_eps, 1)
                    pool.wait_ge(ms_eps, step)
                    pool.tensor_tensor(r_rms[:, which, cut], mean_sq[:, which, cut], c.minus_half[:, 0:count], ALU.pow).then_inc(rms_done, 1)

                r_rms_of(0, 0, B, 1)
                pool.memset(values[:, :, :, HD:], 0.0).then_inc(constants, 1)
                for g in range(GH):
                    pool.tensor_copy(causal4[:, g], c.causal_qk[:]).then_inc(constants, 1)

                def cuts(s):
                    for i in range(4):
                        pool.wait_ge(part1_cut, 4 * s + i + 1)
                        pool.tensor_tensor(parts[:, i, 2], rest[:, i % 2], parts[:, i, 1], ALU.subtract).then_inc(part2_cut, 1)

                def attend(s):
                    for n in range(UNITS * s, UNITS * s + UNITS):
                        pool.wait_ge(sums_inverted, n + 1)
                        pool.tensor_tensor(probs[:, n % 3], probs[:, n % 3], r_sums[:, n % 4].unsqueeze(2).to_broadcast([P, GH, P]),
                                           ALU.mult).then_inc(probs_scaled, 1)

                cuts(0)
                attend(0)
                cuts(1)
                pool.wait_ge(sq_done, B + BS)
                r_rms_of(1, 0, BS, 2)
                attend(1)
                pool.wait_ge(sq_done, B + 2 * BS)
                r_rms_of(1, BS, BS, 3)

            @block.scalar
            def _(act):
                def features(j, gain, free, value):
                    wait(act, free, value)
                    for k in range(KD):
                        act.wait_ge(t_full, 2 * j + k + 1)
                        act.activation(xT[:, k], general[:, bank("xT", j, k)], ACT.Copy, scale=gains[:, gain, k:k + 1]
                                       ).then_inc(general_read[bank("xT", j, k)], 1)

                def cuts(s):
                    for i in range(4):
                        act.wait_ge(qk_full, 4 * s + i + 1)
                        wait(act, parts_stored, 64 * s)
                        act.activation(parts[:, i, 0], general[:, bank("qk", s, i)], ACT.Copy).then_inc(part0_cut, 1)
                        act.wait_ge(rest_done, 4 * s + i + 1)
                        act.activation(parts[:, i, 1], rest[:, i % 2], ACT.Copy).then_inc(part1_cut, 1)

                def copy_out(q):
                    act.wait_ge(pv_done, NG * q + NG)
                    wait(act, attn_full, q - 1)
                    act.activation(attended[:, q % 2], out_ps[:, q % 2], ACT.Copy).then_inc(attended_copied, 1)

                def attend(s):
                    for i in range(UNITS + 5):
                        n = UNITS * s + i
                        if i < UNITS:
                            act.wait_ge(max_done, n + 1)
                            wait(act, turned, n - 2)
                            for g in range(GH):
                                act.activation(probs[:, n % 3, g], score_ps[:, n % 2, P * g:P * g + P], ACT.Exp, bias=neg_max[:, n % 4, g:g + 1],
                                               accum_out=sums[:, n % 4, g:g + 1]).then_inc(exp_done, 1)
                        if i >= NG and i % NG == 0 and i // NG <= BS:
                            copy_out(BS * s + i // NG - 1)

                def squares_of(s):
                    for q in range(BS * s, BS * s + BS):
                        act.wait_ge(attn_added, q + 1)
                        act.wait_ge(sq_done, B + q)
                        act.activation(squares2[:], chosen[:, q], ACT.Square, accum_out=mean_sq[:, 1, q:q + 1]).then_inc(sq_done, 1)

                def feed_forward(s):
                    for f in range(FT):
                        n = FT * s + f
                        act.wait_ge(hidden_full, n + 1)
                        wait(act, gated_done, n - 1)
                        r = rows_of(f)
                        act.activation(silu[0:r, f % 2], score_ps[0:r, f % 2], ACT.Silu).then_inc(silu_done, 1)

                features(0, 0, None, 0)
                cuts(0)
                attend(0)
                features(1, 0, v_full, 2)
                cuts(1)
                squares_of(0)
                features(2, 1, v_full, 4)
                feed_forward(0)
                attend(1)
                squares_of(1)
                features(3, 1, hidden_full, FT)
                feed_forward(1)

            @block.vector
            def _(dve):
                def normed(j, which, s):
                    dve.wait_ge(rms_done, (1, 1, 2, 3)[j])
                    wait(dve, t_full, 2 * j)
                    for i in range(BS):
                        q = BS * s + i
                        dve.tensor_scalar(rows[:, i], chosen[:, q], r_rms[:, which, q:q + 1], None, ALU.mult).then_inc(rows_done, 1)

                def leftover(s):
                    for i in range(4):
                        dve.wait_ge(part0_cut, 4 * s + i + 1)
                        wait(dve, part2_cut, 4 * s + i - 1)
                        b = bank("qk", s, i)
                        dve.tensor_tensor(rest[:, i % 2], general[:, b], parts[:, i, 0], ALU.subtract).then_inc(rest_done, 1)

                def valued(s):
                    for i in range(2):
                        dve.wait_ge(v_full, 2 * s + i + 1)
                        wait(dve, pv_done, UNITS * s)
                        dve.tensor_copy(values[:, 2 * i:2 * i + 2, :, 0:HD],
                                        general[:, bank("v", s, i)].rearrange("p (t h d) -> p t h d", t=2, d=HD)
                                        ).then_inc(v_copied, 1)

                def keep(q):
                    s, i = q // BS, q % BS
                    dve.wait_ge(attn_full, q + 1)
                    dve.tensor_copy(delta[:, q], general[:, bank("attn", s, i), 0:D]).then_inc(attn_kept, 1)
                    dve.wait_ge(attn_kept, q + 1)
                    dve.tensor_tensor(chosen[:, q], chosen[:, q], delta[:, q], ALU.add).then_inc(attn_added, 1)

                def attend(s):
                    for i in range(UNITS + 7):
                        n = UNITS * s + i
                        if i < UNITS:
                            dve.wait_ge(score_full, n + 1)
                            wait(dve, exp_done, GH * (n - 3))
                            dve.tensor_reduce(neg_max[:, n % 4], score_ps[:, n % 2].rearrange("p (g k) -> p g k", g=GH), AX, ALU.max,
                                              negate=True).then_inc(max_done, 1)
                        if 1 <= i <= UNITS:
                            dve.wait_ge(exp_done, GH * n)
                            wait(dve, probs_scaled, n - 4)
                            dve.reciprocal(r_sums[:, (n - 1) % 4], sums[:, (n - 1) % 4]).then_inc(sums_inverted, 1)
                        if 2 <= i <= UNITS + 1:
                            dve.wait_ge(turned, n - 1)
                            wait(dve, pv_done, n - 3)
                            dve.tensor_copy(probsT[:, n % 2], turned_ps[:, n % 2]).then_inc(turned_copied, 1)
                        if i >= 7 and (i - 7) % NG == 3:
                            keep(BS * s + (i - 7) // NG)
                    keep(BS * s + BS - 1) if (UNITS + 7 - 1 - 7) // NG < BS - 1 else None

                def feed_forward(s):
                    for f in range(FT):
                        n, r = FT * s + f, rows_of(f)
                        dve.wait_ge(silu_done, n + 1)
                        wait(dve, ff_full, BS * s)
                        dve.tensor_tensor(gated[0:r, f], silu[0:r, f % 2], turned_ps[0:r, f % 2], ALU.mult).then_inc(gated_done, 1)
                    for i in range(BS + 1):
                        if i < BS:
                            q = BS * s + i
                            dve.wait_ge(ff_full, q + 1)
                            dve.wait_ge(attn_added, q + 1)
                            dve.tensor_tensor(delta[:, q], out_ps[:, i % 2, 0:D], delta[:, q], ALU.add).then_inc(ff_added, 1)
                        if i >= 1:
                            q = BS * s + i - 1
                            for half in range(2):
                                dve.wait_ge(back_out, 2 * q + half + 1)
                                b = bank("back", s, 2 * (i - 1) + half)
                                dst = c.x[:, q, 2 * half:2 * half + 2]
                                dve.tensor_tensor(dst, general[:, b].rearrange("p (t d) -> p t d", t=2), dst, ALU.add).then_inc(general_read[b], 1)

                dve.wait_ge(constants, 1 + GH)
                normed(0, 0, 0)
                leftover(0)
                valued(0)
                attend(0)
                normed(1, 0, 1)
                leftover(1)
                valued(1)
                normed(2, 1, 0)
                feed_forward(0)
                attend(1)
                normed(3, 1, 1)
                feed_forward(1)

            @block.tensor
            def _(pe):
                def readers(kind, s, i):
                    if kind in ("xT", "back"):
                        b = bank(kind, s, i)
                        before = [u for u in uses[:uses.index((kind, s, i))] if u[0] in ("xT", "back") and bank(*u) == b]
                        return general_read[b], len(before) + 1
                    return {"qk": (rest_done, 4 * s + i + 1), "v": (v_copied, 2 * s + i + 1), "attn": (attn_kept, BS * s + i + 1)}[kind]

                def free(*use):
                    at = uses.index(use)
                    if at >= 2:
                        pe.wait_ge(*readers(*uses[at - 2]))

                def turn(j):
                    pe.wait_ge(rows_done, BS * j + BS)
                    for k in range(KD):
                        free("xT", j, k)
                        for i in range(BS):
                            last = pe.transpose(general[:, bank("xT", j, k), P * i:P * i + P], rows[:, i, P * k:P * k + P], c.ident[:])
                        last.then_inc(t_full, 1)
                    for k in range(KD):
                        pe.wait_ge(*readers("xT", j, k))

                def project(s):
                    turn(s)
                    for i in range(4):
                        free("qk", s, i)
                        col = (0, D, P, D + P)[i]
                        for k in range(KD):
                            last = pe.matmul(general[:, bank("qk", s, i)], wqkv[:, k, col:col + P], xT[:, k], start=(k == 0), stop=(k == KD - 1))
                        last.then_inc(qk_full, 1)
                    for i in range(2):
                        free("v", s, i)
                        for t in range(2):
                            tok = P * (2 * i + t)
                            for k in range(KD):
                                last = pe.matmul(general[:, bank("v", s, i), D * t:D * t + D], xT[:, k, tok:tok + P], wqkv[:, k, 2 * D:],
                                                 start=(k == 0), stop=(k == KD - 1))
                        last.then_inc(v_full, 1)

                def scores(n):
                    s, q, g = n // UNITS, (n % UNITS) // NG, n % NG
                    if n % UNITS == 0:
                        pe.wait_ge(stacked, 384 * s + 384)
                    if n % UNITS < 2:
                        wait(pe, silu_done, FT * s)
                    wait(pe, exp_done, GH * (n - 1))
                    for h in range(GH):
                        cols = slice(P * q, P * q + P)
                        pe.matmul(score_ps[:, n % 2, P * h:P * h + P], q_stack[0:ROWS, GH * g + h, cols], k_stack[0:ROWS, GH * g + h, cols],
                                  start=(h == 0), stop=False, skip_group_check=True)
                    pe.matmul(score_ps[:, n % 2], c.ident_b[:], causal4[:].rearrange("p g k -> p (g k)"),
                              start=False, stop=True, skip_group_check=True).then_inc(score_full, 1)

                def turn_probs(n):
                    pe.wait_ge(probs_scaled, n + 1)
                    wait(pe, turned_copied, n - 1)
                    if n % UNITS < 2:
                        wait(pe, gated_done, FT * (n // UNITS))
                    for g in range(GH):
                        last = pe.transpose(turned_ps[:, n % 2, P * g:P * g + P], probs[:, n % 3, g], c.ident[:])
                    last.then_inc(turned, 1)

                def with_values(n):
                    s, q, g = n // UNITS, n // NG, n % NG
                    pe.wait_ge(turned_copied, n + 1)
                    if g == 0:
                        pe.wait_ge(v_copied, 2 * s + 2)
                        wait(pe, attended_copied, q - 1)
                        if q % BS < 2:
                            wait(pe, ff_added, BS * s)
                    for h in range(GH):
                        last = pe.matmul(out_ps[32 * h:32 * h + 32, q % 2, P * g:P * g + P], values[:, q % BS, GH * g + h],
                                         probsT[:, n % 2, P * h:P * h + P], start=True, stop=True, tile_position=(0, 32 * h))
                    last.then_inc(pv_done, 1)

                def output(q):
                    s, i = q // BS, q % BS
                    pe.wait_ge(attended_copied, q + 1)
                    free("attn", s, i)
                    for g in range(NG):
                        last = pe.matmul(general[:, bank("attn", s, i), 0:D], attended[:, q % 2, P * g:P * g + P], wo[:, g],
                                         start=(g == 0), stop=(g == NG - 1))
                    last.then_inc(attn_full, 1)

                def attend(s):
                    for i in range(UNITS + 6):
                        n = UNITS * s + i
                        if i < UNITS:
                            scores(n)
                        if 2 <= i < UNITS + 2:
                            turn_probs(n - 2)
                        if 3 <= i < UNITS + 3:
                            with_values(n - 3)
                        if i >= 5 and (i - 5) % NG == 3:
                            output(BS * s + (i - 5) // NG)
                    if (UNITS + 6 - 1 - 5) // NG < BS - 1 or (UNITS + 6 - 1 - 5) % NG < 3 and (UNITS + 6 - 1 - 5) // NG == BS - 1:
                        output(BS * s + BS - 1)

                def feed_forward(s):
                    turn(SB + s)
                    for f in range(FT):
                        n, r = FT * s + f, rows_of(f)
                        if f < 2:
                            pe.wait_ge(exp_done, GH * UNITS * (s + 1))
                            pe.wait_ge(turned_copied, UNITS * (s + 1))
                        else:
                            pe.wait_ge(gated_done, n - 1)
                        for dst, w in ((score_ps, w1), (turned_ps, w2)):
                            for k in range(KD):
                                last = pe.matmul(dst[0:r, f % 2], w[:, k, P * f:P * f + r], xT[:, k], start=(k == 0), stop=(k == KD - 1))
                        last.then_inc(hidden_full, 1)
                    pe.wait_ge(gated_done, FT * s + FT)
                    for i in range(BS + 1):
                        if i < BS:
                            q = BS * s + i
                            if i < 2:
                                pe.wait_ge(attended_copied, BS * s + BS)
                            else:
                                pe.wait_ge(ff_added, q - 1)
                            for f in range(FT):
                                last = pe.matmul(out_ps[:, i % 2, 0:D], gated[0:rows_of(f), f, P * i:P * i + P], w3[0:rows_of(f), f],
                                                 start=(f == 0), stop=(f == FT - 1))
                            last.then_inc(ff_full, 1)
                        if i >= 1:
                            q = BS * s + i - 1
                            pe.wait_ge(ff_added, q + 1)
                            for half in range(2):
                                use = ("back", s, 2 * (i - 1) + half)
                                free(*use)
                                for t in range(2):
                                    tok = P * (2 * half + t)
                                    last = pe.matmul(general[:, bank(*use), D * t:D * t + D], back[:, q, tok:tok + P], delta[:, q], start=True, stop=True)
                                last.then_inc(back_out, 1)

                pe.wait_ge(constants, 1 + GH)
                project(0)
                attend(0)
                project(1)
                feed_forward(0)
                attend(1)
                feed_forward(1)

    nc.clear_and_free_semaphores(made)
    nc.all_engine_barrier()


def mixture_of_experts(nc, c, w_router, w_up, b_up, w_down, b_down, out):
    made = []
    E = w_up.shape[0]
    U = w_up.shape[2]
    UT = U // P
    NT = B * TT

    def sem(what):
        s = nc.alloc_semaphore(f"moe_{what}")
        made.append(s)
        return s

    with ExitStack() as ctx:
        def sb(what, shape, dt=F32):
            return ctx.enter_context(nc.sbuf_tensor(f"experts_{what}", shape, dt))

        def ps(what, shape, dt=F32):
            return ctx.enter_context(nc.psum_tensor(f"experts_{what}", shape, dt))

        up = sb("up", [P, 2, KD, U])
        down = sb("down", [P, 2, UT, D])
        up_bias = sb("up_bias", [P, E, UT])
        down_bias = sb("down_bias", [E, D])
        router = sb("router", [P, KD, E])
        stats = sb("stats", [P, NT, 6])
        mean_var = sb("mean_var", [P, NT, 2])
        var_eps = sb("var_eps", [P, NT])
        rstd = sb("rstd", [P, NT])
        xn = sb("xn", [P, 2, TT, D])
        xnT = sb("xnT", [P, B, KD, S])
        logits = sb("logits", [P, NT, E])
        below = sb("below", [P, NT, E])
        count = sb("count", [P, NT, E])
        past = sb("past", [P, NT, E])
        first, second = sb("first", [P, NT, E]), sb("second", [P, NT, E])
        best, place, gap, odds, total, gate1, gate2 = (
            sb(what, [P, NT]) for what in ("best", "place", "gap", "odds", "total", "gate1", "gate2"))
        best2, place2 = sb("best2", [P, NT]), sb("place2", [P, NT])
        gates = sb("gates", [P, NT, E])
        gatesT = sb("gatesT", [E, NT, P])
        bias_now = sb("bias_now", [P, 2, UT])
        gate_now = sb("gate_now", [P, 2, NT])
        hidden = sb("hidden", [P, 2, UT, S])

        up_ps = ps("up_ps", [P, 4, S])
        down_ps = ps("down_ps", [P, 2, TT, D])

        loaded = sem("loaded")
        weights_loaded = [sem(f"weights_loaded{s}") for s in range(2)]
        ready, ln_stats, ln_aggr, ln_eps, ln_rstd, ln_done = (
            sem(s) for s in ("ready", "ln_stats", "ln_aggr", "ln_eps", "ln_rstd", "ln_done"))
        xt_full, xt_copied, logits_full, logits_copied = (sem(s) for s in ("xt_full", "xt_copied", "logits_full", "logits_copied"))
        routed, odds_done, gt_full, gt_copied = (sem(s) for s in ("routed", "odds_done", "gt_full", "gt_copied"))
        bias_full, bias_added = sem("bias_full"), sem("bias_added")
        up_full, gelu_done, down_full, gate_taken, x_done = (
            sem(s) for s in ("up_full", "gelu_done", "down_full", "gate_taken", "x_done"))
        bias_taken = sem("bias_taken")
        sp_passed, dve_passed, stored = sem("sp_passed"), sem("dve_passed"), sem("stored")

        with nc.Block() as block:
            @block.sync
            def _(sp):
                sp.dma_start(router[:], w_router.rearrange("(k p) e -> p k e", p=P)).then_inc(loaded, 16)
                sp.dma_start(up_bias[:], b_up).then_inc(loaded, 16)
                sp.dma_start(down_bias[:], b_down).then_inc(loaded, 16)

                def load(e, slot):
                    hold(sp, down_full, TT * B * (e - 1), sp_passed)
                    one = lambda a: (a[e] if isinstance(e, int) else a[bass.ds(e, 1)].rearrange("o r n -> (o r) n")).rearrange(
                        "(k p) n -> p k n", p=P)
                    sp.dma_start(up[:, slot], one(w_up)).then_inc(weights_loaded[slot], 16)
                    sp.dma_start(down[:, slot], one(w_down)).then_inc(weights_loaded[slot], 16)

                load(0, 0)
                load(1, 1)
                with sp.Fori(1, E // 2) as i:
                    load(2 * i, 0)
                    load(2 * i + 1, 1)
                for b in range(B):
                    sp.wait_ge(x_done, TT * (B * (E - 1) + b + 1))
                    sp.dma_start(out[b].rearrange("(t p) d -> p t d", p=P), c.x[:, b]).then_inc(stored, 16)
                sp.wait_ge(stored, 16 * B)

            @block.gpsimd
            def _(pool):
                for e in range(E):
                    pool.memset(count[:, :, e], float(e)).then_inc(ready, 1)
                pool.wait_ge(ln_aggr, NT)
                pool.tensor_scalar(var_eps[:], mean_var[:, :, 1], 1e-5, None, ALU.add).then_inc(ln_eps, 1)
                pool.wait_ge(ln_eps, 1)
                pool.tensor_tensor(rstd[:], var_eps[:], c.minus_half[:, 0:NT], ALU.pow).then_inc(ln_rstd, 1)

            @block.scalar
            def _(act):
                act.preload_act_table_set("natural_log_exp_and_others")
                for b in range(B):
                    for k in range(KD):
                        act.wait_ge(xt_full, 2 * b + k + 1)
                        act.activation(xnT[:, b, k], up_ps[:, (2 * b + k) % 4], ACT.Copy).then_inc(xt_copied, 1)
                act.wait_ge(logits_full, 1)
                act.activation(logits[:].rearrange("p n e -> p (n e)"), down_ps[:, 0, 0], ACT.Copy).then_inc(logits_copied, 1)
                act.wait_ge(routed, 12)
                act.activation(odds[:], gap[:], ACT.Exp).then_inc(odds_done, 1)
                for i in range(NT // 4):
                    act.wait_ge(gt_full, i + 1)
                    act.activation(gatesT[:, 4 * i:4 * i + 4].rearrange("e n p -> e (n p)"), up_ps[0:E, i % 4], ACT.Copy).then_inc(gt_copied, 1)
                act.preload_act_table_set("gelu_and_others")

                def step(e, slot, b):
                    n = B * e + b
                    wait(act, down_full, TT * (n - 1))
                    for u in range(UT):
                        act.wait_ge(up_full, UT * n + u + 1)
                        bias = bias_now[:, slot, u:u + 1]
                        act.activation(hidden[:, b % 2, u], up_ps[:, u % 4], ACT.Gelu, bias=bias).then_inc(gelu_done, 1)

                def pair(i):
                    for slot in range(2):
                        take_bias(2 * i + slot, slot)
                        for b in range(B):
                            step(2 * i + slot, slot, b)

                def take_bias(e, slot):
                    wait(act, gelu_done, UT * B * (e - 1))
                    act.activation(bias_now[:, slot], up_bias[:, e] if isinstance(e, int) else up_bias[:, bass.ds(e, 1), :].rearrange("p o u -> p (o u)"),
                                   ACT.Copy).then_inc(bias_taken, 1)
                    act.wait_ge(bias_taken, e + 1)

                act.wait_ge(loaded, 16 * 3)
                pair(0)
                with act.Fori(1, E // 2) as i:
                    pair(i)

            @block.vector
            def _(dve):
                for b in range(B):
                    for t in range(TT):
                        dve.bn_stats(stats[:, TT * b + t], c.x[:, b, t]).then_inc(ln_stats, 1)
                for n in range(NT):
                    dve.wait_ge(ln_stats, n + 1)
                    dve.bn_aggr(mean_var[:, n], stats[:, n]).then_inc(ln_aggr, 1)
                dve.wait_ge(ln_rstd, 1)
                dve.wait_ge(ln_aggr, NT)
                for b in range(B):
                    wait(dve, xt_full, 2 * (b - 1))
                    for t in range(TT):
                        n = TT * b + t
                        dve.tensor_scalar(xn[:, b % 2, t], c.x[:, b, t], mean_var[:, n, 0:1], rstd[:, n:n + 1],
                                          ALU.subtract, ALU.mult).then_inc(ln_done, 1)

                def wide(a):
                    return a[:].unsqueeze(2).to_broadcast([P, NT, E])

                steps = 0

                def then(instruction):
                    nonlocal steps
                    steps += 1
                    instruction.then_inc(routed, 1)
                    dve.wait_ge(routed, steps)

                def pick(source, value, where, one_hot):
                    then(dve.tensor_reduce(value[:], source[:], AX, ALU.max))
                    then(dve.tensor_tensor(past[:], source[:], wide(value), ALU.is_lt))
                    then(dve.scalar_tensor_tensor(past[:], past[:], float(E), count[:], ALU.mult, ALU.add))
                    then(dve.tensor_reduce(where[:], past[:], AX, ALU.min))
                    then(dve.tensor_tensor(one_hot[:], count[:], wide(where), ALU.is_equal))

                dve.wait_ge(ready, E)
                dve.wait_ge(logits_copied, 1)
                pick(logits, best, place, first)
                then(dve.scalar_tensor_tensor(below[:], first[:], NEG, logits[:], ALU.mult, ALU.add))
                pick(below, best2, place2, second)
                then(dve.tensor_tensor(gap[:], best2[:], best[:], ALU.subtract))
                assert steps == 12
                dve.wait_ge(odds_done, 1)
                then(dve.tensor_scalar(total[:], odds[:], 1.0, None, ALU.add))
                then(dve.reciprocal(gate1[:], total[:]))
                then(dve.tensor_tensor(gate2[:], gate1[:], odds[:], ALU.mult))
                then(dve.tensor_tensor(first[:], first[:], wide(gate1), ALU.mult))
                then(dve.tensor_tensor(second[:], second[:], wide(gate2), ALU.mult))
                then(dve.tensor_tensor(gates[:], first[:], second[:], ALU.add))

                def take_gate(e, slot):
                    wait(dve, x_done, TT * B * (e - 1))
                    src = gates[:, :, e] if isinstance(e, int) else gates[:, :, bass.ds(e, 1)].rearrange("p n o -> p (n o)")
                    hold(dve, x_done, TT * B * (e - 1), dve_passed)
                    dve.tensor_copy(gate_now[:, slot], src).then_inc(gate_taken, 1)
                    dve.wait_ge(gate_taken, e + 1)

                def step(e, slot, b):
                    n = B * e + b
                    for t in range(TT):
                        dve.wait_ge(down_full, TT * n + 2 * (t // 2) + 2)
                        wait(dve, x_done, TT * (n - B) + t + 1)
                        dve.scalar_tensor_tensor(c.x[:, b, t], down_ps[:, b % 2, t], gate_now[:, slot, TT * b + t:TT * b + t + 1],
                                                 c.x[:, b, t], ALU.mult, ALU.add).then_inc(x_done, 1)

                for i in range(NT // 2):
                    dve.wait_ge(bias_full, i + 1)
                    dst = c.x[:, i // 2, 2 * (i % 2):2 * (i % 2) + 2]
                    dve.tensor_tensor(dst, down_ps[:, (i // 2) % 2, 2 * (i % 2):2 * (i % 2) + 2], dst, ALU.add).then_inc(bias_added, 1)
                dve.wait_ge(bias_added, NT // 2)

                def pair(i):
                    for slot in range(2):
                        take_gate(2 * i + slot, slot)
                        for b in range(B):
                            step(2 * i + slot, slot, b)

                pair(0)
                with dve.Fori(1, E // 2) as i:
                    pair(i)

            @block.tensor
            def _(pe):
                pe.wait_ge(loaded, 16 * 3)
                for b in range(B):
                    pe.wait_ge(ln_done, TT * b + TT)
                    for k in range(KD):
                        n = 2 * b + k
                        wait(pe, xt_copied, n - 3)
                        for t in range(TT):
                            last = pe.transpose(up_ps[:, n % 4, P * t:P * t + P], xn[:, b % 2, t, P * k:P * k + P], c.ident[:])
                        last.then_inc(xt_full, 1)
                for b in range(B):
                    pe.wait_ge(xt_copied, 2 * b + 2)
                    for t in range(TT):
                        for k in range(KD):
                            last = pe.matmul(down_ps[:, 0, 0, E * (TT * b + t):E * (TT * b + t) + E], xnT[:, b, k, P * t:P * t + P],
                                             router[:, k], start=(k == 0), stop=(k == KD - 1))
                last.then_inc(logits_full, 1)
                pe.wait_ge(routed, 18)
                for i in range(NT // 4):
                    wait(pe, gt_copied, i - 3)
                    for t in range(4):
                        last = pe.transpose(up_ps[0:E, i % 4, P * t:P * t + P], gates[:, 4 * i + t], c.ident[:])
                    last.then_inc(gt_full, 1)
                for i in range(NT // 2):
                    pe.wait_ge(gt_copied, i // 2 + 1)
                    wait(pe, bias_added, i - 3)
                    for t in range(2):
                        last = pe.matmul(down_ps[:, (i // 2) % 2, 2 * (i % 2) + t], gatesT[:, 2 * i + t], down_bias[:], start=True, stop=True)
                    last.then_inc(bias_full, 1)

                def hidden_tile(e, slot, b, u):
                    n = B * e + b
                    if b == 0 and u == 0:
                        pe.wait_ge(weights_loaded[slot], 16 * (e - slot) + 32)
                    wait(pe, gelu_done, UT * n + u - 3)
                    for k in range(KD):
                        last = pe.matmul(up_ps[:, u % 4], up[:, slot, k, P * u:P * u + P], xnT[:, b, k], start=(k == 0), stop=(k == KD - 1))
                    last.then_inc(up_full, 1)

                def output_part(e, slot, b, i):
                    n, t = B * e + b, i // 2
                    if i == 0:
                        pe.wait_ge(gelu_done, UT * n + UT)
                        wait(pe, x_done, TT * (n - 1))
                    for u in range(UT // 2 * (i % 2), UT // 2 * (i % 2) + UT // 2):
                        last = pe.matmul(down_ps[:, b % 2, t], hidden[:, b % 2, u, P * t:P * t + P], down[:, slot, u],
                                         start=(u == 0), stop=(u == UT - 1))
                    if i % 2 == 1:
                        last.then_inc(down_full, 1)

                def step(e, slot, b, behind):
                    for u in range(UT):
                        hidden_tile(e, slot, b, u)
                        if behind is not None:
                            output_part(*behind, u)

                def pair(i):
                    for slot in range(2):
                        for b in range(B):
                            if b > 0:
                                behind = (2 * i + slot, slot, b - 1)
                            elif slot == 1:
                                behind = (2 * i, 0, B - 1)
                            else:
                                behind = None if isinstance(i, int) else (2 * i - 1, 1, B - 1)
                            step(2 * i + slot, slot, b, behind)

                pe.wait_ge(gt_copied, NT // 4)
                pe.wait_ge(bias_added, NT // 2)
                pair(0)
                with pe.Fori(1, E // 2) as i:
                    pair(i)
                for u in range(UT):
                    output_part(E - 1, 1, B - 1, u)

    nc.clear_and_free_semaphores(made)
    nc.all_engine_barrier()


class Shared:

    def __init__(self, nc, ctx):
        def sb(name, shape, dt=F32):
            return ctx.enter_context(nc.sbuf_tensor(name, shape, dt))

        self.x = sb("x_stream", [P, B, TT, D])
        self.ident = sb("ident", [P, P])
        self.ident_b = sb("ident_b", [P, P], BF16)
        self.causal_kq = sb("causal_kq", [P, P], BF16)
        self.causal_qk = sb("causal_qk", [P, P], BF16)
        self.head_ones = sb("head_ones", [P, P])
        self.minus_half = sb("minus_half", [P, 32])


def lay_out(**a):
    a = {k: np.asarray(v) for k, v in a.items()}

    def out_rows(w, bias=None):
        rows = np.zeros((NG, GH, 32, D), np.float32)
        rows[:, :, :HD] = w.reshape(NG, GH, HD, D)
        if bias is not None:
            rows[0, 0, HD] = bias
        return rows.reshape(NG, P, D)

    def cross(name, wq, wk, wv, wo, bq, bk, bv, bo):
        return {name + "_wq": wq, name + "_wk": wk, name + "_wv": wv, name + "_wo": out_rows(wo, bo),
                name + "_bq": np.ascontiguousarray(bq.reshape(KD, P).T), name + "_bk": np.ascontiguousarray(bk.reshape(KD, P).T),
                name + "_bv": np.tile(bv, (P, 1))}

    S2 = a["ctx_1024"].shape[1]
    t = lambda w: np.ascontiguousarray(w.T)
    qkv0, qkv1 = t(a["L0_attn_w_attn"]), t(a["L1_attn_qkv_w"])
    return {
        "x": a["x"],
        "l0_qk": np.ascontiguousarray(qkv0[:, :2 * D]), "l0_v": np.ascontiguousarray(qkv0[:, 2 * D:]),
        "l0_o": out_rows(t(a["L0_attn_w_proj"])),
        "l1_qk": np.ascontiguousarray(qkv1[:, :2 * D]), "l1_v": np.ascontiguousarray(qkv1[:, 2 * D:]),
        "l1_o": out_rows(t(a["L1_attn_proj_w"]), a["L1_attn_proj_b"]),
        "ctx_t": np.ascontiguousarray(a["ctx_1024"].reshape(B * S2, D).T),
        "ctx_twice": np.ascontiguousarray(np.repeat(a["ctx_1024"].transpose(0, 2, 1).reshape(B, KD, P, 1, S2), 2, axis=3)).reshape(B, KD, P, P),
        "mask_t": np.ascontiguousarray(a["mask_BxSxS2_ff0"].transpose(0, 2, 1)),
        **cross("x0", a["L0_xattn_wq"], a["L0_xattn_wk"], a["L0_xattn_wv"], a["L0_xattn_wo"],
                a["L0_xattn_bq"], a["L0_xattn_bk"], a["L0_xattn_bv"], a["L0_xattn_bo"]),
        **cross("x1", t(a["L1_xattn_WQ_w"]), t(a["L1_xattn_WK_w"]), t(a["L1_xattn_WV_w"]), t(a["L1_xattn_WO_w"]),
                a["L1_xattn_WQ_b"], a["L1_xattn_WK_b"], a["L1_xattn_WV_b"], a["L1_xattn_WO_b"]),
        "mod_router": np.tile(a["L0_ffn_w_router"], (P, 1)), "mod_qkv": t(a["L0_ffn_W_qkv"]), "mod_o": out_rows(t(a["L0_ffn_W_out"])),
        "mod_g1": np.ascontiguousarray(a["L0_ffn_g1"].reshape(KD, P).T), "mod_g2": np.ascontiguousarray(a["L0_ffn_g2"].reshape(KD, P).T),
        "mod_w1": t(a["L0_ffn_W1"]), "mod_w2": t(a["L0_ffn_W2"]), "mod_w3": t(a["L0_ffn_W3"]),
        "moe_router": t(a["L1_ffn_w_router"]), "moe_up": np.ascontiguousarray(a["L1_ffn_w_up"].transpose(0, 2, 1)),
        "moe_down": np.ascontiguousarray(a["L1_ffn_w_down"].transpose(0, 2, 1)), "moe_bu": np.ascontiguousarray(a["L1_ffn_b_up"].reshape(8, -1, P).transpose(2, 0, 1)), "moe_bd": a["L1_ffn_b_down"],
        "l1_qg": np.tile(a["L1_attn_q_norm_w"], P // HD).reshape(P, 1),
        "l1_kg": np.tile(a["L1_attn_k_norm_w"], P // HD).reshape(P, 1),
    }


def cross_stage(nc, c, name, i, masked):
    w = lambda what: i[f"{name}_{what}"]
    cross_attention(nc, c, "cross" + name, w("wq"), w("wk"), w("wv"), w("wo"), w("bq"), w("bk"), w("bv"), i["ctx_t"], i["ctx_twice"],
                    i["mask_t"] if masked else None)


STAGES = {
    "1": lambda nc, c, i: self_attention(nc, c, "self0", i["l0_qk"], i["l0_v"], i["l0_o"], True, x_in=i["x"]),
    "2": lambda nc, c, i: cross_stage(nc, c, "x0", i, False),
    "3": lambda nc, c, i: mixture_of_depths(nc, c, *(i["mod_" + w] for w in ("router", "qkv", "o", "g1", "g2", "w1", "w2", "w3"))),
    "4": lambda nc, c, i: self_attention(nc, c, "self1", i["l1_qk"], i["l1_v"], i["l1_o"], False, norm_weights=(i["l1_qg"], i["l1_kg"])),
    "5": lambda nc, c, i: cross_stage(nc, c, "x1", i, True),
    "6": lambda nc, c, i: mixture_of_experts(nc, c, i["moe_router"], i["moe_up"], i["moe_bu"], i["moe_down"], i["moe_bd"], i["out"]),
}


def program(nc, i):
    with ExitStack() as ctx:
        c = Shared(nc, ctx)
        constants_made = make_constants(nc, c)
        nc.clear_and_free_semaphores(constants_made)
        nc.all_engine_barrier()
        for stage in STAGES.values():
            stage(nc, c, i)


def kernel(**inputs):
    import concourse.bacc as _bacc
    from concourse import mybir as _mybir
    from concourse.bass_utils import run_bass_kernel_spmd as _run

    arrays = lay_out(**inputs)
    nc = _bacc.Bacc("TRN2", target_bir_lowering=False, num_devices=1)
    tensors = {name: nc.dram_tensor(name + "_dram", a.shape, _mybir.dt.from_np(a.dtype), kind="ExternalInput").ap()
               for name, a in arrays.items()}
    tensors["out"] = nc.dram_tensor("out_dram", (B, S, D), F32, kind="ExternalOutput").ap()
    program(nc, tensors)
    nc.finalize()
    r = _run(nc, [{name + "_dram": a for name, a in arrays.items()}], core_ids=[0])
    return np.array(r.results[0]["out_dram"]).reshape(B, S, D)
```

```python
from contextlib import ExitStack

import numpy as np

import concourse.bass as bass
from concourse import mybir

F32 = mybir.dt.float32
BF16 = mybir.dt.bfloat16
I32 = mybir.dt.int32
U32 = mybir.dt.uint32
ALU = mybir.AluOpType
ACT = mybir.ActivationFunctionType
AX = mybir.AxisListType.X

P = 128
B, S, D, H = 8, 512, 256, 16
HD = D // H
TT = S // P
KD = D // P
NG, GH = 4, 4
SPLITS = 6
ROWS = SPLITS * HD
SHIFT = ROWS
KROWS = ROWS + 3
NEG = -1.0e30
Q_PART = (0, 1, 2, 0, 1, 0)
K_PART = (0, 0, 0, 1, 1, 2)


def wait(eng, sem, value):
    if not isinstance(value, int) or value > 0:
        eng.wait_ge(sem, value)


def hold(eng, sem, value, passed):
    if not isinstance(value, int):
        eng.wait_ge(sem, value)
        eng.sem_inc(passed)
    elif value > 0:
        eng.wait_ge(sem, value)


def make_constants(nc, c):
    made = nc.alloc_semaphore("constants_made")

    with nc.Block() as block:
        @block.gpsimd
        def _(pool):
            pool.memset(c.ident[:], 0.0).then_inc(made, 1)
            pool.memset(c.causal_kq[:], 0.0).then_inc(made, 1)
            pool.memset(c.causal_qk[:], 0.0).then_inc(made, 1)
            pool.memset(c.head_ones[:], 1.0).then_inc(made, 1)
            pool.memset(c.minus_half[:], -0.5).then_inc(made, 1)
            pool.memset(c.slots.filling[:], 0.0).then_inc(made, 1)
            pool.wait_ge(made, 6)
            pool.memset(c.slots.filling[:, Slots.ID:Slots.ID + 1].bitcast(U32), Slots.NOBODY).then_inc(made, 1)
            pool.affine_select(out=c.ident[:], in_=c.ident[:], compare_op=ALU.not_equal, fill=1.0, base=0,
                               pattern=[[-1, P]], channel_multiplier=1).then_inc(made, 1)
            pool.affine_select(out=c.causal_kq[:], in_=c.causal_kq[:], compare_op=ALU.is_ge, fill=NEG, base=0,
                               pattern=[[1, P]], channel_multiplier=-1).then_inc(made, 1)
            pool.affine_select(out=c.causal_qk[:], in_=c.causal_qk[:], compare_op=ALU.is_ge, fill=NEG, base=0,
                               pattern=[[-1, P]], channel_multiplier=1).then_inc(made, 1)
            view = c.head_ones[:].rearrange("p (h d) -> p h d", d=HD)
            pool.affine_select(out=view, in_=view, compare_op=ALU.is_ge, fill=0.0, base=0,
                               pattern=[[-HD, P // HD], [0, HD]], channel_multiplier=1).then_inc(made, 1)
            pool.wait_ge(made, 11)
            pool.affine_select(out=view, in_=view, compare_op=ALU.is_ge, fill=0.0, base=HD - 1,
                               pattern=[[HD, P // HD], [0, HD]], channel_multiplier=-1).then_inc(made, 1)
            pool.tensor_copy(c.ident_b[:], c.ident[:]).then_inc(made, 1)
            pool.wait_ge(made, 13)
    return [made]


def self_attention(nc, c, name, w_qk, w_v, w_o, causal, norm_weights=None, x_in=None):
    norm = norm_weights is not None
    made = []

    def sem(what):
        s = nc.alloc_semaphore(f"{name}_{what}")
        made.append(s)
        return s

    with ExitStack() as ctx:
        def sb(what, shape, dt=F32):
            return ctx.enter_context(nc.sbuf_tensor(f"{name}_{what}", shape, dt))

        def ps(what, shape, dt=F32):
            return ctx.enter_context(nc.psum_tensor(f"{name}_{what}", shape, dt))

        wqk = sb("wqk", [P, KD, 2 * D])
        wv = sb("wv", [P, KD, D])
        wo = sb("wo", [P, NG, D])
        stats = sb("stats", [P, TT, 6])
        mean_var = sb("mean_var", [P, TT, 2])
        var_eps = sb("var_eps", [P, TT])
        rstd = sb("rstd", [P, TT])
        xn = sb("xn", [P, TT, D])
        xnT = sb("xnT", [P, KD, S])
        qk = sb("qk", [P, 4, S])
        parts = sb("parts", [P, 4, 3, S], BF16)
        rest = sb("rest", [P, 4, S])
        q_stack = sb("q_stack", [P, H, S], BF16)
        k_stack = sb("k_stack", [P, H, S], BF16)
        values = sb("values", [P, TT, H, 32])
        neg_max = sb("neg_max", [P, 2, TT, GH])
        shift1 = sb("shift1", [GH, 2, 3, S], BF16)
        shift_rest = sb("shift_rest", [GH, 2, S])
        probs = sb("probs", [P, 8, S])
        o_raw = sb("o_raw", [P, 2, S])
        denom = sb("denom", [P, 2, S])
        r_denom = sb("r_denom", [P, 2, S])
        log_sum = sb("log_sum", [P, S])
        residue = sb("residue", [P, S])
        o_norm = sb("o_norm", [P, NG, S])
        if norm:
            squares = sb("squares", [P, 2, S])
            log_ms = sb("log_ms", [P, 2, S])
            r_rms = sb("r_rms", [P, 2, S])
            qk_raw = sb("qk_raw", [P, 4, S])
            gains = sb("gains", [P, 2])
            rms_eps = sb("rms_eps", [P, 1])
        scratch = nc.dram_tensor(f"{name}_parts_dram", [4, P, 3, S], BF16).ap()

        general = ps("general", [P, 2, S])
        max_ps = ps("max_ps", [P, 2, S])
        score_ps = ps("score_ps", [P, 3, S])
        out_ps = ps("out_ps", [P, S])

        ready = sem("ready")
        pool_passed, dve_passed, sp_passed = sem("pool_passed"), sem("dve_passed"), sem("sp_passed")
        loaded = sem("loaded")
        x_loaded = [sem(f"x_loaded{b}") for b in range(B)] if x_in is not None else None
        scaled = sem("scaled")
        ln_stats, ln_aggr, ln_eps, ln_rstd, ln_done = (sem(s) for s in ("ln_stats", "ln_aggr", "ln_eps", "ln_rstd", "ln_done"))
        xt_full, xt_copied = sem("xt_full"), sem("xt_copied")
        qk_full, qk_copied = sem("qk_full"), sem("qk_copied")
        sq_done, ss_full, ss_log, ss_rstd, qk_normed = (sem(s) for s in ("sq_done", "ss_full", "ss_log", "ss_rstd", "qk_normed")) if norm else [None] * 5
        part0_cut, rest_done, part1_cut, part2_cut = (sem(s) for s in ("part0_cut", "rest_done", "part1_cut", "part2_cut"))
        parts_stored = [sem(f"parts_stored{i}") for i in range(2)]
        stacked = [sem(f"stacked{g}") for g in range(NG)]
        max_full, max_read = sem("max_full"), sem("max_read")
        mt_full, shift_a, shift_r, shift_b, shift_c = (sem(s) for s in ("mt_full", "shift_a", "shift_r", "shift_b", "shift_c"))
        shift_placed = [sem(f"shift_placed{g}") for g in range(NG)]
        score_full, exp_done, pv_done = sem("score_full"), sem("exp_done"), sem("pv_done")
        o_copied, denom_done, recip_done, o_done = sem("o_copied"), sem("denom_done"), sem("recip_done"), sem("o_done")
        log_done, guess_done, residue_done = sem("log_done"), sem("guess_done"), sem("residue_done")
        v_full, v_copied = sem("v_full"), sem("v_copied")
        e_full, x_done = sem("e_full"), sem("x_done")

        ITEMS = range(4)
        COLUMNS = (0, D, P, D + P)

        order = ["mt1", "xt0", "xt1", "p0", "p1", "p2"] + (["s0", "p3", "s1", "s2", "s3"] if norm else ["p3"])
        order += ["mt2", "e0", "e1", "mt3", "mt0", "v0", "v1"]
        assert len(order) % 2 == 0
        bank = {what: n % 2 for n, what in enumerate(order)}

        def width(j):
            return S - P * j if causal else S

        with nc.Block() as block:
            @block.sync
            def _(sp):
                def load_x(b):
                    sp.dma_start(c.x[:, b], x_in[b].rearrange("(t p) d -> p t d", p=P)).then_inc(x_loaded[b], 16)

                if x_in is not None:
                    load_x(0)
                sp.dma_start(wqk[:], w_qk.rearrange("(k p) n -> p k n", p=P)).then_inc(loaded, 16)
                sp.dma_start(wv[:], w_v.rearrange("(k p) n -> p k n", p=P)).then_inc(loaded, 16)
                sp.dma_start(wo[:], w_o.rearrange("g p n -> p g n")).then_inc(loaded, 16)
                if norm:
                    for i in range(2):
                        sp.dma_start(gains[:, i:i + 1], norm_weights[i]).then_inc(loaded, 16)

                if x_in is not None:
                    for b in range(1, B):
                        load_x(b)

                def stack(b, g):
                    half = g // 2
                    if g % 2 == 0:
                        for item in (2 * half, 2 * half + 1):
                            hold(sp, part2_cut, 4 * b + item + 1, sp_passed)
                            hold(sp, stacked[2 * half], 192 * b, sp_passed)
                            hold(sp, stacked[2 * half + 1], 192 * b, sp_passed)
                            sp.dma_start(scratch[item], parts[:, item]).then_inc(parts_stored[half], 16)
                        hold(sp, parts_stored[half], 32 * b + 32, sp_passed)
                    rows = slice((g % 2) * 64, (g % 2) * 64 + 64)
                    for stk, item, which in ((q_stack, 2 * half, Q_PART), (k_stack, 2 * half + 1, K_PART)):
                        for r, part in enumerate(which):
                            sp.dma_start(stk[HD * r:HD * r + HD, GH * g:GH * g + GH, :],
                                         scratch[item, rows, part, :].rearrange("(h d) t -> d h t", d=HD)
                                         ).then_inc(stacked[g], 16)

                def place_shift(number, g):
                    hold(sp, shift_c, number, sp_passed)
                    for i in range(3):
                        sp.dma_start(q_stack[SHIFT + i:SHIFT + i + 1, GH * g:GH * g + GH, :],
                                     shift1[:, g % 2, i, :]).then_inc(shift_placed[g], 16)

                for g in range(NG):
                    stack(0, g)
                place_shift(1, 0)

                def sequence(b):
                    if x_in is not None:
                        c.slots.fill(sp, b)
                    for g in range(NG):
                        for group in ((1, 2), (), (3,), (4,))[g]:
                            place_shift(4 * b + group + 1, group % NG)
                        hold(sp, score_full, 64 * b + 16 * g + 16, sp_passed)
                        stack(b + 1, g)

                sequence(0)
                with sp.Fori(1, B - 1) as b:
                    sequence(b)
                if x_in is not None:
                    c.slots.fill(sp, B - 1)
                for g in (1, 2, 3):
                    place_shift(4 * (B - 1) + g + 1, g)

            @block.gpsimd
            def _(pool):
                pool.memset(values[:, :, :, HD:], 1.0).then_inc(ready, 1)
                pool.wait_ge(ready, 1)
                pool.memset(k_stack[SHIFT:KROWS], 1.0).then_inc(ready, 1)
                pool.wait_ge(ready, 2)
                if norm:
                    pool.memset(rms_eps[:], 1e-6).then_inc(ready, 1)
                pool.wait_ge(loaded, 16 * (5 if norm else 3))
                if norm:
                    pool.tensor_scalar(gains[:, 0:1], gains[:, 0:1], HD ** -0.5, None, ALU.mult).then_inc(scaled, 1)
                else:
                    pool.tensor_scalar(wqk[:, :, 0:D], wqk[:, :, 0:D], HD ** -0.5, None, ALU.mult).then_inc(scaled, 1)

                def layer_norm(b):
                    hold(pool, ln_aggr, 4 * b + 4, pool_passed)
                    pool.tensor_scalar(var_eps[:], mean_var[:, :, 1], 1e-5, None, ALU.add).then_inc(ln_eps, 1)
                    pool.wait_ge(ln_eps, b + 1)
                    pool.tensor_tensor(rstd[:], var_eps[:], c.minus_half[:, 0:TT], ALU.pow).then_inc(ln_rstd, 1)

                def square(b, i):
                    pool.wait_ge(qk_copied, 4 * b + i + 1)
                    if i >= 2:
                        pool.wait_ge(ss_full, 4 * b + i - 1)
                    pool.tensor_tensor(squares[:, i % 2], qk_raw[:, i], qk_raw[:, i], ALU.mult).then_inc(sq_done, 1)

                def square_all(b):
                    for i in ITEMS:
                        square(b, i)

                def cut(b, i):
                    pool.wait_ge(part1_cut, 4 * b + i + 1)
                    pool.tensor_tensor(parts[:, i, 2], rest[:, i], parts[:, i, 1], ALU.subtract).then_inc(part2_cut, 1)

                def cut_all(b):
                    for i in ITEMS:
                        cut(b, i)

                def shift(b, g):
                    n = 4 * b + g
                    hold(pool, shift_r, n + 1, pool_passed)
                    pool.tensor_copy(shift1[:, g % 2, 1], shift_rest[:, g % 2]).then_inc(shift_b, 1)
                    pool.wait_ge(shift_b, n + 1)
                    pool.tensor_tensor(shift1[:, g % 2, 2], shift_rest[:, g % 2], shift1[:, g % 2, 1],
                                       ALU.subtract).then_inc(shift_c, 1)

                def normalise(b, g):
                    pool.wait_ge(recip_done, 4 * b + g + 1)
                    wait(pool, e_full, 2 * b)
                    pool.tensor_tensor(o_norm[:, g], o_raw[:, g % 2], r_denom[:, g % 2], ALU.mult).then_inc(o_done, 1)

                layer_norm(0)
                if norm:
                    square_all(0)
                cut_all(0)
                shift(0, 0)

                def sequence(b):
                    layer_norm(b + 1)
                    shift(b, 1)
                    if not isinstance(b, int) or b > 0:
                        normalise(b - 1, 3)
                    if norm:
                        square_all(b + 1)
                    shift(b, 2)
                    cut_all(b + 1)
                    normalise(b, 0)
                    shift(b, 3)
                    normalise(b, 1)
                    shift(b + 1, 0)
                    normalise(b, 2)

                sequence(0)
                with pool.Fori(1, B - 1) as b:
                    sequence(b)
                last = B - 1
                for g in range(NG):
                    if g + 1 < NG:
                        shift(last, g + 1)
                    if g > 0:
                        normalise(last, g - 1)
                    else:
                        normalise(last - 1, 3)
                normalise(last, 3)

            @block.scalar
            def _(act):
                act.preload_act_table_set("natural_log_exp_and_others")
                act.wait_ge(ready, 3 if norm else 2)

                def transposed(b):
                    for k in range(KD):
                        act.wait_ge(xt_full, 2 * b + k + 1)
                        act.activation(xnT[:, k], general[:, bank[f"xt{k}"]], ACT.Copy).then_inc(xt_copied, 1)

                def mean_square(b, i):
                    act.wait_ge(ss_full, 4 * b + i + 1)
                    wait(act, qk_normed, 4 * b + i - 1)
                    act.activation(log_ms[:, i % 2], general[:, bank[f"s{i}"]], ACT.Ln, bias=rms_eps[:],
                                   scale=1.0 / HD).then_inc(ss_log, 1)
                    act.wait_ge(ss_log, 4 * b + i + 1)
                    act.activation(r_rms[:, i % 2], log_ms[:, i % 2], ACT.Exp, scale=-0.5).then_inc(ss_rstd, 1)

                def projected(b, items):
                    for i in items:
                        act.wait_ge(qk_full, 4 * b + i + 1)
                        if norm:
                            wait(act, qk_normed, 4 * b + i - 3)
                            act.activation(qk_raw[:, i], general[:, bank[f"p{i}"]], ACT.Copy).then_inc(qk_copied, 1)
                            if i >= 2:
                                mean_square(b, i - 2)
                        else:
                            first_part(b, i)
                        if norm and i == 3:
                            mean_square(b, 2)
                            mean_square(b, 3)

                def first_part(b, i):
                    wait(act, parts_stored[i // 2], 32 * b)
                    if norm:
                        act.wait_ge(qk_normed, 4 * b + i + 1)
                    act.activation(parts[:, i, 0], qk[:, i] if norm else general[:, bank[f"p{i}"]], ACT.Copy).then_inc(part0_cut, 1)

                def second_part(b, i):
                    act.wait_ge(rest_done, 4 * b + i + 1)
                    act.activation(parts[:, i, 1], rest[:, i], ACT.Copy).then_inc(part1_cut, 1)

                def shift(b, g):
                    act.wait_ge(mt_full, 4 * b + g + 1)
                    wait(act, shift_placed[(g + 2) % NG], 48 * b + (48 if g >= 2 else 0))
                    act.activation(shift1[:, g % 2, 0], general[0:GH, bank[f"mt{g}"]], ACT.Copy).then_inc(shift_a, 1)

                def invert(b, g):
                    n = 4 * b + g
                    act.wait_ge(denom_done, n + 1)
                    act.activation(log_sum[:], denom[:, g % 2], ACT.Ln).then_inc(log_done, 1)
                    act.wait_ge(log_done, n + 1)
                    wait(act, o_done, n - 1)
                    act.activation(r_denom[:, g % 2], log_sum[:], ACT.Exp, scale=-1.0).then_inc(guess_done, 1)

                def copy_out(b, g):
                    n = 4 * b + g
                    act.wait_ge(pv_done, 4 * n + 4)
                    wait(act, o_done, n - 1)
                    act.activation(o_raw[:, g % 2], out_ps[:], ACT.Copy).then_inc(o_copied, 1)

                def group(b, g, after):
                    n = 4 * b + g
                    for j in range(TT):
                        w = width(j)
                        wait(act, pv_done, 4 * n + j - 1)
                        for h in range(GH):
                            i = 4 * j + h
                            act.wait_ge(score_full, 16 * n + i + 1)
                            act.activation(probs[:, i % 8, 0:w], score_ps[:, i % 3, 0:w], ACT.Exp).then_inc(exp_done, 1)
                        for work, *of in after.get(j, ()):
                            work(*of)

                def cuts(b):
                    if norm:
                        return ([(first_part, b, 0), (first_part, b, 1)],
                                [(second_part, b, 0), (second_part, b, 1), (first_part, b, 2), (first_part, b, 3)],
                                [(second_part, b, 2), (second_part, b, 3)])
                    return [(second_part, b, 0), (second_part, b, 1)], [(second_part, b, 2), (second_part, b, 3)], []

                transposed(0)
                projected(0, ITEMS)
                for work, *of in sum(cuts(0), []):
                    work(*of)
                shift(0, 0)

                def group0(b, more):
                    first = isinstance(b, int) and b == 0
                    group(b, 0, {0: [(shift, b, 1)] + ([] if first else [(invert, b - 1, 3)]),
                                 1: [(transposed, b + 1)] if more else [], 3: [(projected, b + 1, (0, 1))] if more else []})

                def sequence(b):
                    group0(b, True)
                    copy_out(b, 0)
                    projected(b + 1, (2, 3))
                    c0, c1, c2 = cuts(b + 1)
                    group(b, 1, {0: [(shift, b, 2)] + c0, 1: [(invert, b, 0)] + c1, 2: c2})
                    group(b, 2, {0: [(copy_out, b, 1), (shift, b, 3)], 1: [(invert, b, 1)]})
                    group(b, 3, {0: [(copy_out, b, 2), (shift, b + 1, 0)], 1: [(invert, b, 2)]})
                    copy_out(b, 3)

                sequence(0)
                with act.Fori(1, B - 1) as b:
                    sequence(b)
                last = B - 1
                group0(last, False)
                for g in range(1, NG):
                    group(last, g, {0: [(copy_out, last, g - 1)] + ([(shift, last, g + 1)] if g < 3 else []),
                                    1: [(invert, last, g - 1)]})
                copy_out(last, 3)
                invert(last, 3)

            @block.vector
            def _(dve):
                def statistics(b):
                    if x_in is not None:
                        x_arrived(dve, b)
                    wait(dve, ln_aggr, 4 * b)
                    for t in range(TT):
                        dve.bn_stats(stats[:, t], xtile(b, t)).then_inc(ln_stats, 1)
                    for t in range(TT):
                        hold(dve, ln_stats, 4 * b + t + 1, dve_passed)
                        if t == 0:
                            hold(dve, ln_eps, b, dve_passed)
                            hold(dve, ln_done, 4 * b, dve_passed)
                        dve.bn_aggr(mean_var[:, t], stats[:, t]).then_inc(ln_aggr, 1)

                def layer_norm(b):
                    dve.wait_ge(ln_aggr, 4 * b + 4)
                    wait(dve, xt_full, 2 * b)
                    dve.wait_ge(ln_rstd, b + 1)
                    for t in range(TT):
                        dve.tensor_scalar(xn[:, t], xtile(b, t), mean_var[:, t, 0:1], rstd[:, t:t + 1],
                                          ALU.subtract, ALU.mult).then_inc(ln_done, 1)

                def xtile(b, t):
                    return c.x[:, b, t] if isinstance(b, int) else c.x[:, bass.ds(b, 1), t, :]

                def x_arrived(eng, b):
                    for s in (x_loaded[b:b + 1] if b < 1 else x_loaded[1:]) if isinstance(b, int) else ():
                        eng.wait_ge(s, 16)

                def normed(b, items):
                    for i in items:
                        dve.wait_ge(ss_rstd, 4 * b + i + 1)
                        wait(dve, part2_cut, 4 * b + i - 3)
                        dve.scalar_tensor_tensor(qk[:, i], qk_raw[:, i], gains[:, i % 2:i % 2 + 1], r_rms[:, i % 2],
                                                 ALU.mult, ALU.mult).then_inc(qk_normed, 1)

                def leftover(b, items):
                    for i in items:
                        dve.wait_ge(part0_cut, 4 * b + i + 1)
                        wait(dve, part2_cut, 4 * b + i - 3)
                        dve.tensor_tensor(rest[:, i], qk[:, i] if norm else general[:, bank[f"p{i}"]], parts[:, i, 0], ALU.subtract).then_inc(rest_done, 1)

                def maxima(b, g, tiles):
                    n = 4 * b + g
                    for i in tiles:
                        h, t = i // TT, i % TT
                        if i == 0:
                            wait(dve, mt_full, n - 1)
                        dve.wait_ge(max_full, 16 * n + i + 1)
                        w = P * (t + 1) if causal else S
                        dve.tensor_reduce(neg_max[:, g % 2, t, h:h + 1], max_ps[:, i % 2, 0:w], AX, ALU.max,
                                          negate=True).then_inc(max_read, 1)

                def shift(b, g):
                    n = 4 * b + g
                    dve.wait_ge(shift_a, n + 1)
                    wait(dve, shift_c, n - 1)
                    dve.tensor_tensor(shift_rest[:, g % 2], general[0:GH, bank[f"mt{g}"]], shift1[:, g % 2, 0],
                                      ALU.subtract).then_inc(shift_r, 1)

                def spread(b, g):
                    n = 4 * b + g
                    hold(dve, o_copied, n + 1, dve_passed)
                    dve.stream_shuffle(denom[:, g % 2], o_raw[:, g % 2], mask=[HD + d % HD for d in range(32)]).then_inc(denom_done, 1)

                def refine(b, g):
                    n = 4 * b + g
                    dve.wait_ge(guess_done, n + 1)
                    dve.scalar_tensor_tensor(residue[:], denom[:, g % 2], -1.0, r_denom[:, g % 2], ALU.mult, ALU.mult).then_inc(residue_done, 1)
                    dve.wait_ge(residue_done, n + 1)
                    dve.scalar_tensor_tensor(r_denom[:, g % 2], residue[:], 2.0, r_denom[:, g % 2], ALU.add, ALU.mult).then_inc(recip_done, 1)

                def valued(b):
                    wait(dve, pv_done, 16 * b)
                    for t in range(2):
                        dve.wait_ge(v_full, 2 * b + t + 1)
                        dve.tensor_copy(values[:, 2 * t:2 * t + 2, :, 0:HD],
                                        general[:, bank[f"v{t}"]].rearrange("p (t h d) -> p t h d", t=2, d=HD)).then_inc(v_copied, 1)

                def add(b):
                    for t in range(2):
                        dve.wait_ge(e_full, 2 * b + t + 1)
                        dst = c.x[:, b, 2 * t:2 * t + 2] if isinstance(b, int) else c.x[:, bass.ds(b, 1), 2 * t:2 * t + 2, :]
                        dve.tensor_tensor(dst, general[:, bank[f"e{t}"]].rearrange("p (t d) -> p t d", t=2), dst, ALU.add).then_inc(x_done, 1)

                def group(b, g, nxt, turned, behind=(), then=(), later=()):
                    def some(tiles):
                        if nxt is not None:
                            maxima(*nxt, tiles)

                    some(range(2))
                    for work, *of in behind:
                        work(*of)
                    some(range(2, 5))
                    if turned is not None:
                        shift(*turned)
                    if g >= 2 or (g == 1 and isinstance(b, int) and b == B - 1):
                        spread(b, g - 1)
                    for work, *of in then:
                        work(*of)
                    some(range(5, 9))
                    for work, *of in later:
                        work(*of)
                    if g >= 1:
                        refine(b, g - 1)
                    some(range(9, 16))

                def group0(b, more):
                    first = isinstance(b, int) and b == 0
                    group(b, 0, (b, 2), (b, 1), [(statistics, b + 1)] if more else [], [(layer_norm, b + 1)] if more else [],
                          [] if first else [(refine, b - 1, 3)])

                dve.wait_ge(ready, 3 if norm else 2)
                statistics(0)
                layer_norm(0)
                if norm:
                    normed(0, ITEMS)
                leftover(0, ITEMS)
                valued(0)
                maxima(0, 0, range(16))
                maxima(0, 1, range(16))
                shift(0, 0)

                def sequence(b):
                    group0(b, True)
                    spread(b, 0)
                    if norm:
                        normed(b + 1, (0, 1))
                    else:
                        leftover(b + 1, ITEMS)
                    group(b, 1, (b, 3), (b, 2), [(normed, b + 1, (2, 3)), (leftover, b + 1, (0, 1))] if norm else (),
                          (), [(leftover, b + 1, (2, 3))] if norm else ())
                    if not isinstance(b, int) or b > 0:
                        add(b - 1)
                    group(b, 2, (b + 1, 0), (b, 3))
                    group(b, 3, (b + 1, 1), (b + 1, 0))
                    spread(b, 3)
                    valued(b + 1)

                sequence(0)
                with dve.Fori(1, B - 1) as b:
                    sequence(b)
                last = B - 1
                group0(last, False)
                group(last, 1, (last, 3), (last, 2))
                add(last - 1)
                group(last, 2, None, (last, 3))
                group(last, 3, None, None)
                spread(last, 3)
                refine(last, 3)
                add(last)
                dve.wait_ge(x_done, 2 * B)

            @block.tensor
            def _(pe):
                freed = qk_copied if norm else rest_done

                def transposes(b):
                    for k in range(KD):
                        pe.wait_ge(ln_done, 4 * b + 4)
                        if k == 0:
                            wait(pe, v_copied, 2 * b)
                        else:
                            wait(pe, shift_r, 4 * b - 2)
                        for t in range(TT):
                            last = pe.transpose(general[:, bank[f"xt{k}"], P * t:P * t + P], xn[:, t, P * k:P * k + P], c.ident[:])
                        last.then_inc(xt_full, 1)

                def project(b, i, *free):
                    wait(pe, *free)
                    for k in range(KD):
                        last = pe.matmul(general[:, bank[f"p{i}"]], wqk[:, k, COLUMNS[i]:COLUMNS[i] + P], xnT[:, k],
                                         start=(k == 0), stop=(k == KD - 1))
                    last.then_inc(qk_full, 1)

                def sum_squares(b, i, *free):
                    wait(pe, *free)
                    pe.wait_ge(sq_done, 4 * b + i + 1)
                    pe.matmul(general[:, bank[f"s{i}"]], c.head_ones[:], squares[:, i % 2], start=True, stop=True).then_inc(ss_full, 1)

                def first_half(b):
                    project(b, 0, xt_copied, 2 * b + 2)
                    project(b, 1, xt_copied, 2 * b + 2)

                def second_half(b):
                    project(b, 2, freed, 4 * b + 1)
                    if norm:
                        sum_squares(b, 0, freed, 4 * b + 2)
                        project(b, 3, freed, 4 * b + 3)
                        sum_squares(b, 1, ss_log, 4 * b + 1)
                        sum_squares(b, 2, freed, 4 * b + 4)
                        sum_squares(b, 3, ss_log, 4 * b + 2)
                    else:
                        project(b, 3, freed, 4 * b + 2)

                def value_rows(b, t, *free):
                    wait(pe, *free)
                    for t2 in range(2):
                        tok = P * (2 * t + t2)
                        for k in range(KD):
                            last = pe.matmul(general[:, bank[f"v{t}"], D * t2:D * t2 + D], xnT[:, k, tok:tok + P], wv[:, k],
                                             start=(k == 0), stop=(k == KD - 1))
                    last.then_inc(v_full, 1)

                def max_tile(b, g, i):
                    n = 16 * (4 * b + g) + i
                    h, t = GH * g + i // TT, i % TT
                    if i == 0:
                        pe.wait_ge(stacked[g], 192 * b + 192)
                    wait(pe, max_read, n - 1)
                    w = P * (t + 1) if causal else S
                    last = pe.matmul(max_ps[:, i % 2, 0:w], q_stack[0:ROWS, h, P * t:P * t + P], k_stack[0:ROWS, h, 0:w],
                                     start=True, stop=not causal)
                    if causal:
                        last = pe.matmul(max_ps[:, i % 2, w - P:w], c.ident_b[:], c.causal_qk[:], start=False, stop=True)
                    last.then_inc(max_full, 1)

                def turn_maxima(b, g, *free):
                    wait(pe, *free)
                    pe.wait_ge(max_read, 16 * (4 * b + g) + 16)
                    for t in range(TT):
                        last = pe.transpose(general[0:GH, bank[f"mt{g}"], P * t:P * t + P], neg_max[:, g % 2, t], c.ident[:])
                    last.then_inc(mt_full, 1)

                def with_values(b, g, j):
                    n = 4 * b + g
                    pe.wait_ge(exp_done, 16 * n + 4 * j + 4)
                    if j == 0:
                        pe.wait_ge(v_copied, 2 * b + 2)
                        wait(pe, o_copied, n)
                    w = width(j)
                    for h in range(GH):
                        last = pe.matmul(out_ps[32 * h:32 * h + 32, S - w:S], values[:, j, GH * g + h], probs[:, (4 * j + h) % 8, 0:w],
                                         start=(j == 0), stop=(j == TT - 1), tile_position=(0, 32 * h))
                    last.then_inc(pv_done, 1)

                def group(b, g, nxt, turn, carried=None, fill={}):
                    n = 4 * b + g
                    pe.wait_ge(shift_placed[g], 48 * b + 48)
                    for j in range(TT):
                        w = width(j)
                        for h in range(GH):
                            i = 4 * j + h
                            wait(pe, exp_done, 16 * n + (i - 2 if i >= 3 else (0, -2, -1)[i]))
                            head = GH * g + h
                            last = pe.matmul(score_ps[:, i % 3, 0:w], k_stack[0:KROWS, head, P * j:P * j + P],
                                             q_stack[0:KROWS, head, S - w:S], start=True, stop=not causal)
                            if causal:
                                last = pe.matmul(score_ps[:, i % 3, 0:P], c.ident_b[:], c.causal_kq[:], start=False, stop=True)
                            last.then_inc(score_full, 1)
                            if nxt is not None:
                                max_tile(*nxt, i)
                        if j == 0 and carried is not None:
                            with_values(*carried, TT - 1)
                        if j == 0 and turn is not None:
                            turn_maxima(*turn)
                        if j >= 1:
                            with_values(b, g, j - 1)
                        for work, *of in fill.get(j, ()):
                            work(*of)

                def output(b, t, *free):
                    wait(pe, *free)
                    pe.wait_ge(o_done, 4 * b + 4)
                    for t2 in range(2):
                        tok = P * (2 * t + t2)
                        for g in range(NG):
                            last = pe.matmul(general[:, bank[f"e{t}"], D * t2:D * t2 + D], o_norm[:, g, tok:tok + P], wo[:, g],
                                             start=(g == 0), stop=(g == NG - 1))
                    last.then_inc(e_full, 1)

                pe.wait_ge(loaded, 16 * (5 if norm else 3))
                pe.wait_ge(scaled, 1)
                pe.wait_ge(ready, 3 if norm else 2)
                transposes(0)
                first_half(0)
                second_half(0)
                value_rows(0, 0, ss_log if norm else freed, 4)
                value_rows(0, 1, ss_log if norm else freed, 4)
                for g in range(2):
                    for i in range(16):
                        max_tile(0, g, i)
                turn_maxima(0, 0, v_copied, 2)
                pe.wait_ge(shift_r, 1)

                left = ((ss_log, 3), (ss_log, 4)) if norm else ((freed, 3), (freed, 4))

                def group0(b, more):
                    group(b, 0, (b, 2), (b, 1, v_copied, 2 * b + 1), None, {1: [(transposes, b + 1)], 2: [(first_half, b + 1)]} if more else {})

                def sequence(b):
                    first = isinstance(b, int) and b == 0
                    group0(b, True)
                    with_values(b, 0, TT - 1)
                    second_half(b + 1)
                    projected = [(left[i][0], 4 * b + 4 + left[i][1]) for i in range(2)]
                    group(b, 1, (b, 3), (b, 2, *projected[0]), None,
                          {} if first else {2: [(output, b - 1, 0, *projected[1])], 3: [(output, b - 1, 1, shift_r, 4 * b + 3)]})
                    group(b, 2, (b + 1, 0), (b, 3, *(projected[1] if first else (x_done, 2 * b - 1))), (b, 1))
                    group(b, 3, (b + 1, 1), (b + 1, 0, *((shift_r, 3) if first else (x_done, 2 * b))), (b, 2),
                          {1: [(value_rows, b + 1, 0, shift_r, 4 * b + 4)], 2: [(value_rows, b + 1, 1, shift_r, 4 * b + 5)]})
                    with_values(b, 3, TT - 1)

                sequence(0)
                with pe.Fori(1, B - 1) as b:
                    sequence(b)
                last = B - 1
                group0(last, False)
                group(last, 1, (last, 3), (last, 2, v_copied, 2 * last + 2), (last, 0),
                      {2: [(output, last - 1, 0, shift_r, 4 * last + 2)], 3: [(output, last - 1, 1, shift_r, 4 * last + 3)]})
                group(last, 2, None, (last, 3, x_done, 2 * last - 1), (last, 1))
                group(last, 3, None, None, (last, 2))
                with_values(last, 3, TT - 1)
                output(last, 0, shift_r, 4 * last + 4)
                output(last, 1, x_done, 2 * last)

    nc.clear_and_free_semaphores(made)
    nc.all_engine_barrier()


def cross_attention(nc, c, name, w_q, w_k, w_v, w_o, bias_q, bias_k, bias_v, ctx_t, ctx_twice, mask_t=None):
    masked = mask_t is not None
    made = []
    S2 = ctx_t.shape[1] // B
    NP = H // 2

    def sem(what):
        s = nc.alloc_semaphore(f"{name}_{what}")
        made.append(s)
        return s

    with ExitStack() as ctx:
        def sb(what, shape, dt=F32):
            return ctx.enter_context(nc.sbuf_tensor(f"{name}_{what}", shape, dt))

        def ps(what, shape, dt=F32):
            return ctx.enter_context(nc.psum_tensor(f"{name}_{what}", shape, dt))

        wq, wk, wv = (sb(what, [P, KD, D]) for what in ("wq", "wk", "wv"))
        wo = sb("wo", [P, NG, D])
        bias = sb("bias", [P, 4])
        bias_row = sb("bias_row", [P, D])
        ctx_all = sb("ctx_all", [P, KD, S])
        ctx_one = sb("ctx_one", [P, KD, P])
        stats = sb("stats", [P, TT, 6])
        mean_var = sb("mean_var", [P, TT, 2])
        var_eps = sb("var_eps", [P, TT])
        rstd = sb("rstd", [P, TT])
        xn = sb("xn", [P, TT, D])
        xnT = sb("xnT", [P, KD, S])
        parts = sb("parts", [P, 2, 3, S], BF16)
        rest = sb("rest", [P, 2, S])
        q_stack = sb("q_stack", [P, 2, H, S], BF16)
        k_stack = sb("k_stack", [P, H, B * S2], BF16)
        k_one = sb("k_one", [P, H, S2], BF16)
        values = sb("values", [P, NP, 64])
        neg_max = sb("neg_max", [P, TT, H])
        shift1 = sb("shift1", [H, 3, S], BF16)
        shift_rest = sb("shift_rest", [H, S])
        probs = sb("probs", [P, 4, S])
        o_raw, denom, r_denom, o_norm = (sb(what, [P, NG, S]) for what in ("o_raw", "denom", "r_denom", "o_norm"))
        log_sum, residue = sb("log_sum", [P, S]), sb("residue", [P, S])
        if masked:
            mask_raw = sb("mask_raw", [P, S])
            mask_rest = sb("mask_rest", [P, S])
            mask12 = sb("mask12", [P, 2, S], BF16)
            mask3 = sb("mask3", [P, 2, S], BF16)
            spread_keys = sb("spread_keys", [P, S], BF16)
        scratch = nc.dram_tensor(f"{name}_parts_dram", [2, P, 3, S], BF16).ap()

        general = ps("general", [P, 2, S])
        max_ps = ps("max_ps", [P, 2, S])
        score_ps = ps("score_ps", [P, 2, S])
        out_ps = ps("out_ps", [P, 2, S])

        ready, scaled = sem("ready"), sem("scaled")
        pool_passed, dve_passed, sp_passed = sem("pool_passed"), sem("dve_passed"), sem("sp_passed")
        loaded, ctx_loaded = sem("loaded"), sem("ctx_loaded")
        ln_stats, ln_aggr, ln_eps, ln_rstd, ln_done = (sem(s) for s in ("ln_stats", "ln_aggr", "ln_eps", "ln_rstd", "ln_done"))
        xt_full, xt_copied, qk_full = sem("xt_full"), sem("xt_copied"), sem("qk_full")
        part0_cut, rest_done, part1_cut, part2_cut = (sem(s) for s in ("part0_cut", "rest_done", "part1_cut", "part2_cut"))
        parts_stored, k_stacked, stacked, k_copied = (sem(s) for s in ("parts_stored", "k_stacked", "stacked", "k_copied"))
        max_full, max_read = sem("max_full"), sem("max_read")
        mt_full, shift_a, shift_r, shift_b, shift_c, shift_placed = (
            sem(s) for s in ("mt_full", "shift_a", "shift_r", "shift_b", "shift_c", "shift_placed"))
        score_full, exp_done, pv_done = sem("score_full"), sem("exp_done"), sem("pv_done")
        o_copied, denom_done, log_done, guess_done, residue_done, recip_done, o_done = (
            sem(s) for s in ("o_copied", "denom_done", "log_done", "guess_done", "residue_done", "recip_done", "o_done"))
        v_full, v_copied, e_full, x_done = sem("v_full"), sem("v_copied"), sem("e_full"), sem("x_done")
        if masked:
            mask_loaded, mask_a, mask_r, mask_b, mask_c = (sem(s) for s in ("mask_loaded", "mask_a", "mask_r", "mask_b", "mask_c"))
        constants = 8 if masked else 4

        order = ["xt0", "xt1", "q0", "q1", "v", "mt", "e0", "e1"]
        bank = {what: n % 2 for n, what in enumerate(order)}

        def loop(eng, sequence):
            sequence(0, 0)
            with eng.Fori(0, (B - 2) // 2) as i:
                sequence(2 * i + 1, 1)
                sequence(2 * i + 2, 0)

        def loop_apart(eng, sequence):
            sequence(0, 0, True)
            with eng.Fori(0, (B - 4) // 2) as i:
                sequence(2 * i + 1, 1, True)
                sequence(2 * i + 2, 0, True)
            sequence(B - 3, 1, True)
            sequence(B - 2, 0, False)

        with nc.Block() as block:
            @block.sync
            def _(sp):
                sp.dma_start(ctx_all[:], ctx_t.rearrange("(k p) n -> p k n", p=P)).then_inc(loaded, 16)
                for dst, src in ((wk, w_k), (wq, w_q), (wv, w_v)):
                    sp.dma_start(dst[:], src.rearrange("(k p) n -> p k n", p=P)).then_inc(loaded, 16)
                sp.dma_start(bias[:, 0:2], bias_k).then_inc(loaded, 16)
                sp.dma_start(bias[:, 2:4], bias_q).then_inc(loaded, 16)
                sp.dma_start(bias_row[:], bias_v).then_inc(loaded, 16)
                sp.dma_start(wo[:], w_o.rearrange("g p n -> p g n")).then_inc(loaded, 16)

                def load(b):
                    hold(sp, v_full, b, sp_passed)
                    src = ctx_twice[b] if isinstance(b, int) else ctx_twice[bass.ds(b, 1)].rearrange("o k p n -> (o k) p n")
                    sp.dma_start(ctx_one[:], src.rearrange("k p n -> p k n")).then_inc(ctx_loaded, 16)
                    if masked:
                        hold(sp, mask_r, b, sp_passed)
                        hold(sp, mask_a, b, sp_passed)
                        src = mask_t[b] if isinstance(b, int) else mask_t[bass.ds(b, 1)].rearrange("o k s -> (o k) s")
                        for half in range(2):
                            sp.dma_start(mask_raw[S2 * half:S2 * half + S2, :], src).then_inc(mask_loaded, 16)

                def store_parts(s):
                    for i in range(2):
                        hold(sp, part2_cut, 2 * s + i + 1, sp_passed)
                        if not isinstance(s, int) or s > 0:
                            sp.wait_ge(k_stacked, 192)
                            hold(sp, stacked, 192 * (s - 1), sp_passed)
                        sp.dma_start(scratch[i], parts[:, i]).then_inc(parts_stored, 16)
                    hold(sp, parts_stored, 32 * s + 32, sp_passed)

                def stack(dst, which, signal):
                    for half in range(2):
                        for r, part in enumerate(which):
                            sp.dma_start(dst[HD * r:HD * r + HD, 8 * half:8 * half + 8, :],
                                         scratch[half, :, part, :].rearrange("(h d) t -> d h t", d=HD)).then_inc(signal, 16)

                def queries(b, slot):
                    store_parts(b + 1)
                    hold(sp, score_full, NP * (b - 1), sp_passed)
                    stack(q_stack[:, slot], Q_PART, stacked)

                def place_shift(b, slot):
                    hold(sp, shift_c, b + 1, sp_passed)
                    for i in range(3):
                        sp.dma_start(q_stack[SHIFT + i:SHIFT + i + 1, slot, :, :], shift1[:, i, :]).then_inc(shift_placed, 16)

                load(0)
                store_parts(0)
                stack(k_stack, K_PART, k_stacked)
                queries(0, 0)
                place_shift(0, 0)

                def sequence(b, slot):
                    load(b + 1)
                    queries(b + 1, 1 - slot)
                    place_shift(b + 1, 1 - slot)

                loop(sp, sequence)

            @block.gpsimd
            def _(pool):
                n = 0

                def constant(instruction):
                    nonlocal n
                    n += 1
                    instruction.then_inc(ready, 1)
                    pool.wait_ge(ready, n)

                constant(pool.memset(values[:], 0.0))
                constant(pool.memset(values[0:S2, :, HD:2 * HD], 1.0))
                constant(pool.memset(values[S2:P, :, 3 * HD:4 * HD], 1.0))
                constant(pool.memset(k_stack[SHIFT:KROWS], 1.0))
                if masked:
                    constant(pool.memset(mask3[:], 0.0))
                    constant(pool.memset(spread_keys[:], 0.0))
                    view = spread_keys[:].rearrange("p (h k) -> p h k", k=S2)
                    for base in (0, -S2):
                        constant(pool.affine_select(out=view, in_=view, compare_op=ALU.not_equal, fill=1.0, base=base,
                                                    pattern=[[0, S // S2], [-1, S2]], channel_multiplier=1))
                pool.wait_ge(loaded, 16 * 8)
                pool.tensor_scalar(wq[:], wq[:], HD ** -0.5, None, ALU.mult).then_inc(scaled, 1)
                pool.tensor_scalar(bias[:, 2:4], bias[:, 2:4], HD ** -0.5, None, ALU.mult).then_inc(scaled, 1)

                def layer_norm(b):
                    hold(pool, ln_aggr, 4 * b + 4, pool_passed)
                    pool.tensor_scalar(var_eps[:], mean_var[:, :, 1], 1e-5, None, ALU.add).then_inc(ln_eps, 1)
                    pool.wait_ge(ln_eps, b + 1)
                    pool.tensor_tensor(rstd[:], var_eps[:], c.minus_half[:, 0:TT], ALU.pow).then_inc(ln_rstd, 1)

                def cut(s):
                    for i in range(2):
                        pool.wait_ge(part1_cut, 2 * s + i + 1)
                        pool.tensor_tensor(parts[:, i, 2], rest[:, i], parts[:, i, 1], ALU.subtract).then_inc(part2_cut, 1)

                def shift(b):
                    hold(pool, shift_r, b + 1, pool_passed)
                    hold(pool, shift_placed, 48 * b, pool_passed)
                    pool.tensor_copy(shift1[:, 1], shift_rest[:]).then_inc(shift_b, 1)
                    pool.wait_ge(shift_b, b + 1)
                    pool.tensor_tensor(shift1[:, 2], shift_rest[:], shift1[:, 1], ALU.subtract).then_inc(shift_c, 1)

                def normalise(b, g):
                    pool.wait_ge(recip_done, 4 * b + g + 1)
                    wait(pool, e_full, 2 * b)
                    pool.tensor_tensor(o_norm[:, g], o_raw[:, g], r_denom[:, g], ALU.mult).then_inc(o_done, 1)

                def cut_mask(b, slot):
                    pool.wait_ge(mask_a, b + 1)
                    pool.tensor_tensor(mask_rest[:], mask_raw[:], mask12[:, slot], ALU.subtract).then_inc(mask_r, 1)
                    pool.wait_ge(mask_b, b + 1)
                    pool.tensor_tensor(mask3[S2:P, slot], mask_rest[S2:P], mask12[S2:P, slot], ALU.subtract).then_inc(mask_c, 1)
                    hold(pool, mask_c, b + 1, pool_passed)

                layer_norm(0)
                cut(0)
                cut(1)
                if masked:
                    cut_mask(0, 0)
                layer_norm(1)
                shift(0)

                def sequence(b, slot, more):
                    cut(b + 2)
                    if masked:
                        cut_mask(b + 1, 1 - slot)
                    for g in range(NG):
                        normalise(b, g)
                    if more:
                        layer_norm(b + 2)
                    shift(b + 1)

                loop_apart(pool, sequence)
                for g in range(NG):
                    normalise(B - 1, g)

            @block.scalar
            def _(act):
                act.preload_act_table_set("natural_log_exp_and_others")

                def cut(s, column):
                    for i in range(2):
                        act.wait_ge(qk_full, 2 * s + i + 1)
                        wait(act, parts_stored, 32 * s)
                        act.activation(parts[:, i, 0], general[:, bank[f"q{i}"]], ACT.Identity, bias=bias[:, column + i:column + i + 1]).then_inc(part0_cut, 1)
                    for i in range(2):
                        act.wait_ge(rest_done, 2 * s + i + 1)
                        act.activation(parts[:, i, 1], rest[:, i], ACT.Copy).then_inc(part1_cut, 1)

                def transposed(b):
                    for k in range(KD):
                        act.wait_ge(xt_full, 2 * b + k + 1)
                        act.activation(xnT[:, k], general[:, bank[f"xt{k}"]], ACT.Copy).then_inc(xt_copied, 1)

                def cut_mask(b, slot):
                    act.wait_ge(mask_loaded, 32 * b + 32)
                    wait(act, score_full, NP * (b - 1))
                    act.activation(mask12[:, slot], mask_raw[:], ACT.Copy).then_inc(mask_a, 1)
                    act.wait_ge(mask_r, b + 1)
                    act.activation(mask12[S2:P, slot], mask_rest[S2:P], ACT.Copy).then_inc(mask_b, 1)

                def shift(b):
                    act.wait_ge(mt_full, b + 1)
                    wait(act, shift_placed, 48 * b)
                    act.activation(shift1[:, 0], general[0:H, bank["mt"]], ACT.Copy).then_inc(shift_a, 1)

                def exponentials(b, pairs):
                    for p in pairs:
                        act.wait_ge(score_full, NP * b + p + 1)
                        wait(act, pv_done, NP * b + p - 3)
                        act.activation(probs[:, p % 4], score_ps[:, p % 2], ACT.Exp).then_inc(exp_done, 1)

                def copy_out(b, g):
                    act.wait_ge(pv_done, NP * b + 2 * g + 2)
                    wait(act, o_done, 4 * b + g - 3)
                    act.activation(o_raw[:, g], out_ps[:, g % 2], ACT.Copy).then_inc(o_copied, 1)

                def invert(b, g):
                    n = 4 * b + g
                    act.wait_ge(denom_done, n + 1)
                    wait(act, guess_done, n)
                    act.activation(log_sum[:], denom[:, g], ACT.Ln).then_inc(log_done, 1)
                    act.wait_ge(log_done, n + 1)
                    act.activation(r_denom[:, g], log_sum[:], ACT.Exp, scale=-1.0).then_inc(guess_done, 1)

                act.wait_ge(loaded, 16 * 8)
                act.wait_ge(scaled, 2)
                cut(0, 0)
                transposed(0)
                cut(1, 2)
                if masked:
                    cut_mask(0, 0)
                shift(0)

                def attend(b):
                    exponentials(b, range(4))
                    copy_out(b, 0)
                    exponentials(b, (4, 5))
                    copy_out(b, 1)
                    invert(b, 0)
                    exponentials(b, (6, 7))
                    copy_out(b, 2)
                    invert(b, 1)
                    copy_out(b, 3)
                    invert(b, 2)
                    invert(b, 3)

                def sequence(b, slot):
                    transposed(b + 1)
                    cut(b + 2, 2)
                    if masked:
                        cut_mask(b + 1, 1 - slot)
                    attend(b)
                    shift(b + 1)

                loop(act, sequence)
                attend(B - 1)

            @block.vector
            def _(dve):
                def xtile(b, t):
                    return c.x[:, b, t] if isinstance(b, int) else c.x[:, bass.ds(b, 1), t, :]

                def statistics(b):
                    wait(dve, ln_aggr, 4 * b)
                    for t in range(TT):
                        dve.bn_stats(stats[:, t], xtile(b, t)).then_inc(ln_stats, 1)
                    for t in range(TT):
                        hold(dve, ln_stats, 4 * b + t + 1, dve_passed)
                        if t == 0:
                            hold(dve, ln_eps, b, dve_passed)
                            hold(dve, ln_done, 4 * b, dve_passed)
                        dve.bn_aggr(mean_var[:, t], stats[:, t]).then_inc(ln_aggr, 1)

                def layer_norm(b):
                    dve.wait_ge(ln_aggr, 4 * b + 4)
                    wait(dve, xt_full, 2 * b)
                    dve.wait_ge(ln_rstd, b + 1)
                    for t in range(TT):
                        dve.tensor_scalar(xn[:, t], xtile(b, t), mean_var[:, t, 0:1], rstd[:, t:t + 1],
                                          ALU.subtract, ALU.mult).then_inc(ln_done, 1)

                def leftover(s, column):
                    for i in range(2):
                        dve.wait_ge(part0_cut, 2 * s + i + 1)
                        wait(dve, part2_cut, 2 * s + i - 1)
                        dve.scalar_tensor_tensor(rest[:, i], general[:, bank[f"q{i}"]], bias[:, column + i:column + i + 1],
                                                 parts[:, i, 0], ALU.add, ALU.subtract).then_inc(rest_done, 1)

                def keys(b):
                    wait(dve, score_full, NP * b)
                    src = k_stack[0:KROWS, :, S2 * b:S2 * b + S2] if isinstance(b, int) else k_stack[0:KROWS, :, bass.ds(S2 * b, S2)]
                    dve.tensor_copy(k_one[0:KROWS], src).then_inc(k_copied, 1)

                def valued(b):
                    dve.wait_ge(v_full, b + 1)
                    for half in range(2):
                        rows = slice(S2 * half, S2 * half + S2)
                        heads = lambda a: a.rearrange("p (h two d) -> p h two d", two=2, d=HD)[:, :, half, :]
                        dve.tensor_tensor(values[rows, :, 2 * HD * half:2 * HD * half + HD], heads(general[rows, bank["v"], 0:D]),
                                          heads(bias_row[rows]), ALU.add).then_inc(v_copied, 1)

                def maxima(b, tiles):
                    wait(dve, mt_full, b)
                    for n in tiles:
                        t, half = n // 2, n % 2
                        dve.wait_ge(max_full, 8 * b + n + 1)
                        dve.tensor_reduce(neg_max[:, t, 8 * half:8 * half + 8], max_ps[:, half].rearrange("p (h k) -> p h k", k=S2),
                                          AX, ALU.max, negate=True).then_inc(max_read, 1)

                def shift(b):
                    dve.wait_ge(shift_a, b + 1)
                    wait(dve, shift_c, b)
                    dve.tensor_tensor(shift_rest[:], general[0:H, bank["mt"]], shift1[:, 0], ALU.subtract).then_inc(shift_r, 1)

                def spread(b, g):
                    hold(dve, o_copied, 4 * b + g + 1, dve_passed)
                    dve.stream_shuffle(denom[:, g], o_raw[:, g], mask=[HD + d % HD for d in range(32)]).then_inc(denom_done, 1)

                def refine(b, g):
                    n = 4 * b + g
                    dve.wait_ge(guess_done, n + 1)
                    wait(dve, recip_done, n)
                    dve.scalar_tensor_tensor(residue[:], denom[:, g], -1.0, r_denom[:, g], ALU.mult, ALU.mult).then_inc(residue_done, 1)
                    dve.wait_ge(residue_done, n + 1)
                    dve.scalar_tensor_tensor(r_denom[:, g], residue[:], 2.0, r_denom[:, g], ALU.add, ALU.mult).then_inc(recip_done, 1)

                def add(b):
                    for t in range(2):
                        dve.wait_ge(e_full, 2 * b + t + 1)
                        dst = c.x[:, b, 2 * t:2 * t + 2] if isinstance(b, int) else c.x[:, bass.ds(b, 1), 2 * t:2 * t + 2, :]
                        dve.tensor_tensor(dst, general[:, bank[f"e{t}"]].rearrange("p (t d) -> p t d", t=2), dst, ALU.add).then_inc(x_done, 1)

                def attended(b):
                    spread(b, 0)
                    spread(b, 1)
                    refine(b, 0)
                    spread(b, 2)
                    refine(b, 1)
                    spread(b, 3)

                dve.wait_ge(ready, constants)
                dve.wait_ge(loaded, 16 * 8)
                dve.wait_ge(scaled, 2)
                statistics(0)
                layer_norm(0)
                leftover(0, 0)
                leftover(1, 2)
                statistics(1)
                dve.wait_ge(k_stacked, 192)
                valued(0)
                keys(0)
                layer_norm(1)
                maxima(0, range(8))
                shift(0)

                def sequence(b, slot, more):
                    leftover(b + 2, 2)
                    attended(b)
                    keys(b + 1)
                    valued(b + 1)
                    refine(b, 2)
                    maxima(b + 1, range(3))
                    refine(b, 3)
                    maxima(b + 1, range(3, 8))
                    if more:
                        statistics(b + 2)
                    shift(b + 1)
                    if more:
                        layer_norm(b + 2)
                    add(b)

                loop_apart(dve, sequence)
                attended(B - 1)
                refine(B - 1, 2)
                refine(B - 1, 3)
                add(B - 1)
                dve.wait_ge(x_done, 2 * B)

            @block.tensor
            def _(pe):
                def project(item, weights, source, free, *value):
                    i = item
                    wait(pe, free, *value)
                    for k in range(KD):
                        last = pe.matmul(general[:, bank[f"q{i}"]], weights[:, k, P * i:P * i + P], source[:, k],
                                         start=(k == 0), stop=(k == KD - 1))
                    last.then_inc(qk_full, 1)

                def queries(b, last_x):
                    for k in range(KD):
                        pe.wait_ge(ln_done, 4 * b + 4)
                        wait(pe, *last_x[k])
                        for t in range(TT):
                            last = pe.transpose(general[:, bank[f"xt{k}"], P * t:P * t + P], xn[:, t, P * k:P * k + P], c.ident[:])
                        last.then_inc(xt_full, 1)
                    for i in range(2):
                        project(i, wq, xnT, xt_copied, 2 * b + 2)

                def value_rows(b):
                    pe.wait_ge(ctx_loaded, 16 * b + 16)
                    pe.wait_ge(rest_done, 2 * b + 3)
                    for k in range(KD):
                        last = pe.matmul(general[:, bank["v"], 0:D], ctx_one[:, k], wv[:, k], start=(k == 0), stop=(k == KD - 1))
                    last.then_inc(v_full, 1)

                def maxima(b, slot):
                    pe.wait_ge(stacked, 192 * b + 192)
                    pe.wait_ge(k_copied, b + 1)
                    if masked:
                        pe.wait_ge(mask_c, b + 1)
                    for n in range(8):
                        t, half = n // 2, n % 2
                        tok = slice(P * t, P * t + P)
                        wait(pe, max_read, 8 * b + n - 1)
                        for h in range(8):
                            last = pe.matmul(max_ps[:, half, S2 * h:S2 * h + S2], q_stack[0:ROWS, slot, 8 * half + h, tok],
                                             k_one[0:ROWS, 8 * half + h], start=(h == 0 or not masked), stop=not masked, skip_group_check=masked)
                        if masked:
                            pe.matmul(max_ps[:, half], mask12[:, slot, tok], spread_keys[:], start=False, stop=False, skip_group_check=True)
                            last = pe.matmul(max_ps[:, half], mask3[:, slot, tok], spread_keys[:], start=False, stop=True, skip_group_check=True)
                        last.then_inc(max_full, 1)
                    pe.wait_ge(rest_done, 2 * b + 4)
                    pe.wait_ge(max_read, 8 * b + 8)
                    for t in range(TT):
                        last = pe.transpose(general[0:H, bank["mt"], P * t:P * t + P], neg_max[:, t], c.ident[:])
                    last.then_inc(mt_full, 1)

                def scores(b, slot, p):
                    wait(pe, exp_done, NP * b + p - 1)
                    for half in range(2):
                        rows = slice(S2 * half, S2 * half + S2)
                        last = pe.matmul(score_ps[rows, p % 2], k_one[0:KROWS, 2 * p + half], q_stack[0:KROWS, slot, 2 * p + half],
                                         start=True, stop=not masked, tile_position=(0, S2 * half), skip_group_check=masked)
                    if masked:
                        pe.matmul(score_ps[:, p % 2], spread_keys[:, 0:P], mask12[:, slot], start=False, stop=False, skip_group_check=True)
                        last = pe.matmul(score_ps[:, p % 2], spread_keys[:, 0:P], mask3[:, slot], start=False, stop=True, skip_group_check=True)
                    last.then_inc(score_full, 1)

                def with_values(b, p):
                    pe.wait_ge(exp_done, NP * b + p + 1)
                    g, half = p // 2, p % 2
                    if half == 0:
                        wait(pe, o_copied, 4 * b + g - 1)
                    if p == 0:
                        pe.wait_ge(v_copied, 2 * b + 2)
                    pe.matmul(out_ps[64 * half:64 * half + 64, g % 2], values[:, p], probs[:, p % 4],
                              start=True, stop=True, tile_position=(0, 64 * half)).then_inc(pv_done, 1)

                def attend(b, slot):
                    pe.wait_ge(shift_placed, 48 * b + 48)
                    for p in range(NP + 2):
                        if p < NP:
                            scores(b, slot, p)
                        if p >= 2:
                            with_values(b, p - 2)

                def output(b, last_of_bank):
                    pe.wait_ge(o_done, 4 * b + 4)
                    for t in range(2):
                        wait(pe, *last_of_bank[t])
                        for t2 in range(2):
                            tok = P * (2 * t + t2)
                            for g in range(NG):
                                last = pe.matmul(general[:, bank[f"e{t}"], D * t2:D * t2 + D], o_norm[:, g, tok:tok + P], wo[:, g],
                                                 start=(g == 0), stop=(g == NG - 1))
                        last.then_inc(e_full, 1)

                pe.wait_ge(loaded, 16 * 8)
                pe.wait_ge(ready, constants)
                pe.wait_ge(scaled, 2)
                for i in range(2):
                    project(i, wk, ctx_all, loaded, 16)
                queries(0, ((rest_done, 1), (rest_done, 2)))
                value_rows(0)
                maxima(0, 0)

                def sequence(b, slot):
                    if isinstance(b, int) and b == 0:
                        queries(1, ((v_copied, 2), (shift_r, 1)))
                    else:
                        queries(b + 1, ((x_done, 2 * b - 1), (x_done, 2 * b)))
                    attend(b, slot)
                    value_rows(b + 1)
                    maxima(b + 1, 1 - slot)
                    output(b, ((v_copied, 2 * b + 4), (shift_r, b + 2)))

                loop(pe, sequence)
                attend(B - 1, 1)
                output(B - 1, ((x_done, 2 * B - 3), (x_done, 2 * B - 2)))

    nc.clear_and_free_semaphores(made)
    nc.all_engine_barrier()


def mixture_of_depths(nc, c, w_router, w_qkv, w_o, gain1, gain2, w_1, w_2, w_3):
    made = []
    R = P
    SB = 2
    BS = B // SB
    F = w_1.shape[1]
    FT = -(-F // P)
    rows_of = lambda f: min(P, F - P * f)
    UNITS = BS * NG

    def sem(what):
        s = nc.alloc_semaphore(f"depths_{what}")
        made.append(s)
        return s

    with ExitStack() as ctx:
        def allocate(to):
            return (lambda what, shape, dt=F32: to.enter_context(nc.sbuf_tensor(f"depths_{what}", shape, dt)),
                    lambda what, shape, dt=F32: to.enter_context(nc.psum_tensor(f"depths_{what}", shape, dt)))

        sb, ps = allocate(ctx)
        wqkv = sb("wqkv", [P, KD, 3 * D])
        wo = sb("wo", [P, NG, D])
        gains = sb("gains", [P, 2, KD])
        w1, w2 = sb("w1", [P, KD, F]), sb("w2", [P, KD, F])
        w3 = sb("w3", [P, FT, D])
        back = sb("back", [P, B, S])
        chosen = sb("chosen", [P, B, D])
        delta = sb("delta", [P, B, D])
        mean_sq = sb("mean_sq", [P, 2, B])
        r_rms = sb("r_rms", [P, 2, B])

        loaded, scaled = sem("loaded"), sem("scaled")
        sq_done = sem("sq_done")

        with ExitStack() as inner:
            sb1, ps1 = allocate(inner)
            router = sb1("router", [P, D])
            column = sb1("column", [P, P])
            before = sb1("before", [P, P])
            stats = sb1("stats", [P, TT, 6])
            mean_var = sb1("mean_var", [P, TT, 2])
            var_eps = sb1("var_eps", [P, TT])
            rstd = sb1("rstd", [P, TT])
            h = sb1("h", [P, 2, TT, D])
            product = sb1("product", [P, TT, D])
            score = sb1("score", [P, 2, TT])
            above = sb1("above", [P, TT, S], BF16)
            tied = sb1("tied", [P, TT, P], BF16)
            counts = sb1("counts", [P, TT, 3])
            rank = sb1("rank", [P, TT])
            pick = sb1("pick", [P, 2, TT, R])
            squares = sb1("squares", [P, D])
            score_rows = ps1("score_rows", [P, 2, S])
            back_ps = ps1("back_ps", [P, 2, S])
            chosen_ps = ps1("chosen_ps", [P, 2, S])

            ready, router_loaded = sem("ready"), sem("router_loaded")
            pool_passed, dve_passed = sem("pool_passed"), sem("dve_passed")
            ln_stats, ln_aggr, ln_eps, ln_rstd, ln_done = (sem(s) for s in ("ln_stats", "ln_aggr", "ln_eps", "ln_rstd", "ln_done"))
            scored, rows_full, counted, ranked, picked = (sem(s) for s in ("scored", "rows_full", "counted", "ranked", "picked"))
            h_added, back_full, back_copied, chosen_full, chosen_copied = (
                sem(s) for s in ("h_added", "back_full", "back_copied", "chosen_full", "chosen_copied"))
            COUNTS = 3 * TT - 1

            def pairs(eng, one):
                one(0, 0)
                one(1, 1)
                with eng.Fori(1, B // 2) as i:
                    one(2 * i, 0)
                    one(2 * i + 1, 1)

            def at(tensor, b):
                return tensor[:, b] if isinstance(b, int) else tensor[:, bass.ds(b, 1)].rearrange(
                    "p o t d -> p (o t) d" if len(tensor.shape) == 4 else "p o n -> p (o n)")

            def xtile(b, t):
                return c.x[:, b, t] if isinstance(b, int) else c.x[:, bass.ds(b, 1), t, :]

            with nc.Block() as block:
                @block.sync
                def _(sp):
                    sp.dma_start(router[:], w_router).then_inc(router_loaded, 16)
                    sp.dma_start(wqkv[:], w_qkv.rearrange("(k p) n -> p k n", p=P)).then_inc(loaded, 16)
                    sp.dma_start(wo[:], w_o.rearrange("g p n -> p g n")).then_inc(loaded, 16)
                    for i, gain in enumerate((gain1, gain2)):
                        sp.dma_start(gains[:, i], gain).then_inc(loaded, 16)
                    sp.dma_start(w1[:], w_1.rearrange("(k p) n -> p k n", p=P)).then_inc(loaded, 16)
                    sp.dma_start(w2[:], w_2.rearrange("(k p) n -> p k n", p=P)).then_inc(loaded, 16)
                    for f in range(FT):
                        sp.dma_start(w3[0:rows_of(f), f], w_3[P * f:P * f + rows_of(f)]).then_inc(loaded, 16)

                @block.gpsimd
                def _(pool):
                    pool.iota(column[:], pattern=[[1, P]], base=0, channel_multiplier=0, allow_small_or_imprecise_dtypes=True).then_inc(ready, 1)
                    pool.memset(before[:], 1.0).then_inc(ready, 1)
                    pool.memset(counts[:], 0.0).then_inc(ready, 1)
                    pool.wait_ge(ready, 3)
                    pool.affine_select(out=before[:], in_=before[:], compare_op=ALU.is_gt, fill=0.0, base=0,
                                       pattern=[[-1, P]], channel_multiplier=1).then_inc(ready, 1)

                    def layer_norm(b):
                        hold(pool, ln_aggr, TT * b + TT, pool_passed)
                        pool.tensor_scalar(var_eps[:], mean_var[:, :, 1], 1e-5, None, ALU.add).then_inc(ln_eps, 1)
                        pool.wait_ge(ln_eps, b + 1)
                        pool.tensor_tensor(rstd[:], var_eps[:], c.minus_half[:, 0:TT], ALU.pow).then_inc(ln_rstd, 1)

                    def add(b, slot):
                        layer_norm(b)
                        hold(pool, ln_done, TT * b + TT, pool_passed)
                        pool.tensor_tensor(at(c.x, b), at(c.x, b), h[:, slot], ALU.add).then_inc(h_added, 1)

                    pairs(pool, add)

                    pool.wait_ge(loaded, 16 * (6 + FT))
                    pool.tensor_scalar(wqkv[:, :, 0:D], wqkv[:, :, 0:D], HD ** -0.5, None, ALU.mult).then_inc(scaled, 1)

                @block.scalar
                def _(act):
                    act.preload_act_table_set("natural_log_exp_and_others")

                    def keep(b, slot):
                        act.wait_ge(back_full, b + 1)
                        act.activation(at(back, b), back_ps[:, slot], ACT.Copy).then_inc(back_copied, 1)
                        act.wait_ge(chosen_full, b + 1)
                        act.activation(at(chosen, b), chosen_ps[:, slot, 0:D], ACT.Copy).then_inc(chosen_copied, 1)
                        wait(act, sq_done, b)
                        total = mean_sq[:, 0, b:b + 1] if isinstance(b, int) else mean_sq[:, 0, bass.ds(b, 1)]
                        act.activation(squares[:], chosen_ps[:, slot, 0:D], ACT.Square, accum_out=total).then_inc(sq_done, 1)

                    pairs(act, keep)

                @block.vector
                def _(dve):
                    def normalise(b, slot):
                        wait(dve, ln_aggr, TT * b)
                        for t in range(TT):
                            dve.bn_stats(stats[:, t], xtile(b, t)).then_inc(ln_stats, 1)
                        for t in range(TT):
                            hold(dve, ln_stats, TT * b + t + 1, dve_passed)
                            if t == 0:
                                hold(dve, ln_eps, b, dve_passed)
                                hold(dve, ln_done, TT * b, dve_passed)
                            dve.bn_aggr(mean_var[:, t], stats[:, t]).then_inc(ln_aggr, 1)
                        dve.wait_ge(ln_aggr, TT * b + TT)
                        wait(dve, chosen_full, b - 1)
                        wait(dve, h_added, b - 1)
                        dve.wait_ge(ln_rstd, b + 1)
                        for t in range(TT):
                            dve.tensor_scalar(h[:, slot, t], xtile(b, t), mean_var[:, t, 0:1], rstd[:, t:t + 1],
                                              ALU.subtract, ALU.mult).then_inc(ln_done, 1)
                        wait(dve, rows_full, b - 1)
                        wait(dve, counted, COUNTS * (b - 1))
                        wait(dve, scored, TT * b)
                        for t in range(TT):
                            dve.wait_ge(ln_done, TT * b + t + 1)
                            dve.scalar_tensor_tensor(product[:, t], h[:, slot, t], 1.0, router[:], ALU.mult, ALU.mult,
                                                     accum_out=score[:, slot, t:t + 1]).then_inc(scored, 1)

                    def choose(b, slot):
                        dve.wait_ge(rows_full, b + 1)
                        wait(dve, counted, COUNTS * b)
                        wait(dve, ranked, b)
                        for t in range(TT):
                            own = score[:, slot, t:t + 1]
                            if t > 0:
                                dve.tensor_scalar(above[:, t, 0:P * t], score_rows[:, slot, 0:P * t], own, 0.0, ALU.is_ge, ALU.add,
                                                  accum_out=counts[:, t, 0:1]).then_inc(counted, 1)
                            dve.tensor_scalar(above[:, t, P * t:S], score_rows[:, slot, P * t:S], own, 0.0, ALU.is_gt, ALU.add,
                                              accum_out=counts[:, t, 1:2]).then_inc(counted, 1)
                            dve.scalar_tensor_tensor(tied[:, t], score_rows[:, slot, P * t:P * t + P], own, before[:], ALU.is_equal, ALU.mult,
                                                     accum_out=counts[:, t, 2:3]).then_inc(counted, 1)
                        dve.wait_ge(counted, COUNTS * b + COUNTS)
                        hold(dve, picked, TT * b, dve_passed)
                        dve.tensor_reduce(rank[:], counts[:], AX, ALU.add).then_inc(ranked, 1)
                        dve.wait_ge(ranked, b + 1)
                        wait(dve, chosen_full, b - 1)
                        for t in range(TT):
                            dve.tensor_scalar(pick[:, slot, t], column[:], rank[:, t:t + 1], None, ALU.is_equal).then_inc(picked, 1)

                    dve.wait_ge(ready, 4)
                    dve.wait_ge(router_loaded, 16)
                    normalise(0, 0)

                    def both(b, slot):
                        normalise(b + 1, 1 - slot)
                        choose(b, slot)

                    both(0, 0)
                    both(1, 1)
                    both(2, 0)
                    with dve.Fori(1, B // 2 - 1) as i:
                        both(2 * i + 1, 1)
                        both(2 * i + 2, 0)
                    choose(B - 1, 1)

                @block.tensor
                def _(pe):
                    def gather(b, slot):
                        pe.wait_ge(scored, TT * b + TT)
                        wait(pe, counted, COUNTS * (b - 1))
                        for t in range(TT):
                            last = pe.transpose(score_rows[:, slot, P * t:P * t + P], score[:, slot, t:t + 1].to_broadcast([P, P]), c.ident[:])
                        last.then_inc(rows_full, 1)
                        pe.wait_ge(picked, TT * b + TT)
                        wait(pe, back_copied, b - 1)
                        for t in range(TT):
                            last = pe.transpose(back_ps[:, slot, P * t:P * t + P], pick[:, slot, t], c.ident[:])
                        last.then_inc(back_full, 1)
                        wait(pe, sq_done, b - 1)
                        for t in range(TT):
                            last = pe.matmul(chosen_ps[:, slot, 0:D], pick[:, slot, t], h[:, slot, t], start=(t == 0), stop=(t == TT - 1))
                        last.then_inc(chosen_full, 1)

                    pairs(pe, gather)

        xT = sb("xT", [P, KD, S])
        rows = sb("rows", [P, BS, D])
        parts = sb("parts", [P, 4, 3, S], BF16)
        rest = sb("rest", [P, 2, S])
        q_stack, k_stack = sb("q_stack", [P, H, S], BF16), sb("k_stack", [P, H, S], BF16)
        values = sb("values", [P, BS, H, 32])
        causal4 = sb("causal4", [P, GH, P], BF16)
        neg_max, sums, r_sums = (sb(what, [P, 4, GH]) for what in ("neg_max", "sums", "r_sums"))
        probs = sb("probs", [P, 3, GH, P])
        probsT = sb("probsT", [P, 2, S])
        attended = sb("attended", [P, 2, S])
        squares2 = sb("squares2", [P, D])
        silu = sb("silu", [P, 2, S])
        gated = sb("gated", [P, FT, S])
        scratch = nc.dram_tensor("depths_parts_dram", [4, P, 3, S], BF16).ap()
        general = ps("general", [P, 2, S])
        score_ps = ps("score_ps", [P, 2, S])
        turned_ps = ps("turned_ps", [P, 2, S])
        out_ps = ps("out_ps", [P, 2, S])

        constants, rms_done, rows_done, t_full, qk_full, v_full, v_copied = (
            sem(s) for s in ("constants", "rms_done", "rows_done", "t_full", "qk_full", "v_full", "v_copied"))
        ms_eps = sem("ms_eps")
        general_read = [sem(f"general_read{i}") for i in range(2)]
        part0_cut, rest_done, part1_cut, part2_cut, parts_stored, stacked = (
            sem(s) for s in ("part0_cut", "rest_done", "part1_cut", "part2_cut", "parts_stored", "stacked"))
        score_full, max_done, exp_done, sums_inverted, probs_scaled, turned, turned_copied = (
            sem(s) for s in ("score_full", "max_done", "exp_done", "sums_inverted", "probs_scaled", "turned", "turned_copied"))
        pv_done, attended_copied, attn_full, attn_kept, attn_added = (
            sem(s) for s in ("pv_done", "attended_copied", "attn_full", "attn_kept", "attn_added"))
        hidden_full, silu_done, gated_done, ff_full, ff_added, back_out = (
            sem(s) for s in ("hidden_full", "silu_done", "gated_done", "ff_full", "ff_added", "back_out"))

        uses = []
        for s in range(SB):
            uses += [("xT", s, k) for k in range(KD)] + [("qk", s, i) for i in range(4)] + [("v", s, i) for i in range(2)]
            if s == 0:
                uses += [("attn", 0, i) for i in range(BS)]
            else:
                uses += [("xT", SB, k) for k in range(KD)] + [("back", 0, i) for i in range(2 * BS)]
                uses += [("attn", 1, i) for i in range(BS)]
                uses += [("xT", SB + 1, k) for k in range(KD)] + [("back", 1, i) for i in range(2 * BS)]
        place = {use: (n % 2, n // 2) for n, use in enumerate(uses)}

        def bank(*use):
            return place[use][0]

        def nth(*use):
            return place[use][1]

        with nc.Block() as block:
            @block.sync
            def _(sp):
                for s in range(SB):
                    for i in range(4):
                        sp.wait_ge(part2_cut, 4 * s + i + 1)
                        wait(sp, stacked, 384 * s)
                        sp.dma_start(scratch[i], parts[:, i]).then_inc(parts_stored, 16)
                    wait(sp, score_full, UNITS * s)
                    sp.wait_ge(parts_stored, 64 * s + 64)
                    for half in range(2):
                        for stk, item, which in ((q_stack, 2 * half, Q_PART), (k_stack, 2 * half + 1, K_PART)):
                            for r, part in enumerate(which):
                                sp.dma_start(stk[HD * r:HD * r + HD, 8 * half:8 * half + 8, :],
                                             scratch[item, :, part, :].rearrange("(h d) t -> d h t", d=HD)).then_inc(stacked, 16)

            @block.gpsimd
            def _(pool):
                def r_rms_of(which, first, count, step):
                    cut = slice(first, first + count)
                    pool.tensor_scalar(mean_sq[:, which, cut], mean_sq[:, which, cut], 1.0 / D, 1e-6, ALU.mult, ALU.add).then_inc(ms_eps, 1)
                    pool.wait_ge(ms_eps, step)
                    pool.tensor_tensor(r_rms[:, which, cut], mean_sq[:, which, cut], c.minus_half[:, 0:count], ALU.pow).then_inc(rms_done, 1)

                r_rms_of(0, 0, B, 1)
                pool.memset(values[:, :, :, HD:], 0.0).then_inc(constants, 1)
                for g in range(GH):
                    pool.tensor_copy(causal4[:, g], c.causal_qk[:]).then_inc(constants, 1)

                def cuts(s):
                    for i in range(4):
                        pool.wait_ge(part1_cut, 4 * s + i + 1)
                        pool.tensor_tensor(parts[:, i, 2], rest[:, i % 2], parts[:, i, 1], ALU.subtract).then_inc(part2_cut, 1)

                def attend(s):
                    for n in range(UNITS * s, UNITS * s + UNITS):
                        pool.wait_ge(sums_inverted, n + 1)
                        pool.tensor_tensor(probs[:, n % 3], probs[:, n % 3], r_sums[:, n % 4].unsqueeze(2).to_broadcast([P, GH, P]),
                                           ALU.mult).then_inc(probs_scaled, 1)

                cuts(0)
                attend(0)
                cuts(1)
                pool.wait_ge(sq_done, B + BS)
                r_rms_of(1, 0, BS, 2)
                attend(1)
                pool.wait_ge(sq_done, B + 2 * BS)
                r_rms_of(1, BS, BS, 3)

            @block.scalar
            def _(act):
                def features(j, gain, free, value):
                    wait(act, free, value)
                    for k in range(KD):
                        act.wait_ge(t_full, 2 * j + k + 1)
                        act.activation(xT[:, k], general[:, bank("xT", j, k)], ACT.Copy, scale=gains[:, gain, k:k + 1]
                                       ).then_inc(general_read[bank("xT", j, k)], 1)

                def cuts(s):
                    for i in range(4):
                        act.wait_ge(qk_full, 4 * s + i + 1)
                        wait(act, parts_stored, 64 * s)
                        act.activation(parts[:, i, 0], general[:, bank("qk", s, i)], ACT.Copy).then_inc(part0_cut, 1)
                        act.wait_ge(rest_done, 4 * s + i + 1)
                        act.activation(parts[:, i, 1], rest[:, i % 2], ACT.Copy).then_inc(part1_cut, 1)

                def copy_out(q):
                    act.wait_ge(pv_done, NG * q + NG)
                    wait(act, attn_full, q - 1)
                    act.activation(attended[:, q % 2], out_ps[:, q % 2], ACT.Copy).then_inc(attended_copied, 1)

                def attend(s):
                    for i in range(UNITS + 5):
                        n = UNITS * s + i
                        if i < UNITS:
                            act.wait_ge(max_done, n + 1)
                            wait(act, turned, n - 2)
                            for g in range(GH):
                                act.activation(probs[:, n % 3, g], score_ps[:, n % 2, P * g:P * g + P], ACT.Exp, bias=neg_max[:, n % 4, g:g + 1],
                                               accum_out=sums[:, n % 4, g:g + 1]).then_inc(exp_done, 1)
                        if i >= NG and i % NG == 0 and i // NG <= BS:
                            copy_out(BS * s + i // NG - 1)

                def squares_of(s):
                    for q in range(BS * s, BS * s + BS):
                        act.wait_ge(attn_added, q + 1)
                        act.wait_ge(sq_done, B + q)
                        act.activation(squares2[:], chosen[:, q], ACT.Square, accum_out=mean_sq[:, 1, q:q + 1]).then_inc(sq_done, 1)

                def feed_forward(s):
                    for f in range(FT):
                        n = FT * s + f
                        act.wait_ge(hidden_full, n + 1)
                        wait(act, gated_done, n - 1)
                        r = rows_of(f)
                        act.activation(silu[0:r, f % 2], score_ps[0:r, f % 2], ACT.Silu).then_inc(silu_done, 1)

                features(0, 0, None, 0)
                cuts(0)
                attend(0)
                features(1, 0, v_full, 2)
                cuts(1)
                squares_of(0)
                features(2, 1, v_full, 4)
                feed_forward(0)
                attend(1)
                squares_of(1)
                features(3, 1, hidden_full, FT)
                feed_forward(1)

            @block.vector
            def _(dve):
                def normed(j, which, s):
                    dve.wait_ge(rms_done, (1, 1, 2, 3)[j])
                    wait(dve, t_full, 2 * j)
                    for i in range(BS):
                        q = BS * s + i
                        dve.tensor_scalar(rows[:, i], chosen[:, q], r_rms[:, which, q:q + 1], None, ALU.mult).then_inc(rows_done, 1)

                def leftover(s):
                    for i in range(4):
                        dve.wait_ge(part0_cut, 4 * s + i + 1)
                        wait(dve, part2_cut, 4 * s + i - 1)
                        b = bank("qk", s, i)
                        dve.tensor_tensor(rest[:, i % 2], general[:, b], parts[:, i, 0], ALU.subtract).then_inc(rest_done, 1)

                def valued(s):
                    for i in range(2):
                        dve.wait_ge(v_full, 2 * s + i + 1)
                        wait(dve, pv_done, UNITS * s)
                        dve.tensor_copy(values[:, 2 * i:2 * i + 2, :, 0:HD],
                                        general[:, bank("v", s, i)].rearrange("p (t h d) -> p t h d", t=2, d=HD)
                                        ).then_inc(v_copied, 1)

                def keep(q):
                    s, i = q // BS, q % BS
                    dve.wait_ge(attn_full, q + 1)
                    dve.tensor_copy(delta[:, q], general[:, bank("attn", s, i), 0:D]).then_inc(attn_kept, 1)
                    dve.wait_ge(attn_kept, q + 1)
                    dve.tensor_tensor(chosen[:, q], chosen[:, q], delta[:, q], ALU.add).then_inc(attn_added, 1)

                def attend(s):
                    for i in range(UNITS + 7):
                        n = UNITS * s + i
                        if i < UNITS:
                            dve.wait_ge(score_full, n + 1)
                            wait(dve, exp_done, GH * (n - 3))
                            dve.tensor_reduce(neg_max[:, n % 4], score_ps[:, n % 2].rearrange("p (g k) -> p g k", g=GH), AX, ALU.max,
                                              negate=True).then_inc(max_done, 1)
                        if 1 <= i <= UNITS:
                            dve.wait_ge(exp_done, GH * n)
                            wait(dve, probs_scaled, n - 4)
                            dve.reciprocal(r_sums[:, (n - 1) % 4], sums[:, (n - 1) % 4]).then_inc(sums_inverted, 1)
                        if 2 <= i <= UNITS + 1:
                            dve.wait_ge(turned, n - 1)
                            wait(dve, pv_done, n - 3)
                            dve.tensor_copy(probsT[:, n % 2], turned_ps[:, n % 2]).then_inc(turned_copied, 1)
                        if i >= 7 and (i - 7) % NG == 3:
                            keep(BS * s + (i - 7) // NG)
                    keep(BS * s + BS - 1) if (UNITS + 7 - 1 - 7) // NG < BS - 1 else None

                def feed_forward(s):
                    for f in range(FT):
                        n, r = FT * s + f, rows_of(f)
                        dve.wait_ge(silu_done, n + 1)
                        wait(dve, ff_full, BS * s)
                        dve.tensor_tensor(gated[0:r, f], silu[0:r, f % 2], turned_ps[0:r, f % 2], ALU.mult).then_inc(gated_done, 1)
                    for i in range(BS + 1):
                        if i < BS:
                            q = BS * s + i
                            dve.wait_ge(ff_full, q + 1)
                            dve.wait_ge(attn_added, q + 1)
                            dve.tensor_tensor(delta[:, q], out_ps[:, i % 2, 0:D], delta[:, q], ALU.add).then_inc(ff_added, 1)
                        if i >= 1:
                            q = BS * s + i - 1
                            for half in range(2):
                                dve.wait_ge(back_out, 2 * q + half + 1)
                                b = bank("back", s, 2 * (i - 1) + half)
                                dst = c.x[:, q, 2 * half:2 * half + 2]
                                dve.tensor_tensor(dst, general[:, b].rearrange("p (t d) -> p t d", t=2), dst, ALU.add).then_inc(general_read[b], 1)

                dve.wait_ge(constants, 1 + GH)
                normed(0, 0, 0)
                leftover(0)
                valued(0)
                attend(0)
                normed(1, 0, 1)
                leftover(1)
                valued(1)
                normed(2, 1, 0)
                feed_forward(0)
                attend(1)
                normed(3, 1, 1)
                feed_forward(1)

            @block.tensor
            def _(pe):
                def readers(kind, s, i):
                    if kind in ("xT", "back"):
                        b = bank(kind, s, i)
                        before = [u for u in uses[:uses.index((kind, s, i))] if u[0] in ("xT", "back") and bank(*u) == b]
                        return general_read[b], len(before) + 1
                    return {"qk": (rest_done, 4 * s + i + 1), "v": (v_copied, 2 * s + i + 1), "attn": (attn_kept, BS * s + i + 1)}[kind]

                def free(*use):
                    at = uses.index(use)
                    if at >= 2:
                        pe.wait_ge(*readers(*uses[at - 2]))

                def turn(j):
                    pe.wait_ge(rows_done, BS * j + BS)
                    for k in range(KD):
                        free("xT", j, k)
                        for i in range(BS):
                            last = pe.transpose(general[:, bank("xT", j, k), P * i:P * i + P], rows[:, i, P * k:P * k + P], c.ident[:])
                        last.then_inc(t_full, 1)
                    for k in range(KD):
                        pe.wait_ge(*readers("xT", j, k))

                def project(s):
                    turn(s)
                    for i in range(4):
                        free("qk", s, i)
                        col = (0, D, P, D + P)[i]
                        for k in range(KD):
                            last = pe.matmul(general[:, bank("qk", s, i)], wqkv[:, k, col:col + P], xT[:, k], start=(k == 0), stop=(k == KD - 1))
                        last.then_inc(qk_full, 1)
                    for i in range(2):
                        free("v", s, i)
                        for t in range(2):
                            tok = P * (2 * i + t)
                            for k in range(KD):
                                last = pe.matmul(general[:, bank("v", s, i), D * t:D * t + D], xT[:, k, tok:tok + P], wqkv[:, k, 2 * D:],
                                                 start=(k == 0), stop=(k == KD - 1))
                        last.then_inc(v_full, 1)

                def scores(n):
                    s, q, g = n // UNITS, (n % UNITS) // NG, n % NG
                    if n % UNITS == 0:
                        pe.wait_ge(stacked, 384 * s + 384)
                    if n % UNITS < 2:
                        wait(pe, silu_done, FT * s)
                    wait(pe, exp_done, GH * (n - 1))
                    for h in range(GH):
                        cols = slice(P * q, P * q + P)
                        pe.matmul(score_ps[:, n % 2, P * h:P * h + P], q_stack[0:ROWS, GH * g + h, cols], k_stack[0:ROWS, GH * g + h, cols],
                                  start=(h == 0), stop=False, skip_group_check=True)
                    pe.matmul(score_ps[:, n % 2], c.ident_b[:], causal4[:].rearrange("p g k -> p (g k)"),
                              start=False, stop=True, skip_group_check=True).then_inc(score_full, 1)

                def turn_probs(n):
                    pe.wait_ge(probs_scaled, n + 1)
                    wait(pe, turned_copied, n - 1)
                    if n % UNITS < 2:
                        wait(pe, gated_done, FT * (n // UNITS))
                    for g in range(GH):
                        last = pe.transpose(turned_ps[:, n % 2, P * g:P * g + P], probs[:, n % 3, g], c.ident[:])
                    last.then_inc(turned, 1)

                def with_values(n):
                    s, q, g = n // UNITS, n // NG, n % NG
                    pe.wait_ge(turned_copied, n + 1)
                    if g == 0:
                        pe.wait_ge(v_copied, 2 * s + 2)
                        wait(pe, attended_copied, q - 1)
                        if q % BS < 2:
                            wait(pe, ff_added, BS * s)
                    for h in range(GH):
                        last = pe.matmul(out_ps[32 * h:32 * h + 32, q % 2, P * g:P * g + P], values[:, q % BS, GH * g + h],
                                         probsT[:, n % 2, P * h:P * h + P], start=True, stop=True, tile_position=(0, 32 * h))
                    last.then_inc(pv_done, 1)

                def output(q):
                    s, i = q // BS, q % BS
                    pe.wait_ge(attended_copied, q + 1)
                    free("attn", s, i)
                    for g in range(NG):
                        last = pe.matmul(general[:, bank("attn", s, i), 0:D], attended[:, q % 2, P * g:P * g + P], wo[:, g],
                                         start=(g == 0), stop=(g == NG - 1))
                    last.then_inc(attn_full, 1)

                def attend(s):
                    for i in range(UNITS + 6):
                        n = UNITS * s + i
                        if i < UNITS:
                            scores(n)
                        if 2 <= i < UNITS + 2:
                            turn_probs(n - 2)
                        if 3 <= i < UNITS + 3:
                            with_values(n - 3)
                        if i >= 5 and (i - 5) % NG == 3:
                            output(BS * s + (i - 5) // NG)
                    if (UNITS + 6 - 1 - 5) // NG < BS - 1 or (UNITS + 6 - 1 - 5) % NG < 3 and (UNITS + 6 - 1 - 5) // NG == BS - 1:
                        output(BS * s + BS - 1)

                def feed_forward(s):
                    turn(SB + s)
                    for f in range(FT):
                        n, r = FT * s + f, rows_of(f)
                        if f < 2:
                            pe.wait_ge(exp_done, GH * UNITS * (s + 1))
                            pe.wait_ge(turned_copied, UNITS * (s + 1))
                        else:
                            pe.wait_ge(gated_done, n - 1)
                        for dst, w in ((score_ps, w1), (turned_ps, w2)):
                            for k in range(KD):
                                last = pe.matmul(dst[0:r, f % 2], w[:, k, P * f:P * f + r], xT[:, k], start=(k == 0), stop=(k == KD - 1))
                        last.then_inc(hidden_full, 1)
                    pe.wait_ge(gated_done, FT * s + FT)
                    for i in range(BS + 1):
                        if i < BS:
                            q = BS * s + i
                            if i < 2:
                                pe.wait_ge(attended_copied, BS * s + BS)
                            else:
                                pe.wait_ge(ff_added, q - 1)
                            for f in range(FT):
                                last = pe.matmul(out_ps[:, i % 2, 0:D], gated[0:rows_of(f), f, P * i:P * i + P], w3[0:rows_of(f), f],
                                                 start=(f == 0), stop=(f == FT - 1))
                            last.then_inc(ff_full, 1)
                        if i >= 1:
                            q = BS * s + i - 1
                            pe.wait_ge(ff_added, q + 1)
                            for half in range(2):
                                use = ("back", s, 2 * (i - 1) + half)
                                free(*use)
                                for t in range(2):
                                    tok = P * (2 * half + t)
                                    last = pe.matmul(general[:, bank(*use), D * t:D * t + D], back[:, q, tok:tok + P], delta[:, q], start=True, stop=True)
                                last.then_inc(back_out, 1)

                pe.wait_ge(constants, 1 + GH)
                project(0)
                attend(0)
                project(1)
                feed_forward(0)
                attend(1)
                feed_forward(1)

    nc.clear_and_free_semaphores(made)
    nc.all_engine_barrier()


class Slots:
    E = 8
    TILES = 2 * B * S // P + E - 1
    FILLED = B * -(-TILES // B)
    ID, GATES = D, D + 1
    ROW = D + 1 + E
    NOBODY = 1 << 20

    def __init__(self, nc, ctx):
        self.dram = nc.dram_tensor("expert_rows_dram", [self.FILLED, P, self.ROW], F32).ap()
        self.filling = ctx.enter_context(nc.sbuf_tensor("filling", [P, self.ROW], F32))
        self.filled = nc.alloc_semaphore("slots_filled")

    def fill(self, sp, b):
        n = self.FILLED // B
        dst = self.dram[n * b:n * b + n] if isinstance(b, int) else self.dram[bass.ds(n * b, n)]
        sp.dma_start(dst.rearrange("n p d -> p n d"), self.filling[:].unsqueeze(1).to_broadcast([P, n, self.ROW])).then_inc(self.filled, 16)


def mixture_of_experts(nc, c, slots, w_router, w_up, b_up, w_down, b_down, out):
    made = []
    E = w_up.shape[0]
    U = w_up.shape[2]
    UT = U // P
    NT = B * TT
    TILES, ROW, ID, GATES = slots.TILES, slots.ROW, slots.ID, slots.GATES

    def sem(what):
        s = nc.alloc_semaphore(f"moe_{what}")
        made.append(s)
        return s

    with ExitStack() as ctx:
        def sb(what, shape, dt=F32):
            return ctx.enter_context(nc.sbuf_tensor(f"experts_{what}", shape, dt))

        def ps(what, shape, dt=F32):
            return ctx.enter_context(nc.psum_tensor(f"experts_{what}", shape, dt))

        up = sb("up", [P, E, KD * U])
        down = sb("down", [P, E, UT * D])
        ROUTING = 4
        xn = down[:, 7].rearrange("p (s t d) -> p s t d", s=2, d=D)
        xnT = down[:, 6].rearrange("p (s k n) -> p s k n", s=2, n=S)
        gatesT = down[0:E, 4:6].rearrange("e o (n p) -> e (o n) p", p=P)
        up_now = c.x[:, 0:4].rearrange("p (s b) t d -> p s (b t d)", s=2).rearrange("p s (k u) -> p s k u", k=KD)
        hidden = c.x[:, 4:6].rearrange("p s t d -> p s (t d)").rearrange("p s (u n) -> p s u n", n=P)

        up_bias = sb("up_bias", [P, E, UT])
        down_bias = sb("down_bias", [E, D])
        router = sb("router", [P, KD, E])
        stats = sb("stats", [P, NT, 6])
        mean_var = sb("mean_var", [P, NT, 2])
        var_eps = sb("var_eps", [P, NT])
        rstd = sb("rstd", [P, NT])
        logits = sb("logits", [P, NT, E])
        count = sb("count", [P, NT, E])
        past = sb("past", [P, NT, E])
        first, second = sb("first", [P, NT, E]), sb("second", [P, NT, E])
        best, best2, place, place2, gap, odds, total, gate1, gate2 = (
            sb(what, [P, NT]) for what in ("best", "best2", "place", "place2", "gap", "odds", "total", "gate1", "gate2"))
        gates = sb("gates", [P, NT, E])
        chosen = sb("chosen", [P, NT, E])
        earlier = sb("earlier", [P, P])
        ones = sb("ones", [P, P])
        running = sb("running", [P, 2, NT, E])
        thresholds = sb("thresholds", [P, E, NT])
        filled_tiles = sb("filled_tiles", [P, E, NT])
        tiles = sb("tiles", [P, E])
        tile0 = sb("tile0", [P, E])
        position = sb("position", [P, NT, E])
        where = sb("where", [P, 2, NT])
        slot_of = sb("slot_of", [P, 2, NT], U32)
        tile_number = sb("tile_number", [P, TILES])
        expert = sb("expert", [P, 2, TILES])
        expert_of = sb("expert_of", [P, TILES], U32)
        numbers = sb("numbers", [P, NT], U32)
        rows = sb("rows", [P, 2, TT, ROW])

        tile_rows = sb("tile_rows", [P, 2, ROW])
        tileT = sb("tileT", [P, 2, KD, P])
        bias_now = sb("bias_now", [P, 2, UT])
        gate_now = sb("gate_now", [P, 2])
        token_now = sb("token_now", [P, 2], U32)
        result = sb("result", [P, 2, D])

        up_ps = ps("up_ps", [P, 4, S])
        down_ps = ps("down_ps", [P, 2, S])
        turn_ps = ps("turn_ps", [P, 2, S])

        loaded, biases_loaded, weights_loaded = sem("loaded"), sem("biases_loaded"), sem("weights_loaded")
        ready, ln_stats, ln_aggr, ln_eps, ln_rstd, ln_done = (
            sem(s) for s in ("ready", "ln_stats", "ln_aggr", "ln_eps", "ln_rstd", "ln_done"))
        xt_full, xt_copied, logits_full, logits_copied = (sem(s) for s in ("xt_full", "xt_copied", "logits_full", "logits_copied"))
        routed, odds_done, ranks_full, gt_full, gt_copied = (sem(s) for s in ("routed", "odds_done", "ranks_full", "gt_full", "gt_copied"))
        bias_full, bias_added = sem("bias_full"), sem("bias_added")
        rows_done, scattered, stored = sem("rows_done"), [sem(f"scattered{i}") for i in range(2)], sem("stored")
        rows_in = [sem(f"rows_in{i}") for i in range(2)]
        turned, turned_copied, weights_copied, taken = (sem(s) for s in ("turned", "turned_copied", "weights_copied", "taken"))
        bias_taken, up_full, gelu_done, down_full, weighted, added = (
            sem(s) for s in ("bias_taken", "up_full", "gelu_done", "down_full", "weighted", "added"))
        sp_passed, dve_passed, pool_passed = sem("sp_passed"), sem("dve_passed"), sem("pool_passed")

        def tile_loop(eng, body):
            body(0, 0)
            body(1, 1)
            body(2, 0)
            with eng.Fori(1, (TILES - 3) // 2) as j:
                body(2 * j + 1, 1)
                body(2 * j + 2, 0)

        def expert_at(eng, i):
            cell = expert_of[0:1, i:i + 1] if isinstance(i, int) else expert_of[0:1, bass.ds(i, 1)]
            return eng.value_load(cell, min_val=0, max_val=E - 1)

        def of(tensor, e):
            return tensor[:, bass.ds(e, 1)].rearrange("p o n -> p (o n)")

        assert TILES % 2 == 1
        route_steps = 55

        with nc.Block() as block:
            @block.sync
            def _(sp):
                sp.dma_start(router[:], w_router.rearrange("(k p) e -> p k e", p=P)).then_inc(loaded, 16)
                sp.dma_start(up_bias[:], b_up).then_inc(biases_loaded, 16)
                sp.dma_start(down_bias[:], b_down).then_inc(biases_loaded, 16)
                for e in range(E):
                    sp.dma_start(up[:, e].rearrange("p (k u) -> p k u", k=KD), w_up[e].rearrange("(k p) u -> p k u", p=P)).then_inc(weights_loaded, 16)
                for e in range(E):
                    if e == ROUTING:
                        sp.wait_ge(bias_full, NT // 2)
                        sp.wait_ge(gt_copied, NT // 4)
                        sp.wait_ge(logits_full, 1)
                    sp.dma_start(down[:, e].rearrange("p (u d) -> p u d", d=D), w_down[e].rearrange("(u p) d -> p u d", p=P)).then_inc(weights_loaded, 16)
                for b in range(B):
                    sp.wait_ge(bias_added, 2 * b + 2)
                    sp.dma_start(out[b].rearrange("(t p) d -> p t d", p=P), c.x[:, b]).then_inc(stored, 16)
                sp.wait_ge(scattered[0], 16 * NT)
                sp.wait_ge(scattered[1], 16 * NT)

                def fetch(i, slot):
                    hold(sp, turned, i - 1, sp_passed)
                    hold(sp, taken, 2 * (i - 1), sp_passed)
                    src = slots.dram[i] if isinstance(i, int) else slots.dram[bass.ds(i, 1)].rearrange("o p d -> (o p) d")
                    sp.dma_start(tile_rows[:, slot], src).then_inc(rows_in[slot], 16)

                tile_loop(sp, fetch)
                fetch(TILES - 2, 1)
                fetch(TILES - 1, 0)
                sp.wait_ge(stored, 16 * B)

            @block.gpsimd
            def _(pool):
                for e in range(E):
                    pool.memset(count[:, :, e], float(e)).then_inc(ready, 1)
                pool.memset(ones[:], 1.0).then_inc(ready, 1)
                pool.memset(earlier[:], 1.0).then_inc(ready, 1)
                pool.memset(tile0[:], 0.0).then_inc(ready, 1)
                pool.memset(expert[:], 0.0).then_inc(ready, 1)
                pool.iota(thresholds[:], pattern=[[0, E], [P, NT]], base=0, channel_multiplier=0, allow_small_or_imprecise_dtypes=True).then_inc(ready, 1)
                pool.iota(tile_number[:], pattern=[[1, TILES]], base=0, channel_multiplier=0, allow_small_or_imprecise_dtypes=True).then_inc(ready, 1)
                pool.iota(numbers[:], pattern=[[P, NT]], base=0, channel_multiplier=1).then_inc(ready, 1)
                pool.wait_ge(ready, E + 7)
                pool.affine_select(out=earlier[:], in_=earlier[:], compare_op=ALU.is_gt, fill=0.0, base=0,
                                   pattern=[[1, P]], channel_multiplier=-1).then_inc(ready, 1)
                pool.wait_ge(ln_aggr, NT)
                pool.tensor_scalar(var_eps[:], mean_var[:, :, 1], 1e-5, None, ALU.add).then_inc(ln_eps, 1)
                pool.wait_ge(ln_eps, 1)
                pool.tensor_tensor(rstd[:], var_eps[:], c.minus_half[:, 0:NT], ALU.pow).then_inc(ln_rstd, 1)

                pool.wait_ge(slots.filled, 16 * B)
                for b in range(B):
                    pool.wait_ge(rows_done, (TT + 2) * (b + 1))
                    for t in range(TT):
                        for k in range(2):
                            pool.indirect_dma_start(
                                out=slots.dram.rearrange("n p d -> (n p) d"),
                                out_offset=bass.IndirectOffsetOnAxis(ap=slot_of[:, k, TT * b + t:TT * b + t + 1], axis=0),
                                in_=rows[:, b % 2, t], in_offset=None).then_inc(scattered[b % 2], 16)
                pool.wait_ge(stored, 16 * B)

                def accumulate(i, slot):
                    hold(pool, weighted, i + 1, pool_passed)
                    hold(pool, added, 16 * i, pool_passed)
                    pool.indirect_dma_start(out=out.rearrange("b s d -> (b s) d"),
                                            out_offset=bass.IndirectOffsetOnAxis(ap=token_now[:, slot:slot + 1], axis=0),
                                            in_=result[:, slot], in_offset=None, bounds_check=B * S - 1, oob_is_err=False,
                                            compute_op=ALU.add).then_inc(added, 16)

                tile_loop(pool, accumulate)
                accumulate(TILES - 2, 1)
                accumulate(TILES - 1, 0)
                pool.wait_ge(added, 16 * TILES)

            @block.scalar
            def _(act):
                act.preload_act_table_set("natural_log_exp_and_others")
                for b in range(B):
                    wait(act, logits_full, b - 1)
                    for k in range(KD):
                        act.wait_ge(xt_full, 2 * b + k + 1)
                        act.activation(xnT[:, b % 2, k], up_ps[:, (2 * b + k) % 4], ACT.Copy).then_inc(xt_copied, 1)
                act.wait_ge(logits_full, B)
                act.activation(logits[:].rearrange("p n e -> p (n e)"), down_ps[:, 0, 0:NT * E], ACT.Copy).then_inc(logits_copied, 1)
                act.wait_ge(routed, 12)
                act.activation(odds[:], gap[:], ACT.Exp).then_inc(odds_done, 1)
                for i in range(NT // 4):
                    act.wait_ge(gt_full, i + 1)
                    act.activation(gatesT[:, 4 * i:4 * i + 4].rearrange("e n p -> e (n p)"), up_ps[0:E, i % 4], ACT.Copy).then_inc(gt_copied, 1)
                act.preload_act_table_set("gelu_and_others")
                act.wait_ge(biases_loaded, 32)
                act.wait_ge(stored, 16 * B)
                act.wait_ge(routed, route_steps)

                def units(i, slot):
                    wait(act, gelu_done, UT * (i - 1))
                    act.activation(bias_now[:, slot], of(up_bias, expert_at(act, i)), ACT.Copy).then_inc(bias_taken, 1)
                    act.wait_ge(bias_taken, i + 1)
                    wait(act, down_full, i - 1)
                    for u in range(UT):
                        if u % 4 == 0:
                            act.wait_ge(up_full, 2 * i + u // 4 + 1)
                        act.activation(hidden[:, slot, u], up_ps[:, 2 * slot + u // 4, P * (u % 4):P * (u % 4) + P], ACT.Gelu,
                                       bias=bias_now[:, slot, u:u + 1]).then_inc(gelu_done, 1)

                tile_loop(act, units)
                units(TILES - 2, 1)
                units(TILES - 1, 0)

            @block.vector
            def _(dve):
                for b in range(B):
                    for t in range(TT):
                        dve.bn_stats(stats[:, TT * b + t], c.x[:, b, t]).then_inc(ln_stats, 1)
                for n in range(NT):
                    dve.wait_ge(ln_stats, n + 1)
                    dve.bn_aggr(mean_var[:, n], stats[:, n]).then_inc(ln_aggr, 1)
                dve.wait_ge(ln_rstd, 1)
                dve.wait_ge(ln_aggr, NT)

                def normalise(to, b, done):
                    for t in range(TT):
                        n = TT * b + t
                        dve.tensor_scalar(to[:, b % 2, t, 0:D], c.x[:, b, t], mean_var[:, n, 0:1], rstd[:, n:n + 1],
                                          ALU.subtract, ALU.mult).then_inc(done, 1)

                for b in range(B):
                    wait(dve, xt_full, 2 * (b - 1))
                    normalise(xn, b, ln_done)

                def wide(a):
                    return a.unsqueeze(2).to_broadcast([P, NT, E])

                steps = 0

                def then(instruction):
                    nonlocal steps
                    steps += 1
                    instruction.then_inc(routed, 1)
                    dve.wait_ge(routed, steps)

                def pick(source, value, number, one_hot):
                    then(dve.tensor_reduce(value[:], source[:], AX, ALU.max))
                    then(dve.tensor_tensor(past[:], source[:], wide(value[:]), ALU.is_lt))
                    then(dve.scalar_tensor_tensor(past[:], past[:], float(E), count[:], ALU.mult, ALU.add))
                    then(dve.tensor_reduce(number[:], past[:], AX, ALU.min))
                    then(dve.tensor_tensor(one_hot[:], count[:], wide(number[:]), ALU.is_equal))

                dve.wait_ge(ready, E + 8)
                dve.wait_ge(logits_copied, 1)
                pick(logits, best, place, first)
                then(dve.scalar_tensor_tensor(logits[:], first[:], NEG, logits[:], ALU.mult, ALU.add))
                pick(logits, best2, place2, second)
                then(dve.tensor_tensor(gap[:], best2[:], best[:], ALU.subtract))
                assert steps == 12
                then(dve.tensor_tensor(chosen[:], first[:], second[:], ALU.add))
                dve.wait_ge(odds_done, 1)
                then(dve.tensor_scalar(total[:], odds[:], 1.0, None, ALU.add))
                then(dve.reciprocal(gate1[:], total[:]))
                then(dve.tensor_tensor(gate2[:], gate1[:], odds[:], ALU.mult))
                then(dve.tensor_tensor(gates[:], first[:], wide(gate1[:]), ALU.mult))
                then(dve.tensor_tensor(past[:], second[:], wide(gate2[:]), ALU.mult))
                then(dve.tensor_tensor(gates[:], gates[:], past[:], ALU.add))
                assert steps == 19

                dve.wait_ge(ranks_full, 2)
                flat = lambda a: a.rearrange("p n e -> p (n e)")
                then(dve.tensor_copy(flat(position[:]), down_ps[:, 1, 0:NT * E]))
                then(dve.tensor_copy(flat(running[:, 0]), turn_ps[:, 0, 0:NT * E]))
                at, span = 0, 1
                while span < NT:
                    then(dve.tensor_copy(running[:, 1 - at, 0:span], running[:, at, 0:span]))
                    then(dve.tensor_tensor(running[:, 1 - at, span:], running[:, at, span:], running[:, at, 0:NT - span], ALU.add))
                    at, span = 1 - at, 2 * span
                then(dve.tensor_tensor(position[:, 1:], position[:, 1:], running[:, at, 0:NT - 1], ALU.add))
                then(dve.tensor_tensor(filled_tiles[:], thresholds[:], running[:, at, NT - 1].unsqueeze(2).to_broadcast([P, E, NT]), ALU.is_lt))
                then(dve.tensor_reduce(tiles[:], filled_tiles[:], AX, ALU.add))
                for e in range(1, E):
                    then(dve.tensor_tensor(tile0[:, e:e + 1], tile0[:, e - 1:e], tiles[:, e - 1:e], ALU.add))
                then(dve.scalar_tensor_tensor(position[:], tile0[:].unsqueeze(1).to_broadcast([P, NT, E]), float(P), position[:], ALU.mult, ALU.add))
                for k, one_hot in enumerate((first, second)):
                    then(dve.tensor_tensor(one_hot[:], one_hot[:], position[:], ALU.mult))
                    then(dve.tensor_reduce(where[:, k], one_hot[:], AX, ALU.add))
                then(dve.tensor_copy(slot_of[:], where[:]))

                for b in range(B):
                    wait(dve, scattered[b % 2], 16 * 2 * TT * (b // 2))
                    normalise(rows, b, rows_done)
                    dve.tensor_copy(rows[:, b % 2, :, ID:ID + 1].bitcast(U32).rearrange("p t o -> p (t o)"), numbers[:, TT * b:TT * b + TT]).then_inc(rows_done, 1)
                    dve.tensor_copy(rows[:, b % 2, :, GATES:], gates[:, TT * b:TT * b + TT]).then_inc(rows_done, 1)
                    if b == 0:
                        for e in range(1, E):
                            then(dve.scalar_tensor_tensor(expert[:, e % 2], tile_number[:], tile0[:, e:e + 1], expert[:, (e - 1) % 2], ALU.is_ge, ALU.add))
                        then(dve.tensor_copy(expert_of[:], expert[:, (E - 1) % 2]))
                        assert steps == route_steps, steps
                    for i in (2 * b, 2 * b + 1):
                        dve.wait_ge(bias_full, i + 1)
                        dve.wait_ge(rows_done, (TT + 2) * (b + 1))
                        dst = c.x[:, b, 2 * (i % 2):2 * (i % 2) + 2]
                        dve.tensor_tensor(dst, up_ps[:, i % 4].rearrange("p (t d) -> p t d", t=2), dst, ALU.add).then_inc(bias_added, 1)

                def take(i, slot):
                    e = expert_at(dve, i)
                    dve.wait_ge(rows_in[slot], 8 * (i - slot) + 16)
                    wait(dve, weighted, i - 1)
                    wait(dve, added, 16 * (i - 1))
                    dve.tensor_copy(token_now[:, slot:slot + 1], tile_rows[:, slot, ID:ID + 1].bitcast(U32)).then_inc(taken, 1)
                    dve.tensor_copy(gate_now[:, slot:slot + 1], tile_rows[:, slot, bass.ds(e + GATES, 1)]).then_inc(taken, 1)

                def prepare(i, slot):
                    dve.wait_ge(turned, i + 1)
                    wait(dve, up_full, 2 * (i - 1))
                    dve.tensor_copy(tileT[:, slot], turn_ps[:, slot, 0:D].rearrange("p (k n) -> p k n", k=KD)).then_inc(turned_copied, 1)
                    e = expert_at(dve, i)
                    dve.tensor_copy(up_now[:, slot].rearrange("p k u -> p (k u)"), of(up, e)).then_inc(weights_copied, 1)

                def weigh(i, slot):
                    dve.wait_ge(down_full, i + 1)
                    dve.wait_ge(taken, 2 * i + 2)
                    wait(dve, added, 16 * (i - 1))
                    dve.tensor_scalar(result[:, slot], down_ps[:, slot, 0:D], gate_now[:, slot:slot + 1], None, ALU.mult).then_inc(weighted, 1)

                dve.wait_ge(stored, 16 * B)
                dve.wait_ge(weights_loaded, 16 * 2 * E)
                take(0, 0)
                prepare(0, 0)
                prepare(1, 1)

                def tile(i, slot):
                    take(i + 1, 1 - slot)
                    prepare(i + 2, slot)
                    weigh(i, slot)

                tile_loop(dve, tile)
                take(TILES - 1, 0)
                weigh(TILES - 2, 1)
                weigh(TILES - 1, 0)

            @block.tensor
            def _(pe):
                pe.wait_ge(loaded, 16)
                for b in range(B + 1):
                    if b < B:
                        pe.wait_ge(ln_done, TT * b + TT)
                        for k in range(KD):
                            n = 2 * b + k
                            wait(pe, xt_copied, n - 3)
                            for t in range(TT):
                                last = pe.transpose(up_ps[:, n % 4, P * t:P * t + P], xn[:, b % 2, t, P * k:P * k + P], c.ident[:])
                            last.then_inc(xt_full, 1)
                    if b >= 1:
                        pe.wait_ge(xt_copied, 2 * b)
                        for t in range(TT):
                            n = TT * (b - 1) + t
                            for k in range(KD):
                                last = pe.matmul(down_ps[:, 0, E * n:E * n + E], xnT[:, (b - 1) % 2, k, P * t:P * t + P],
                                                 router[:, k], start=(k == 0), stop=(k == KD - 1))
                        last.then_inc(logits_full, 1)
                pe.wait_ge(routed, 13)
                marks = chosen[:].rearrange("p n e -> p (n e)")
                pe.matmul(down_ps[:, 1, 0:NT * E], earlier[:], marks, start=True, stop=True).then_inc(ranks_full, 1)
                pe.matmul(turn_ps[:, 0, 0:NT * E], ones[:], marks, start=True, stop=True).then_inc(ranks_full, 1)
                pe.wait_ge(routed, 19)
                for i in range(NT // 4):
                    wait(pe, gt_copied, i - 3)
                    for t in range(4):
                        last = pe.transpose(up_ps[0:E, i % 4, P * t:P * t + P], gates[:, 4 * i + t], c.ident[:])
                    last.then_inc(gt_full, 1)
                pe.wait_ge(gt_copied, NT // 4)
                pe.wait_ge(biases_loaded, 32)
                for i in range(NT // 2):
                    wait(pe, bias_added, i - 3)
                    for t in range(2):
                        last = pe.matmul(up_ps[:, i % 4, D * t:D * t + D], gatesT[:, 2 * i + t], down_bias[:], start=True, stop=True)
                    last.then_inc(bias_full, 1)
                pe.wait_ge(bias_added, NT // 2)
                pe.wait_ge(routed, route_steps)
                pe.wait_ge(weights_loaded, 16 * 2 * E)

                def turn(i, slot):
                    pe.wait_ge(rows_in[slot], 8 * (i - slot) + 16)
                    wait(pe, turned_copied, i - 1)
                    for k in range(KD):
                        last = pe.transpose(turn_ps[:, slot, P * k:P * k + P], tile_rows[:, slot, P * k:P * k + P], c.ident[:])
                    last.then_inc(turned, 1)

                def units(i, slot):
                    pe.wait_ge(turned_copied, i + 1)
                    pe.wait_ge(weights_copied, i + 1)
                    wait(pe, gelu_done, UT * (i - 1))
                    for u in range(UT):
                        for k in range(KD):
                            last = pe.matmul(up_ps[:, 2 * slot + u // 4, P * (u % 4):P * (u % 4) + P], up_now[:, slot, k, P * u:P * u + P],
                                             tileT[:, slot, k], start=(k == 0), stop=(k == KD - 1))
                        if u % 4 == 3:
                            last.then_inc(up_full, 1)

                def output(i, slot):
                    e = expert_at(pe, i)
                    pe.wait_ge(gelu_done, UT * i + UT)
                    wait(pe, weighted, i - 1)
                    for u in range(UT):
                        last = pe.matmul(down_ps[:, slot, 0:D], hidden[:, slot, u], down[:, bass.ds(e, 1), D * u:D * u + D].rearrange("p o d -> p (o d)"),
                                         start=(u == 0), stop=(u == UT - 1))
                    last.then_inc(down_full, 1)

                turn(0, 0)
                turn(1, 1)
                units(0, 0)

                def tile(i, slot):
                    units(i + 1, 1 - slot)
                    turn(i + 2, slot)
                    output(i, slot)

                tile_loop(pe, tile)
                units(TILES - 1, 0)
                output(TILES - 2, 1)
                output(TILES - 1, 0)

    nc.clear_and_free_semaphores(made)
    nc.all_engine_barrier()


class Shared:

    def __init__(self, nc, ctx):
        def sb(name, shape, dt=F32):
            return ctx.enter_context(nc.sbuf_tensor(name, shape, dt))

        self.x = sb("x_stream", [P, B, TT, D])
        self.ident = sb("ident", [P, P])
        self.ident_b = sb("ident_b", [P, P], BF16)
        self.causal_kq = sb("causal_kq", [P, P], BF16)
        self.causal_qk = sb("causal_qk", [P, P], BF16)
        self.head_ones = sb("head_ones", [P, P])
        self.minus_half = sb("minus_half", [P, 32])
        self.slots = Slots(nc, ctx)


def lay_out(**a):
    a = {k: np.asarray(v) for k, v in a.items()}

    def out_rows(w, bias=None):
        rows = np.zeros((NG, GH, 32, D), np.float32)
        rows[:, :, :HD] = w.reshape(NG, GH, HD, D)
        if bias is not None:
            rows[0, 0, HD] = bias
        return rows.reshape(NG, P, D)

    def cross(name, wq, wk, wv, wo, bq, bk, bv, bo):
        return {name + "_wq": wq, name + "_wk": wk, name + "_wv": wv, name + "_wo": out_rows(wo, bo),
                name + "_bq": np.ascontiguousarray(bq.reshape(KD, P).T), name + "_bk": np.ascontiguousarray(bk.reshape(KD, P).T),
                name + "_bv": np.tile(bv, (P, 1))}

    S2 = a["ctx_1024"].shape[1]
    t = lambda w: np.ascontiguousarray(w.T)
    qkv0, qkv1 = t(a["L0_attn_w_attn"]), t(a["L1_attn_qkv_w"])
    return {
        "x": a["x"],
        "l0_qk": np.ascontiguousarray(qkv0[:, :2 * D]), "l0_v": np.ascontiguousarray(qkv0[:, 2 * D:]),
        "l0_o": out_rows(t(a["L0_attn_w_proj"])),
        "l1_qk": np.ascontiguousarray(qkv1[:, :2 * D]), "l1_v": np.ascontiguousarray(qkv1[:, 2 * D:]),
        "l1_o": out_rows(t(a["L1_attn_proj_w"]), a["L1_attn_proj_b"]),
        "ctx_t": np.ascontiguousarray(a["ctx_1024"].reshape(B * S2, D).T),
        "ctx_twice": np.ascontiguousarray(np.repeat(a["ctx_1024"].transpose(0, 2, 1).reshape(B, KD, P, 1, S2), 2, axis=3)).reshape(B, KD, P, P),
        "mask_t": np.ascontiguousarray(a["mask_BxSxS2_ff0"].transpose(0, 2, 1)),
        **cross("x0", a["L0_xattn_wq"], a["L0_xattn_wk"], a["L0_xattn_wv"], a["L0_xattn_wo"],
                a["L0_xattn_bq"], a["L0_xattn_bk"], a["L0_xattn_bv"], a["L0_xattn_bo"]),
        **cross("x1", t(a["L1_xattn_WQ_w"]), t(a["L1_xattn_WK_w"]), t(a["L1_xattn_WV_w"]), t(a["L1_xattn_WO_w"]),
                a["L1_xattn_WQ_b"], a["L1_xattn_WK_b"], a["L1_xattn_WV_b"], a["L1_xattn_WO_b"]),
        "mod_router": np.tile(a["L0_ffn_w_router"], (P, 1)), "mod_qkv": t(a["L0_ffn_W_qkv"]), "mod_o": out_rows(t(a["L0_ffn_W_out"])),
        "mod_g1": np.ascontiguousarray(a["L0_ffn_g1"].reshape(KD, P).T), "mod_g2": np.ascontiguousarray(a["L0_ffn_g2"].reshape(KD, P).T),
        "mod_w1": t(a["L0_ffn_W1"]), "mod_w2": t(a["L0_ffn_W2"]), "mod_w3": t(a["L0_ffn_W3"]),
        "moe_router": t(a["L1_ffn_w_router"]), "moe_up": np.ascontiguousarray(a["L1_ffn_w_up"].transpose(0, 2, 1)),
        "moe_down": np.ascontiguousarray(a["L1_ffn_w_down"].transpose(0, 2, 1)), "moe_bu": np.ascontiguousarray(a["L1_ffn_b_up"].reshape(8, -1, P).transpose(2, 0, 1)), "moe_bd": a["L1_ffn_b_down"],
        "l1_qg": np.tile(a["L1_attn_q_norm_w"], P // HD).reshape(P, 1),
        "l1_kg": np.tile(a["L1_attn_k_norm_w"], P // HD).reshape(P, 1),
    }


def cross_stage(nc, c, name, i, masked):
    w = lambda what: i[f"{name}_{what}"]
    cross_attention(nc, c, "cross" + name, w("wq"), w("wk"), w("wv"), w("wo"), w("bq"), w("bk"), w("bv"), i["ctx_t"], i["ctx_twice"],
                    i["mask_t"] if masked else None)


STAGES = {
    "1": lambda nc, c, i: self_attention(nc, c, "self0", i["l0_qk"], i["l0_v"], i["l0_o"], True, x_in=i["x"]),
    "2": lambda nc, c, i: cross_stage(nc, c, "x0", i, False),
    "3": lambda nc, c, i: mixture_of_depths(nc, c, *(i["mod_" + w] for w in ("router", "qkv", "o", "g1", "g2", "w1", "w2", "w3"))),
    "4": lambda nc, c, i: self_attention(nc, c, "self1", i["l1_qk"], i["l1_v"], i["l1_o"], False, norm_weights=(i["l1_qg"], i["l1_kg"])),
    "5": lambda nc, c, i: cross_stage(nc, c, "x1", i, True),
    "6": lambda nc, c, i: mixture_of_experts(nc, c, c.slots, i["moe_router"], i["moe_up"], i["moe_bu"], i["moe_down"], i["moe_bd"], i["out"]),
}


def program(nc, i):
    with ExitStack() as ctx:
        c = Shared(nc, ctx)
        constants_made = make_constants(nc, c)
        nc.clear_and_free_semaphores(constants_made)
        nc.all_engine_barrier()
        for stage in STAGES.values():
            stage(nc, c, i)


def kernel(**inputs):
    import concourse.bacc as _bacc
    from concourse import mybir as _mybir
    from concourse.bass_utils import run_bass_kernel_spmd as _run

    arrays = lay_out(**inputs)
    nc = _bacc.Bacc("TRN2", target_bir_lowering=False, num_devices=1)
    tensors = {name: nc.dram_tensor(name + "_dram", a.shape, _mybir.dt.from_np(a.dtype), kind="ExternalInput").ap()
               for name, a in arrays.items()}
    tensors["out"] = nc.dram_tensor("out_dram", (B, S, D), F32, kind="ExternalOutput").ap()
    program(nc, tensors)
    nc.finalize()
    r = _run(nc, [{name + "_dram": a for name, a in arrays.items()}], core_ids=[0])
    return np.array(r.results[0]["out_dram"]).reshape(B, S, D)
```
